# Optimizing a Trainium2 kernel written in Bass

```python
import numpy as np
import jax
import jax.numpy as jnp

def _softmax(x, axis=-1):
    return jax.nn.softmax(x, axis=axis)

def _gelu(x):
    return jax.nn.gelu(x, approximate=True)

def _silu(x):
    return jax.nn.silu(x)

def _sigmoid(x):
    return jax.nn.sigmoid(x)

def _layernorm(x, axis=-1, eps=1e-05):
    m = jnp.mean(x, axis=axis, keepdims=True)
    v = jnp.var(x, axis=axis, keepdims=True)
    return (x - m) / jnp.sqrt(v + eps)

def _scatter_add(tgt, idx, src, axis=0):
    return tgt.at[idx].add(src)

def _segment_sum(src, seg, n):
    return jax.ops.segment_sum(src, seg, n)
kernel_name = 'mk_xattn_ffn_d2_seqx_r8_45dcfc'

def setup_inputs(seed: int=0):
    np.random.seed(seed)
    _w = jnp.asarray

    def _rec_inputs():
        import jax
        import jax.numpy as jnp
        _rk = jax.random.key(seed)
        x = -0.0002928 + 1 * jax.random.normal(jax.random.fold_in(_rk, 1), (64, 128, 128), jnp.float32)
        _lenS = 128 - jax.random.randint(jax.random.fold_in(_rk, 7), (64,), 0, max(1, 128 // 4) + 1, jnp.int32)
        _lenS2 = 120 - jax.random.randint(jax.random.fold_in(_rk, 8), (64,), 0, max(1, 120 // 4) + 1, jnp.int32)
        _ctx_1024P = jax.random.normal(jax.random.fold_in(_rk, 11), (64, 16, 128), jnp.float32)
        _ctx_1024c = jax.random.dirichlet(jax.random.fold_in(_rk, 511), 0.3 * jnp.ones((16,), jnp.float32), (64, 120))
        _ctx_1024t = jnp.einsum('bsk,bkd->bsd', _ctx_1024c, _ctx_1024P)
        _ctx_1024t = _ctx_1024t * jax.lax.rsqrt(jnp.mean(jnp.square(_ctx_1024t)) + 1e-12) * 0.953939
        ctx_1024 = 4.13588e-05 + 0.999923 * (_ctx_1024t + 0.3 * jax.random.normal(jax.random.fold_in(_rk, 611), (64, 120, 128), jnp.float32))
        return (x, ctx_1024)
    x, ctx_1024 = _rec_inputs()

    def _L0_xattn_setup():
        import jax, jax.numpy as jnp
        import numpy as np
        DIM = 128
        H = 16
        DH = DIM // H
        LN_EPS = 1e-05

        def _linear_params(key, din, dout):
            kw, kb = jax.random.split(key)
            bound = 1.0 / np.sqrt(din)
            W = jax.random.uniform(kw, (din, dout), jnp.float32, -bound, bound)
            b = jax.random.uniform(kb, (dout,), jnp.float32, -bound, bound)
            return (W, b)

        def _layernorm(x, g, b):
            m = jnp.mean(x, axis=-1, keepdims=True)
            v = jnp.mean(jnp.square(x - m), axis=-1, keepdims=True)
            return (x - m) * jax.lax.rsqrt(v + LN_EPS) * g + b

        def _split_heads(x):
            B, N, _ = x.shape
            return x.reshape(B, N, H, DH).transpose(2, 0, 1, 3).reshape(H * B, N, DH)

        def _merge_heads(x, B):
            _, N, _ = x.shape
            return x.reshape(H, B, N, DH).transpose(1, 2, 0, 3).reshape(B, N, DIM)
        key = jax.random.key(seed)
        ks = jax.random.split(key, 10)
        inp = {'Q': jax.random.normal(ks[0], (8, 64, DIM), jnp.float32), 'K1': jax.random.normal(ks[1], (8, 128, DIM), jnp.float32), 'K2': jax.random.normal(ks[2], (8, 128, DIM), jnp.float32)}
        for name, k in zip(['q', 'k1', 'k2', 'v1', 'v2', 'o'], ks[3:9]):
            W, b = _linear_params(k, DIM, DIM)
            inp['W' + name] = W
            inp['b' + name] = b
        inp['g0'] = jnp.ones((DIM,), jnp.float32)
        inp['beta0'] = jnp.zeros((DIM,), jnp.float32)
        inp['g1'] = jnp.ones((DIM,), jnp.float32)
        inp['beta1'] = jnp.zeros((DIM,), jnp.float32)
        return inp
    _L0_xattn_all = _L0_xattn_setup()
    _L0_xattn_in = {k: v for k, v in _L0_xattn_all.items() if k in ('Wq', 'bq', 'Wk1', 'bk1', 'Wk2', 'bk2', 'Wv1', 'bv1', 'Wv2', 'bv2', 'Wo', 'bo', 'g0', 'beta0', 'g1', 'beta1')}
    del _L0_xattn_all

    def _L0_ffn_setup():
        import jax, jax.numpy as jnp
        import numpy as np
        EPS = 1e-05
        LN_EPS = 1e-05
        NUM_EXPERTS = 8
        TOP_K = 2
        HIDDEN = 128
        INTER = 256

        def _swiglu(x, wg, wu, wd):
            return jax.nn.silu(x @ wg) * (x @ wu) @ wd
        key = jax.random.key(seed)
        ks = jax.random.split(key, 10)
        B, S, H, I, E = (8, 512, HIDDEN, INTER, NUM_EXPERTS)
        std_h = 1.0 / np.sqrt(H)
        std_i = 1.0 / np.sqrt(I)
        return {'x': jax.random.normal(ks[0], (B, S, H), dtype=jnp.float32), 'ln_scale': jnp.ones((H,), dtype=jnp.float32), 'ln_bias': jnp.zeros((H,), dtype=jnp.float32), 'gate_w': jax.random.normal(ks[1], (E, H), dtype=jnp.float32) * 0.01, 'Wg': jax.random.normal(ks[2], (E, H, I), dtype=jnp.float32) * std_h, 'Wu': jax.random.normal(ks[3], (E, H, I), dtype=jnp.float32) * std_h, 'Wd': jax.random.normal(ks[4], (E, I, H), dtype=jnp.float32) * std_i, 'sWg': jax.random.normal(ks[5], (H, I), dtype=jnp.float32) * std_h, 'sWu': jax.random.normal(ks[6], (H, I), dtype=jnp.float32) * std_h, 'sWd': jax.random.normal(ks[7], (I, H), dtype=jnp.float32) * std_i}
    _L0_ffn_all = _L0_ffn_setup()
    _L0_ffn_in = {k: v for k, v in _L0_ffn_all.items() if k in ('ln_scale', 'ln_bias', 'gate_w', 'Wg', 'Wu', 'Wd', 'sWg', 'sWu', 'sWd')}
    del _L0_ffn_all

    def _L1_xattn_setup():
        import math
        import jax, jax.numpy as jnp
        import numpy as np
        H = 16
        D_MODEL = 128
        DK = D_MODEL // H
        K_FACTOR = 2

        def _time_delay_agg_inference(v, corr):
            B, _, _, L = v.shape
            top_k = min(int(K_FACTOR * math.log(L)), L)
            mean_value = jnp.mean(corr, axis=(1, 2))
            weights, delay = jax.lax.top_k(mean_value, top_k)
            tmp_corr = jax.nn.softmax(weights, axis=-1)
            idx = (delay[:, :, None] + jnp.arange(L)) % L
            gathered = jnp.take_along_axis(v[:, None], idx[:, :, None, None, :], axis=-1)
            return jnp.einsum('bk,bkhdl->bhdl', tmp_corr, gathered)
        key = jax.random.key(seed)
        ks = jax.random.split(key, 11)
        B, L, D = (4, 256, D_MODEL)
        s = 1.0 / math.sqrt(D)
        return {'queries': jax.random.normal(ks[0], (B, L, D), jnp.float32), 'keys': jax.random.normal(ks[1], (B, L, D), jnp.float32), 'values': jax.random.normal(ks[2], (B, L, D), jnp.float32), 'Wq': jax.random.normal(ks[3], (D, H * DK), jnp.float32) * s, 'bq': jnp.zeros((H * DK,), jnp.float32), 'Wk': jax.random.normal(ks[4], (D, H * DK), jnp.float32) * s, 'bk': jnp.zeros((H * DK,), jnp.float32), 'Wv': jax.random.normal(ks[5], (D, H * DK), jnp.float32) * s, 'bv': jnp.zeros((H * DK,), jnp.float32), 'Wo': jax.random.normal(ks[6], (H * DK, D), jnp.float32) * s, 'bo': jnp.zeros((D,), jnp.float32)}
    _L1_xattn_all = _L1_xattn_setup()
    _L1_xattn_in = {k: v for k, v in _L1_xattn_all.items() if k in ('Wq', 'bq', 'Wk', 'bk', 'Wv', 'bv', 'Wo', 'bo')}
    del _L1_xattn_all

    def _L1_ffn_setup():
        import jax, jax.numpy as jnp
        import numpy as np
        DIM, HEADS, FFN, E = (128, 16, 512, 8)
        B, S = (2, 128)
        EPS = 1e-05

        def _ln(x, g, b):
            mu = jnp.mean(x, axis=-1, keepdims=True)
            var = jnp.mean((x - mu) ** 2, axis=-1, keepdims=True)
            return (x - mu) * jax.lax.rsqrt(var + EPS) * g + b
        key = jax.random.key(seed)
        ks = jax.random.split(key, 20)
        sd = 0.02
        d, f = (DIM, FFN)
        return {'x': jax.random.normal(ks[0], (B, S, d), jnp.float32), 'ln1_g': jnp.ones((d,), jnp.float32), 'ln1_b': jnp.zeros((d,), jnp.float32), 'Wqkv': jax.random.normal(ks[1], (d, 3 * d), jnp.float32) * sd, 'bqkv': jnp.zeros((3 * d,), jnp.float32), 'Wo': jax.random.normal(ks[2], (d, d), jnp.float32) * sd, 'bo': jnp.zeros((d,), jnp.float32), 'ln2_g': jnp.ones((d,), jnp.float32), 'ln2_b': jnp.zeros((d,), jnp.float32), 'gate_w': jax.random.normal(ks[3], (d, E), jnp.float32) * sd, 'W1': jax.random.normal(ks[4], (E, d, f), jnp.float32) * sd, 'b1': jnp.zeros((E, f), jnp.float32), 'W2': jax.random.normal(ks[5], (E, f, d), jnp.float32) * sd, 'b2': jnp.zeros((E, d), jnp.float32), 'rW1': jax.random.normal(ks[6], (d, f), jnp.float32) * sd, 'rb1': jnp.zeros((f,), jnp.float32), 'rW2': jax.random.normal(ks[7], (f, d), jnp.float32) * sd, 'rb2': jnp.zeros((d,), jnp.float32), 'coef_w': jax.random.normal(ks[8], (d, 2), jnp.float32) * sd, 'coef_b': jnp.zeros((2,), jnp.float32)}
    _L1_ffn_all = _L1_ffn_setup()
    _L1_ffn_in = {k: v for k, v in _L1_ffn_all.items() if k in ('ln1_g', 'ln1_b', 'Wqkv', 'bqkv', 'Wo', 'bo', 'ln2_g', 'ln2_b', 'gate_w', 'W1', 'b1', 'W2', 'b2', 'rW1', 'rb1', 'rW2', 'rb2', 'coef_w', 'coef_b')}
    del _L1_ffn_all
    return {'x': x, 'ctx_1024': ctx_1024, 'L0_xattn_Wq': _L0_xattn_in['Wq'], 'L0_xattn_bq': _L0_xattn_in['bq'], 'L0_xattn_Wk1': _L0_xattn_in['Wk1'], 'L0_xattn_bk1': _L0_xattn_in['bk1'], 'L0_xattn_Wk2': _L0_xattn_in['Wk2'], 'L0_xattn_bk2': _L0_xattn_in['bk2'], 'L0_xattn_Wv1': _L0_xattn_in['Wv1'], 'L0_xattn_bv1': _L0_xattn_in['bv1'], 'L0_xattn_Wv2': _L0_xattn_in['Wv2'], 'L0_xattn_bv2': _L0_xattn_in['bv2'], 'L0_xattn_Wo': _L0_xattn_in['Wo'], 'L0_xattn_bo': _L0_xattn_in['bo'], 'L0_xattn_g0': _L0_xattn_in['g0'], 'L0_xattn_beta0': _L0_xattn_in['beta0'], 'L0_xattn_g1': _L0_xattn_in['g1'], 'L0_xattn_beta1': _L0_xattn_in['beta1'], 'L0_ffn_ln_scale': _L0_ffn_in['ln_scale'], 'L0_ffn_ln_bias': _L0_ffn_in['ln_bias'], 'L0_ffn_gate_w': _L0_ffn_in['gate_w'], 'L0_ffn_Wg': _L0_ffn_in['Wg'], 'L0_ffn_Wu': _L0_ffn_in['Wu'], 'L0_ffn_Wd': _L0_ffn_in['Wd'], 'L0_ffn_sWg': _L0_ffn_in['sWg'], 'L0_ffn_sWu': _L0_ffn_in['sWu'], 'L0_ffn_sWd': _L0_ffn_in['sWd'], 'L1_xattn_Wq': _L1_xattn_in['Wq'], 'L1_xattn_bq': _L1_xattn_in['bq'], 'L1_xattn_Wk': _L1_xattn_in['Wk'], 'L1_xattn_bk': _L1_xattn_in['bk'], 'L1_xattn_Wv': _L1_xattn_in['Wv'], 'L1_xattn_bv': _L1_xattn_in['bv'], 'L1_xattn_Wo': _L1_xattn_in['Wo'], 'L1_xattn_bo': _L1_xattn_in['bo'], 'L1_ffn_ln1_g': _L1_ffn_in['ln1_g'], 'L1_ffn_ln1_b': _L1_ffn_in['ln1_b'], 'L1_ffn_Wqkv': _L1_ffn_in['Wqkv'], 'L1_ffn_bqkv': _L1_ffn_in['bqkv'], 'L1_ffn_Wo': _L1_ffn_in['Wo'], 'L1_ffn_bo': _L1_ffn_in['bo'], 'L1_ffn_ln2_g': _L1_ffn_in['ln2_g'], 'L1_ffn_ln2_b': _L1_ffn_in['ln2_b'], 'L1_ffn_gate_w': _L1_ffn_in['gate_w'], 'L1_ffn_W1': _L1_ffn_in['W1'], 'L1_ffn_b1': _L1_ffn_in['b1'], 'L1_ffn_W2': _L1_ffn_in['W2'], 'L1_ffn_b2': _L1_ffn_in['b2'], 'L1_ffn_rW1': _L1_ffn_in['rW1'], 'L1_ffn_rb1': _L1_ffn_in['rb1'], 'L1_ffn_rW2': _L1_ffn_in['rW2'], 'L1_ffn_rb2': _L1_ffn_in['rb2'], 'L1_ffn_coef_w': _L1_ffn_in['coef_w'], 'L1_ffn_coef_b': _L1_ffn_in['coef_b']}

def reference(x, ctx_1024, L0_xattn_Wq, L0_xattn_bq, L0_xattn_Wk1, L0_xattn_bk1, L0_xattn_Wk2, L0_xattn_bk2, L0_xattn_Wv1, L0_xattn_bv1, L0_xattn_Wv2, L0_xattn_bv2, L0_xattn_Wo, L0_xattn_bo, L0_xattn_g0, L0_xattn_beta0, L0_xattn_g1, L0_xattn_beta1, L0_ffn_ln_scale, L0_ffn_ln_bias, L0_ffn_gate_w, L0_ffn_Wg, L0_ffn_Wu, L0_ffn_Wd, L0_ffn_sWg, L0_ffn_sWu, L0_ffn_sWd, L1_xattn_Wq, L1_xattn_bq, L1_xattn_Wk, L1_xattn_bk, L1_xattn_Wv, L1_xattn_bv, L1_xattn_Wo, L1_xattn_bo, L1_ffn_ln1_g, L1_ffn_ln1_b, L1_ffn_Wqkv, L1_ffn_bqkv, L1_ffn_Wo, L1_ffn_bo, L1_ffn_ln2_g, L1_ffn_ln2_b, L1_ffn_gate_w, L1_ffn_W1, L1_ffn_b1, L1_ffn_W2, L1_ffn_b2, L1_ffn_rW1, L1_ffn_rb1, L1_ffn_rW2, L1_ffn_rb2, L1_ffn_coef_w, L1_ffn_coef_b):
    import jax
    import jax.numpy as jnp

    def _L0_xattn_ref(Q, K1, K2, Wq, bq, Wk1, bk1, Wk2, bk2, Wv1, bv1, Wv2, bv2, Wo, bo, g0, beta0, g1, beta1):
        import jax, jax.numpy as jnp
        import numpy as np
        DIM = 128
        H = 16
        DH = DIM // H
        LN_EPS = 1e-05

        def _linear_params(key, din, dout):
            kw, kb = jax.random.split(key)
            bound = 1.0 / np.sqrt(din)
            W = jax.random.uniform(kw, (din, dout), jnp.float32, -bound, bound)
            b = jax.random.uniform(kb, (dout,), jnp.float32, -bound, bound)
            return (W, b)

        def _layernorm(x, g, b):
            m = jnp.mean(x, axis=-1, keepdims=True)
            v = jnp.mean(jnp.square(x - m), axis=-1, keepdims=True)
            return (x - m) * jax.lax.rsqrt(v + LN_EPS) * g + b

        def _split_heads(x):
            B, N, _ = x.shape
            return x.reshape(B, N, H, DH).transpose(2, 0, 1, 3).reshape(H * B, N, DH)

        def _merge_heads(x, B):
            _, N, _ = x.shape
            return x.reshape(H, B, N, DH).transpose(1, 2, 0, 3).reshape(B, N, DIM)
        B = Q.shape[0]
        Qp = Q @ Wq + bq
        K1p = K1 @ Wk1 + bk1
        K2p = K2 @ Wk2 + bk2
        V1p = K1p @ Wv1 + bv1
        V2p = K2p @ Wv2 + bv2
        Q_ = _split_heads(Qp)
        K_ = jnp.concatenate([_split_heads(K1p), _split_heads(K2p)], axis=1)
        V_ = jnp.concatenate([_split_heads(V1p), _split_heads(V2p)], axis=1)
        scores = jnp.einsum('bqd,bkd->bqk', Q_, K_) / np.sqrt(DIM).astype(np.float32)
        A = jax.nn.softmax(scores, axis=1)
        out = Q_ + jnp.einsum('bqk,bkd->bqd', A, V_)
        out = _merge_heads(out, B)
        out = _layernorm(out, g0, beta0)
        out = out + jax.nn.relu(out @ Wo + bo)
        out = _layernorm(out, g1, beta1)
        return out

    def _L0_ffn_ref(x, ln_scale, ln_bias, gate_w, Wg, Wu, Wd, sWg, sWu, sWd):
        import jax, jax.numpy as jnp
        import numpy as np
        EPS = 1e-05
        LN_EPS = 1e-05
        NUM_EXPERTS = 8
        TOP_K = 2
        HIDDEN = 128
        INTER = 256

        def _swiglu(x, wg, wu, wd):
            return jax.nn.silu(x @ wg) * (x @ wu) @ wd
        B, S, H = x.shape
        xf = x.reshape(-1, H)
        mu = jnp.mean(xf, axis=-1, keepdims=True)
        var = jnp.var(xf, axis=-1, keepdims=True)
        xn = (xf - mu) * jax.lax.rsqrt(var + LN_EPS) * ln_scale + ln_bias
        logits = xn @ gate_w.T
        probs = jax.nn.softmax(logits, axis=-1)
        tk_probs, tk_idx = jax.lax.top_k(probs, TOP_K)
        tk_probs = tk_probs / (jnp.sum(tk_probs, axis=-1, keepdims=True) + EPS)
        onehot = tk_idx[..., None] == jnp.arange(NUM_EXPERTS)[None, None, :]
        w = jnp.sum(tk_probs[..., None] * onehot.astype(tk_probs.dtype), axis=1)
        out = _swiglu(xf, sWg, sWu, sWd)
        for e in range(NUM_EXPERTS):
            out = out + w[:, e:e + 1] * _swiglu(xf, Wg[e], Wu[e], Wd[e])
        return out.reshape(B, S, H)

    def _L1_xattn_ref(queries, keys, values, Wq, bq, Wk, bk, Wv, bv, Wo, bo):
        import math
        import jax, jax.numpy as jnp
        import numpy as np
        H = 16
        D_MODEL = 128
        DK = D_MODEL // H
        K_FACTOR = 2

        def _time_delay_agg_inference(v, corr):
            B, _, _, L = v.shape
            top_k = min(int(K_FACTOR * math.log(L)), L)
            mean_value = jnp.mean(corr, axis=(1, 2))
            weights, delay = jax.lax.top_k(mean_value, top_k)
            tmp_corr = jax.nn.softmax(weights, axis=-1)
            idx = (delay[:, :, None] + jnp.arange(L)) % L
            gathered = jnp.take_along_axis(v[:, None], idx[:, :, None, None, :], axis=-1)
            return jnp.einsum('bk,bkhdl->bhdl', tmp_corr, gathered)
        B, Lq, _ = queries.shape
        Lk = keys.shape[1]
        q = (queries @ Wq + bq).reshape(B, Lq, H, DK)
        k = (keys @ Wk + bk).reshape(B, Lk, H, DK)
        v = (values @ Wv + bv).reshape(B, Lk, H, DK)
        if Lq > Lk:
            pad = ((0, 0), (0, Lq - Lk), (0, 0), (0, 0))
            k = jnp.pad(k, pad)
            v = jnp.pad(v, pad)
        else:
            k = k[:, :Lq]
            v = v[:, :Lq]
        qt = jnp.transpose(q, (0, 2, 3, 1))
        kt = jnp.transpose(k, (0, 2, 3, 1))
        vt = jnp.transpose(v, (0, 2, 3, 1))
        qf = jnp.fft.rfft(qt)
        kf = jnp.fft.rfft(kt)
        c = qf.real * kf.real + 1j * -(qf.imag * kf.imag)
        corr = jnp.fft.irfft(c, n=Lq).astype(qt.dtype)
        agg = _time_delay_agg_inference(vt, corr)
        out = jnp.transpose(agg, (0, 3, 1, 2)).reshape(B, Lq, H * DK)
        return out @ Wo + bo

    def _L1_ffn_ref(x, ln1_g, ln1_b, Wqkv, bqkv, Wo, bo, ln2_g, ln2_b, gate_w, W1, b1, W2, b2, rW1, rb1, rW2, rb2, coef_w, coef_b):
        import jax, jax.numpy as jnp
        import numpy as np
        DIM, HEADS, FFN, E = (128, 16, 512, 8)
        B, S = (2, 128)
        EPS = 1e-05

        def _ln(x, g, b):
            mu = jnp.mean(x, axis=-1, keepdims=True)
            var = jnp.mean((x - mu) ** 2, axis=-1, keepdims=True)
            return (x - mu) * jax.lax.rsqrt(var + EPS) * g + b
        b, s, d = x.shape
        h, dh = (HEADS, d // HEADS)
        xn = _ln(x, ln1_g, ln1_b)
        qkv = xn @ Wqkv + bqkv
        q, k, v = jnp.split(qkv, 3, axis=-1)
        q = q.reshape(b, s, h, dh)
        k = k.reshape(b, s, h, dh)
        v = v.reshape(b, s, h, dh)
        scores = jnp.einsum('bqhd,bkhd->bhqk', q, k) / jnp.sqrt(jnp.float32(dh))
        attn = jax.nn.softmax(scores, axis=-1)
        ctx = jnp.einsum('bhqk,bkhd->bqhd', attn, v).reshape(b, s, d)
        x = x + ctx @ Wo + bo
        xn2 = _ln(x, ln2_g, ln2_b)
        xt = xn2.reshape(b * s, d)
        probs = jax.nn.softmax(xt @ gate_w, axis=-1)
        gate_val = jnp.max(probs, axis=-1, keepdims=True)
        expert_idx = jnp.argmax(probs, axis=-1)
        oh = jax.nn.one_hot(expert_idx, E, dtype=xt.dtype)
        xe = jnp.einsum('te,td->etd', oh, xt)
        he = jax.nn.gelu(jnp.einsum('etd,edf->etf', xe, W1) + b1[:, None, :], approximate=False)
        ye = jnp.einsum('etf,efd->etd', he, W2) + b2[:, None, :]
        moe_out = jnp.einsum('te,etd->td', oh, ye) * gate_val
        rm = jax.nn.gelu(xt @ rW1 + rb1, approximate=False) @ rW2 + rb2
        coef = jax.nn.softmax(xt @ coef_w + coef_b, axis=-1)
        ff = moe_out * coef[:, 0:1] + rm * coef[:, 1:2]
        return x + ff.reshape(b, s, d)
    x = x + _L0_xattn_ref(_layernorm(x, axis=-1), ctx_1024, ctx_1024, L0_xattn_Wq, L0_xattn_bq, L0_xattn_Wk1, L0_xattn_bk1, L0_xattn_Wk2, L0_xattn_bk2, L0_xattn_Wv1, L0_xattn_bv1, L0_xattn_Wv2, L0_xattn_bv2, L0_xattn_Wo, L0_xattn_bo, L0_xattn_g0, L0_xattn_beta0, L0_xattn_g1, L0_xattn_beta1)
    x = x + _L0_ffn_ref(_layernorm(x, axis=-1), L0_ffn_ln_scale, L0_ffn_ln_bias, L0_ffn_gate_w, L0_ffn_Wg, L0_ffn_Wu, L0_ffn_Wd, L0_ffn_sWg, L0_ffn_sWu, L0_ffn_sWd)
    x = x + _L1_xattn_ref(_layernorm(x, axis=-1), ctx_1024, ctx_1024, L1_xattn_Wq, L1_xattn_bq, L1_xattn_Wk, L1_xattn_bk, L1_xattn_Wv, L1_xattn_bv, L1_xattn_Wo, L1_xattn_bo)
    x = x + _L1_ffn_ref(_layernorm(x, axis=-1), L1_ffn_ln1_g, L1_ffn_ln1_b, L1_ffn_Wqkv, L1_ffn_bqkv, L1_ffn_Wo, L1_ffn_bo, L1_ffn_ln2_g, L1_ffn_ln2_b, L1_ffn_gate_w, L1_ffn_W1, L1_ffn_b1, L1_ffn_W2, L1_ffn_b2, L1_ffn_rW1, L1_ffn_rb1, L1_ffn_rW2, L1_ffn_rb2, L1_ffn_coef_w, L1_ffn_coef_b)
    return x

_drawn_inputs = setup_inputs


def setup_inputs(seed=0):
    import zlib

    import numpy as np

    out = dict(_drawn_inputs(seed))
    spreads = {'L0_xattn_g0': (1.0, 0.2),
     'L0_xattn_beta0': (0.0, 0.1),
     'L0_xattn_g1': (1.0, 0.2),
     'L0_xattn_beta1': (0.0, 0.1),
     'L0_ffn_ln_scale': (1.0, 0.2),
     'L0_ffn_ln_bias': (0.0, 0.1),
     'L1_xattn_bq': (0.0, 2.0),
     'L1_xattn_bk': (0.0, 0.301),
     'L1_xattn_bv': (0.0, 0.1),
     'L1_xattn_bo': (0.0, 0.1),
     'L1_ffn_ln1_g': (1.0, 0.6),
     'L1_ffn_ln1_b': (0.0, 0.8),
     'L1_ffn_bqkv': (0.0, 0.8),
     'L1_ffn_bo': (0.0, 0.1),
     'L1_ffn_ln2_g': (1.0, 0.6),
     'L1_ffn_ln2_b': (0.0, 0.8),
     'L1_ffn_b1': (0.0, 0.8),
     'L1_ffn_b2': (0.0, 0.8),
     'L1_ffn_rb1': (0.0, 0.8),
     'L1_ffn_rb2': (0.0, 0.43),
     'L1_ffn_coef_b': (0.0, 2.0)}
    factors = {'L1_ffn_Wqkv': 7.239,
     'L1_ffn_Wo': 5.01,
     'L1_ffn_gate_w': 8.0,
     'L1_ffn_W1': 8.0,
     'L1_ffn_W2': 8.0,
     'L1_ffn_rW1': 5.691,
     'L1_ffn_rW2': 5.18,
     'L1_ffn_coef_w': 8.0}
    for name, (base, spread) in spreads.items():
        noise = np.random.default_rng([zlib.crc32(name.encode()), seed]).standard_normal(out[name].shape)
        drawn = base * np.exp(spread * noise) if base else spread * noise
        out[name] = jnp.asarray(drawn.astype(out[name].dtype))
    for name, factor in factors.items():
        out[name] = (out[name] * factor).astype(out[name].dtype)
    return out
```

```python
from contextlib import ExitStack

import concourse.bass as bass
from concourse import mybir

F32 = mybir.dt.float32
BF16 = mybir.dt.bfloat16
I32 = mybir.dt.int32
ALU = mybir.AluOpType
ACT = mybir.ActivationFunctionType
AX = mybir.AxisListType

P = 128
D = 128
S2 = 120
H = 16
DH = D // H
QUAD = 32
HQ = QUAD // DH
EPS = 1e-5
E = 8
GROUP = 4


class Kernel:

    def __init__(self, nc, ctx, ins, out):
        self.nc, self.ctx, self.ins, self.out = nc, ctx, ins, out
        self.NB = ins["x"].shape[0]
        self.sems, self.sem_ctx = [], ExitStack()

    def sb(self, name, shape, dt=F32, ctx=None):
        return (ctx or self.ctx).enter_context(self.nc.sbuf_tensor(name, shape, dt))

    def psum(self, name, shape, ctx, dt=F32):
        return ctx.enter_context(self.nc.psum_tensor(name, shape, dt))

    def sem(self, name):
        self.sems.append(self.sem_ctx.enter_context(self.nc.semaphore(name)))
        return self.sems[-1]

    def pool_dma_sem(self, name):
        return self.ctx.enter_context(self.nc.semaphore(name))

    def retire_semaphores(self):
        with self.nc.Block() as block:
            @block.gpsimd
            def _(pool):
                for sem in self.sems:
                    pool.sem_clear(sem)
        self.sem_ctx.close()
        self.sems, self.sem_ctx = [], ExitStack()


def row_broadcast(vector, rows):
    return vector.partition_broadcast(rows)


def column(vector):
    return vector.rearrange("(d one) -> d one", one=1)


class Chain:

    def __init__(self, sem):
        self.sem, self.n = sem, 0

    def __call__(self, eng, op):
        self.n += 1
        op.then_inc(self.sem, 1)
        eng.wait_ge(self.sem, self.n)


def combine_stats(k, dve, link):
    mean_e, m2_e, mean_o, m2_o = (k.stats[:, :, i] for i in (1, 2, 4, 5))
    link(dve, dve.tensor_tensor(k.mean[:, :], mean_e, mean_o, ALU.subtract))
    link(dve, dve.scalar_tensor_tensor(out=k.var[:, :], in0=k.mean[:, :], scalar=0.25, in1=k.mean[:, :],
                                       op0=ALU.mult, op1=ALU.mult))
    link(dve, dve.tensor_tensor(k.mean[:, :], m2_e, m2_o, ALU.add))
    link(dve, dve.scalar_tensor_tensor(out=k.var[:, :], in0=k.mean[:, :], scalar=1.0 / D, in1=k.var[:, :],
                                       op0=ALU.mult, op1=ALU.add))
    link(dve, dve.tensor_tensor(k.mean[:, :], mean_e, mean_o, ALU.add))
    link(dve, dve.tensor_scalar(k.mean[:, :], k.mean[:, :], 0.5, None, ALU.mult))



def build_load(k):
    nc, ins, NB = k.nc, k.ins, k.NB
    k.x_res = k.sb("x_res", [P, NB, D])
    k.tmp_res = k.sb("tmp_res", [P, NB, D])
    k.vo_res = k.sb("vo_res", [P, NB, D])
    k.ident = k.sb("ident", [P, P])
    k.identb = k.sb("identb", [P, P], BF16)
    k.headmask = k.sb("headmask", [P, HQ])
    k.stats = k.sb("stats", [P, NB, 6])
    k.mean = k.sb("mean", [P, NB])
    k.var = k.sb("var", [P, NB])
    k.rstd = k.sb("rstd", [P, NB])
    k.rstd2 = k.sb("rstd2", [P, NB])
    k.logits = k.sb("logits", [P, NB, E + 2])
    k.coef = k.sb("coef", [P, NB, 2])
    k.coef_shared = k.sb("coef_shared", [P, NB])
    k.choice_w = [k.sb(f"choice_w{j}", [P, NB]) for j in range(2)]
    k.place = [k.sb(f"place{j}", [P, NB], I32) for j in range(2)]
    k.slot_expert = k.sb("slot_expert", [P, 2 * NB + E], I32)
    k.tables = k.sb("tables", [P, P + E + 2 * NB + E])
    k.zeros = k.sb("zeros", [P, 8 * D])
    k.slots = nc.dram_tensor("slots", [(2 * NB + E) * P, D], F32).ap()
    k.results = nc.dram_tensor("results", [(2 * NB + E) * P, D], F32).ap()
    k.xf_dram = nc.dram_tensor("xf_dram", [NB * P, D], F32).ap()
    k.circulant = nc.dram_tensor("circulant", [NB, 2 * P], F32).ap()
    k.w = {}
    for name in ("L0_xattn_Wq", "L0_xattn_Wk1", "L0_xattn_Wk2", "L0_xattn_Wv1", "L0_xattn_Wv2", "L0_xattn_Wo",
                 "L1_xattn_Wv", "L1_xattn_Wo"):
        k.w[name] = k.sb(name, [P, D])
    cols = ("L0_xattn_bq", "L0_xattn_bk1", "L0_xattn_bk2", "L0_xattn_bo", "L0_xattn_g0", "L0_xattn_beta0", "L1_xattn_bv")
    for name in cols:
        k.w[name] = k.sb(name, [P, 1])
    k.v_bias = k.sb("v_bias", [P, 2 * D])
    k.g1_rows = k.sb("g1_rows", [P, D])
    k.beta1_rows = k.sb("beta1_rows", [P, D])
    k.wvo = k.sb("wvo", [P, D])
    k.bvo = k.sb("bvo", [P, D])
    wv_t = k.sb("wv_t", [P, D])
    bv_wide = k.sb("bv_wide", [P, P])

    x_loaded = [k.sem(f"x_loaded{n}") for n in range(4)]
    weights_loaded = k.sem("weights_loaded")
    stats_done = k.sem("stats_done")
    chain = Chain(k.sem("load_chain"))
    ident_cast = k.sem("ident_cast")
    eps_added = k.sem("eps_added")
    root_done = k.sem("root_done")
    zeros_set = k.sem("zeros_set")
    slots_cleared = k.pool_dma_sem("slots_cleared")
    wv_turned = k.sem("wv_turned")
    wv_copied = k.sem("wv_copied")
    wvo_product = k.sem("wvo_product")
    PARTS = 4
    per = NB // PARTS
    loads = [(k.ident, ins["c_ident"]), (k.headmask, ins["c_headmask"]), (k.tables, ins["c_tables"])]
    loads += [(k.w[n], ins[n]) for n in k.w if n not in cols]
    loads += [(k.w[n], column(ins[n])) for n in cols]
    loads += [(k.v_bias[:, 0:D], row_broadcast(ins["L0_xattn_bv1"], P)),
              (k.v_bias[:, D:2 * D], row_broadcast(ins["L0_xattn_bv2"], P)),
              (k.g1_rows[:, :], row_broadcast(ins["L0_xattn_g1"], P)),
              (k.beta1_rows[:, :], row_broadcast(ins["L0_xattn_beta1"], P))]

    with ExitStack() as ctx:
        turn = k.psum("load_turn", [P, 512], ctx)
        prod = k.psum("load_prod", [P, 512], ctx)
        block = ctx.enter_context(nc.Block())

        @block.sync
        def _(sp):
            for n in range(PARTS):
                sp.dma_start(k.x_res[:, n * per:(n + 1) * per, :],
                             ins["x"][n * per:(n + 1) * per].rearrange("b t d -> t b d")).then_inc(x_loaded[n], 16)

        @block.scalar
        def _(act):
            for to, of in loads:
                act.dma_start(to if isinstance(to, bass.AP) else to[:, :], of).then_inc(weights_loaded, 16)
            act.wait_ge(eps_added, 1)
            act.activation(k.rstd[:, :], k.rstd[:, :], ACT.Sqrt).then_inc(root_done, 1)

        @block.gpsimd
        def _(pool):
            pool.memset(k.zeros[:, :], 0.0).then_inc(zeros_set, 1)
            pool.wait_ge(zeros_set, 1)
            for n in range((2 * NB + E) // 8):
                pool.dma_start(k.slots[n * 8 * P:(n + 1) * 8 * P, :].rearrange("(p r) d -> p (r d)", p=P),
                               k.zeros[:, :]).then_inc(slots_cleared, 16)
            pool.wait_ge(slots_cleared, 16 * ((2 * NB + E) // 8))

        @block.tensor
        def _(pe):
            pe.wait_ge(weights_loaded, 16 * len(loads))
            pe.transpose(turn[:, 0:D], k.w["L1_xattn_Wv"][:, :], k.ident[:, :]).then_inc(wv_turned, 1)
            pe.wait_ge(wv_copied, 2)
            pe.matmul(prod[:, 0:D], wv_t[:, :], k.w["L1_xattn_Wo"][:, :], start=True, stop=True)
            pe.matmul(prod[:, D:2 * D], bv_wide[:, :], k.w["L1_xattn_Wo"][:, :],
                      start=True, stop=True).then_inc(wvo_product, 1)

        @block.vector
        def _(dve):
            dve.wait_ge(weights_loaded, 16 * len(loads))
            dve.tensor_copy(k.identb[:, :], k.ident[:, :]).then_inc(ident_cast, 1)
            dve.tensor_copy(bv_wide[:, :], k.w["L1_xattn_bv"][:, 0:1].broadcast_to([P, P])).then_inc(wv_copied, 1)
            dve.wait_ge(wv_turned, 1)
            dve.tensor_copy(wv_t[:, :], turn[:, 0:D]).then_inc(wv_copied, 1)
            for n in range(PARTS):
                dve.wait_ge(x_loaded[n], 16)
                with dve.Fori(n * per, (n + 1) * per) as b:
                    dve.bn_stats(k.stats[:, b, :], k.x_res[:, b, :]).then_inc(stats_done, 1)
            dve.wait_ge(stats_done, NB)
            dve.wait_ge(wvo_product, 1)
            dve.tensor_copy(k.wvo[:, :], prod[:, 0:D]).then_inc(ident_cast, 1)
            dve.tensor_copy(k.bvo[:, :], prod[:, D:2 * D]).then_inc(ident_cast, 1)
            combine_stats(k, dve, chain)
            dve.tensor_scalar(k.rstd[:, :], k.var[:, :], EPS, None, ALU.add).then_inc(eps_added, 1)
            dve.wait_ge(root_done, 1)
            dve.reciprocal(k.rstd[:, :], k.rstd[:, :]).then_inc(ident_cast, 1)
            dve.wait_ge(ident_cast, 4)



def build_context_attention(k):
    nc, ins, NB, w = k.nc, k.ins, k.NB, k.w
    SCALE = 1.0 / float(D) ** 0.5
    W = HQ * P
    CH = 4
    HC = H // 2
    with ExitStack() as ctx:
        sb = lambda n, s, dt=F32: k.sb(n, s, dt, ctx)
        ctx_in = [sb(f"ctx_in{p}", [P, D]) for p in range(2)]
        xn = [sb(f"xn{p}", [P, D]) for p in range(2)]
        xc_t = [sb(f"xc_t{p}", [P, 2 * P]) for p in range(2)]
        q_t = [sb(f"q_t{p}", [P, P]) for p in range(2)]
        k_t = [sb(f"k_t{p}", [P, 2, S2]) for p in range(2)]
        q_wide = [sb(f"q_wide{p}", [P, HQ, P]) for p in range(2)]
        v_sb = [sb(f"v_sb{p}", [P, 2 * D]) for p in range(2)]
        v_heads = [sb(f"v_heads{p}", [P, 2, H, QUAD]) for p in range(2)]
        probs = [sb(f"probs{p}", [P, 2, H, P]) for p in range(2)]
        maxima = sb("maxima", [P, 2, HC], BF16)
        sums = sb("sums", [P, 2, HC])
        rsums = sb("rsums", [P, 4, HC])
        o_t = sb("o_t", [P, P])

        scores = [k.psum(f"scores{i}", [P, 2, W], ctx) for i in range(2)]
        turned = k.psum("turned", [P, 512], ctx)
        qk = k.psum("qk", [P, 512], ctx)
        vv = k.psum("vv", [P, 512], ctx)
        pv = k.psum("pv", [P, 512], ctx)

        s = {n: k.sem("a_" + n) for n in
             ("zeroed", "xn_ready", "turned", "xc_ready", "qk_done", "q_ready", "wide_ready",
              "v_done", "v_ready", "vo_ready", "scores_done", "max_ready", "shifted", "probs_ready", "sums_ready",
              "rsums_ready", "v_heads_ready", "pv_done", "o_ready", "o_turned", "out_ready", "stats")}
        ctx_loaded = [k.sem(f"a_ctx_loaded{p}") for p in range(2)]
        block = ctx.enter_context(nc.Block())

        def all_sequences(eng, step, last):
            for b in (0, 1):
                step(b, b % 2)
            with eng.Fori(1, NB // 2 - 1) as i:
                for p in (0, 1):
                    step(2 * i + p, p)
            for b in (NB - 2, NB - 1):
                step(b, b % 2)
            last()

        def is_(b, n):
            return isinstance(b, int) and b == n

        @block.sync
        def _(sp):
            def step(b, p):
                if not (isinstance(b, int) and b < 2):
                    sp.wait_ge(s["turned"], b - 1)
                sp.dma_start(ctx_in[p][0:S2, :], ins["ctx_1024"][b]).then_inc(ctx_loaded[p], 16)
            all_sequences(sp, step, lambda: None)

        @block.tensor
        def _(pe):
            def turn_inputs(b, p):
                pe.wait_ge(s["xn_ready"], b + 1)
                pe.wait_ge(ctx_loaded[p], 8 * (b - p) + 16)
                pe.wait_ge(s["xc_ready"], b)
                pe.transpose(turned[:, 0:P], xn[p][:, :], k.ident[:, :])
                pe.transpose(turned[:, P:P + S2], ctx_in[p][0:S2, :], k.ident[0:S2, 0:S2]).then_inc(s["turned"], 1)

            def project(b, p):
                pe.wait_ge(s["xc_ready"], b + 1)
                pe.wait_ge(s["q_ready"], b)
                c_t = xc_t[p][:, P:P + S2]
                pe.matmul(qk[:, 0:P], w["L0_xattn_Wq"][:, :], xc_t[p][:, 0:P], start=True, stop=True)
                pe.matmul(qk[:, P:P + S2], w["L0_xattn_Wk1"][:, :], c_t, start=True, stop=True)
                pe.matmul(qk[:, 2 * P:2 * P + S2], w["L0_xattn_Wk2"][:, :], c_t,
                          start=True, stop=True).then_inc(s["qk_done"], 1)

            def values(b, p):
                pe.wait_ge(s["q_ready"], b + 1)
                pe.wait_ge(s["vo_ready"], b)
                pe.matmul(vv[0:S2, 0:D], k_t[p][:, 0, :], w["L0_xattn_Wv1"][:, :], start=True, stop=True)
                pe.matmul(vv[0:S2, D:2 * D], k_t[p][:, 1, :], w["L0_xattn_Wv2"][:, :], start=True, stop=True)
                pe.matmul(vv[0:S2, 2 * D:3 * D], xc_t[p][:, P:P + S2], k.wvo[:, :],
                          start=True, stop=True).then_inc(s["v_done"], 1)

            def score(b, p, c):
                if c == 0:
                    pe.wait_ge(s["wide_ready"], b + 1)
                if not (is_(b, 0) and c < 2):
                    pe.wait_ge(s["probs_ready"], CH * b + c - 1)
                for j in range(2):
                    q0 = QUAD * (2 * (c % 2) + j)
                    mm = pe.matmul(scores[c % 2][0:S2, j, :], k_t[p][q0:q0 + QUAD, c // 2, :],
                                   q_wide[p][q0:q0 + QUAD, :, :], start=True, stop=True)
                mm.then_inc(s["scores_done"], 1)

            def shift(b, c):
                pe.wait_ge(s["max_ready"], CH * b + c + 1)
                for j in range(2):
                    mm = pe.matmul(scores[c % 2][0:S2, j, :], k.identb[0:S2, 0:S2],
                                   maxima[0:S2, c % 2, HQ * j:HQ * (j + 1)].unsqueeze(2).broadcast_to([S2, HQ, P]),
                                   start=False, stop=True, skip_group_check=True)
                mm.then_inc(s["shifted"], 1)

            def weigh(b, p):
                pe.wait_ge(s["v_heads_ready"], CH * b + CH)
                pe.wait_ge(s["out_ready"], b)
                for n in range(2 * HQ):
                    for j in range(H // HQ):
                        h = HQ * j + n % HQ
                        mm = pe.matmul(pv[QUAD * j:QUAD * (j + 1), 0:P], v_heads[p][0:S2, n // HQ, h, :],
                                       probs[p][0:S2, n // HQ, h, :], start=(n == 0), stop=(n == 2 * HQ - 1))
                mm.then_inc(s["pv_done"], 1)

            def turn_output(b):
                pe.wait_ge(s["o_ready"], b + 1)
                pe.transpose(pv[:, P:2 * P], o_t[:, :], k.ident[:, :]).then_inc(s["o_turned"], 1)

            def step(b, p):
                last = is_(b, NB - 1)
                score(b, p, 1)
                shift(b, 0)
                if not last:
                    turn_inputs(b + 1, 1 - p)
                score(b, p, 2)
                shift(b, 1)
                if not is_(b, 0):
                    weigh(b - 1, 1 - p)
                if not last:
                    project(b + 1, 1 - p)
                score(b, p, 3)
                shift(b, 2)
                if not is_(b, 0):
                    turn_output(b - 1)
                if not last:
                    values(b + 1, 1 - p)
                    score(b + 1, 1 - p, 0)
                shift(b, 3)

            def last():
                weigh(NB - 1, 1)
                turn_output(NB - 1)

            turn_inputs(0, 0)
            project(0, 0)
            values(0, 0)
            score(0, 0, 0)
            all_sequences(pe, step, last)

        @block.scalar
        def _(act):
            def copy_turned(b, p):
                pe_done = s["turned"]
                act.wait_ge(pe_done, b + 1)
                if not (isinstance(b, int) and b < 2):
                    act.wait_ge(s["v_done"], b - 1)
                act.activation(xc_t[p][:, 0:P], turned[:, 0:P], ACT.Copy)
                act.activation(xc_t[p][:, P:P + S2], turned[:, P + S2 - 1:P - 1:-1], ACT.Copy).then_inc(s["xc_ready"], 1)

            def bias_qk(b, p):
                act.wait_ge(s["qk_done"], b + 1)
                if not (isinstance(b, int) and b < 2):
                    act.wait_ge(s["scores_done"], CH * b - CH)
                    act.wait_ge(s["v_done"], b - 1)
                    act.wait_ge(s["wide_ready"], b - 1)
                    act.wait_ge(s["o_ready"], b - 1)
                act.activation(q_t[p][:, :], qk[:, 0:P], ACT.Identity, bias=w["L0_xattn_bq"][:, 0:1])
                act.activation(k_t[p][:, 0, :], qk[:, P:P + S2], ACT.Identity, bias=w["L0_xattn_bk1"][:, 0:1])
                act.activation(k_t[p][:, 1, :], qk[:, 2 * P:2 * P + S2], ACT.Identity,
                               bias=w["L0_xattn_bk2"][:, 0:1]).then_inc(s["q_ready"], 1)

            def exponent(b, p, c):
                act.wait_ge(s["shifted"], CH * b + c + 1)
                if c == 0 and not (isinstance(b, int) and b < 2):
                    act.wait_ge(s["pv_done"], b - 1)
                h0 = HC * (c % 2)
                act.activation(probs[p][0:S2, c // 2, h0:h0 + HC, :].rearrange("p h q -> p (h q)"),
                               scores[c % 2][0:S2, :, :].rearrange("p j q -> p (j q)"),
                               ACT.Exp, scale=SCALE).then_inc(s["probs_ready"], 1)

            def step(b, p):
                last = is_(b, NB - 1)
                exponent(b, p, 0)
                if not last:
                    copy_turned(b + 1, 1 - p)
                exponent(b, p, 1)
                if not last:
                    bias_qk(b + 1, 1 - p)
                exponent(b, p, 2)
                exponent(b, p, 3)

            copy_turned(0, 0)
            bias_qk(0, 0)
            all_sequences(act, step, lambda: None)

        @block.gpsimd
        def _(pool):
            def spread(b, p):
                pool.wait_ge(s["q_ready"], b + 1)
                if not (isinstance(b, int) and b < 2):
                    pool.wait_ge(s["scores_done"], CH * b - CH)
                pool.tensor_tensor(q_wide[p][:, :, :], q_t[p][:, :].unsqueeze(1).broadcast_to([P, HQ, P]),
                                   k.headmask[:, :].unsqueeze(2).broadcast_to([P, HQ, P]),
                                   ALU.mult).then_inc(s["wide_ready"], 1)

            def scale_values(b, p, c):
                pool.wait_ge(s["rsums_ready"], CH * b + c + 1)
                if c == 0:
                    pool.wait_ge(s["v_ready"], b + 1)
                    if not (isinstance(b, int) and b < 2):
                        pool.wait_ge(s["pv_done"], b - 1)
                for j in range(2):
                    jj = 2 * (c % 2) + j
                    own = v_heads[p][0:S2, c // 2, HQ * jj:HQ * (jj + 1), :].rearrange("p h c -> p (h c)")
                    own = own.rearrange("p (h c) -> p h c", c=QUAD)
                    v0 = D * (c // 2) + QUAD * jj
                    t = v_heads[p][0:S2, c // 2, HQ * jj:HQ * (jj + 1), :]
                    diag = bass.AP(tensor=t.tensor, offset=t.offset,
                                   ap=[list(t.ap[0]), [QUAD + DH, HQ], [1, DH]])
                    op = pool.tensor_tensor(
                        diag, v_sb[p][0:S2, v0:v0 + QUAD].rearrange("p (h d) -> p h d", d=DH),
                        rsums[0:S2, c, HQ * j:HQ * (j + 1)].unsqueeze(2).broadcast_to([S2, HQ, DH]), ALU.mult)
                op.then_inc(s["v_heads_ready"], 1)

            def step(b, p):
                last = is_(b, NB - 1)
                if not is_(b, 0):
                    scale_values(b - 1, 1 - p, 3)
                scale_values(b, p, 0)
                if not last:
                    spread(b + 1, 1 - p)
                scale_values(b, p, 1)
                scale_values(b, p, 2)

            for p in range(2):
                pool.memset(v_heads[p][:, :, :, :], 0.0).then_inc(s["zeroed"], 1)
            pool.wait_ge(s["zeroed"], 2)
            spread(0, 0)
            all_sequences(pool, step, lambda: scale_values(NB - 1, 1, 3))

        @block.vector
        def _(dve):
            def normalise(b, p):
                if not (isinstance(b, int) and b < 2):
                    dve.wait_ge(s["turned"], b - 1)
                dve.tensor_scalar(xn[p][:, :], k.x_res[:, b, :], k.mean[:, bass.ds(b, 1)], k.rstd[:, bass.ds(b, 1)],
                                  ALU.subtract, ALU.mult).then_inc(s["xn_ready"], 1)

            def bias_values(b, p):
                dve.wait_ge(s["v_done"], b + 1)
                if not (isinstance(b, int) and b < 2):
                    dve.wait_ge(s["v_heads_ready"], CH * b - CH)
                dve.tensor_tensor(v_sb[p][0:S2, :], vv[0:S2, 0:2 * D], k.v_bias[0:S2, :],
                                  ALU.add).then_inc(s["v_ready"], 1)
                dve.tensor_tensor(k.vo_res[0:S2, b, :], vv[0:S2, 2 * D:3 * D], k.bvo[0:S2, :],
                                  ALU.add).then_inc(s["vo_ready"], 1)

            def maximum(b, c):
                dve.wait_ge(s["scores_done"], CH * b + c + 1)
                if not (is_(b, 0) and c < 2):
                    dve.wait_ge(s["shifted"], CH * b + c - 1)
                dve.tensor_reduce(maxima[0:S2, c % 2, :],
                                  scores[c % 2][0:S2, :, :].rearrange("p j (h q) -> p (j h) q", q=P),
                                  AX.X, ALU.max, negate=True).then_inc(s["max_ready"], 1)

            def total(b, p, c):
                dve.wait_ge(s["probs_ready"], CH * b + c + 1)
                h0 = HC * (c % 2)
                dve.tensor_reduce(sums[0:S2, c % 2, :], probs[p][0:S2, c // 2, h0:h0 + HC, :],
                                  AX.X, ALU.add).then_inc(s["sums_ready"], 1)
                dve.wait_ge(s["sums_ready"], CH * b + c + 1)
                if not is_(b, 0):
                    dve.wait_ge(s["v_heads_ready"], CH * b + c - CH + 1)
                dve.reciprocal(rsums[0:S2, c, :], sums[0:S2, c % 2, :]).then_inc(s["rsums_ready"], 1)

            def add_queries(b, p):
                dve.wait_ge(s["pv_done"], b + 1)
                dve.wait_ge(s["o_turned"], b)
                dve.tensor_tensor(o_t[:, :], pv[:, 0:P], q_t[p][:, :], ALU.add).then_inc(s["o_ready"], 1)

            def keep_output(b):
                dve.wait_ge(s["o_turned"], b + 1)
                dve.bn_stats(k.stats[:, b, :], pv[:, P:2 * P]).then_inc(s["stats"], 1)
                dve.tensor_copy(k.tmp_res[:, b, :], pv[:, P:2 * P]).then_inc(s["out_ready"], 1)

            def step(b, p):
                first, last = is_(b, 0), is_(b, NB - 1)
                maximum(b, 0)
                if not first:
                    total(b - 1, 1 - p, 3)
                if not last:
                    normalise(b + 1, 1 - p)
                maximum(b, 1)
                total(b, p, 0)
                if not first:
                    add_queries(b - 1, 1 - p)
                maximum(b, 2)
                total(b, p, 1)
                if not first:
                    keep_output(b - 1)
                if not last:
                    bias_values(b + 1, 1 - p)
                maximum(b, 3)
                total(b, p, 2)

            def last():
                total(NB - 1, 1, 3)
                add_queries(NB - 1, 1)
                keep_output(NB - 1)
                dve.wait_ge(s["out_ready"], NB)
                dve.wait_ge(s["stats"], NB)

            normalise(0, 0)
            bias_values(0, 0)
            all_sequences(dve, step, last)



def build_rstd(k, name, composed=False):
    nc = k.nc
    link = Chain(k.sem(name + "_chain"))
    eps_added = k.sem(name + "_eps_added")
    root_done = k.sem(name + "_root_done")
    with nc.Block() as block:
        @block.scalar
        def _(act):
            act.wait_ge(eps_added, 1)
            act.activation(k.rstd[:, :], k.rstd[:, :], ACT.Sqrt).then_inc(root_done, 1)
            if composed:
                act.wait_ge(eps_added, 2)
                act.activation(k.rstd2[:, :], k.rstd2[:, :], ACT.Sqrt).then_inc(root_done, 1)

        @block.vector
        def _(dve):
            combine_stats(k, dve, link)
            dve.tensor_scalar(k.rstd[:, :], k.var[:, :], EPS, None, ALU.add).then_inc(eps_added, 1)
            dve.wait_ge(root_done, 1)
            link(dve, dve.reciprocal(k.rstd[:, :], k.rstd[:, :]))
            if composed:
                link(dve, dve.tensor_tensor(k.rstd2[:, :], k.rstd[:, :], k.rstd[:, :], ALU.mult))
                link(dve, dve.tensor_tensor(k.rstd2[:, :], k.rstd2[:, :], k.var[:, :], ALU.mult))
                dve.tensor_scalar(k.rstd2[:, :], k.rstd2[:, :], EPS, None, ALU.add).then_inc(eps_added, 1)
                dve.wait_ge(root_done, 2)
                link(dve, dve.reciprocal(k.rstd2[:, :], k.rstd2[:, :]))


def normalise_group(k, dve, to, of, g, rstd, done):
    for n in range(GROUP):
        b = GROUP * g + n
        dve.tensor_scalar(to[:, n, :], of[:, b, :], k.mean[:, bass.ds(b, 1)], rstd[:, bass.ds(b, 1)],
                          ALU.subtract, ALU.mult).then_inc(done, 1)


def group_of(tensor, g):
    return tensor[:, bass.ds(GROUP * g, GROUP), :]


def all_groups(eng, NB, step):
    NG = NB // GROUP
    for g in (0, 1):
        step(g, g)
    if NG > 2:
        with eng.Fori(1, NG // 2) as i:
            for p in (0, 1):
                step(2 * i + p, p)


def early(g, n=2):
    return isinstance(g, int) and g < n



def build_context_output(k):
    nc, NB, w = k.nc, k.NB, k.w
    N = GROUP * D
    with ExitStack() as ctx:
        sb = lambda n, s, dt=F32: k.sb(n, s, dt, ctx)
        normed = [sb(f"normed{p}", [P, GROUP, D]) for p in range(2)]
        o_t = [sb(f"out_t{p}", [P, N]) for p in range(2)]
        r_t = [sb(f"relu_t{p}", [P, N]) for p in range(2)]
        turned = [k.psum(f"bo_turned{p}", [P, N], ctx) for p in range(2)]
        product = [k.psum(f"bo_product{p}", [P, N], ctx) for p in range(2)]
        back = [k.psum(f"bo_back{p}", [P, N], ctx) for p in range(2)]
        s = {n: k.sem("o_" + n) for n in ("normed", "turned", "affine", "product", "relu", "sum", "back", "kept", "stats")}
        block = ctx.enter_context(nc.Block())

        @block.tensor
        def _(pe):
            def step(g, p):
                pe.wait_ge(s["normed"], GROUP * (g + 1))
                if not early(g):
                    pe.wait_ge(s["affine"], g - 1)
                for n in range(GROUP):
                    mm = pe.transpose(turned[p][:, n * P:(n + 1) * P], normed[p][:, n, :], k.ident[:, :])
                mm.then_inc(s["turned"], 1)
                pe.wait_ge(s["affine"], g + 1)
                if not early(g):
                    pe.wait_ge(s["relu"], g - 1)
                pe.matmul(product[p][:, :], w["L0_xattn_Wo"][:, :], o_t[p][:, :], start=True, stop=True).then_inc(s["product"], 1)
                pe.wait_ge(s["sum"], g + 1)
                if not early(g):
                    pe.wait_ge(s["kept"], g - 1)
                    pe.wait_ge(s["stats"], GROUP * (g - 1))
                for n in range(GROUP):
                    mm = pe.transpose(back[p][:, n * P:(n + 1) * P], r_t[p][:, n * P:(n + 1) * P], k.ident[:, :])
                mm.then_inc(s["back"], 1)
            all_groups(pe, NB, step)

        @block.scalar
        def _(act):
            def step(g, p):
                act.wait_ge(s["turned"], g + 1)
                if not early(g):
                    act.wait_ge(s["sum"], g - 1)
                act.activation(o_t[p][:, :], turned[p][:, :], ACT.Identity, bias=w["L0_xattn_beta0"][:, 0:1],
                               scale=w["L0_xattn_g0"][:, 0:1]).then_inc(s["affine"], 1)
                act.wait_ge(s["product"], g + 1)
                if not early(g):
                    act.wait_ge(s["back"], g - 1)
                act.activation(r_t[p][:, :], product[p][:, :], ACT.Relu,
                               bias=w["L0_xattn_bo"][:, 0:1]).then_inc(s["relu"], 1)
            all_groups(act, NB, step)

        @block.gpsimd
        def _(pool):
            def step(g, p):
                pool.wait_ge(s["relu"], g + 1)
                pool.tensor_tensor(r_t[p][:, :], r_t[p][:, :], o_t[p][:, :], ALU.add).then_inc(s["sum"], 1)
            all_groups(pool, NB, step)

        @block.vector
        def _(dve):
            def step(g, p):
                if not early(g):
                    dve.wait_ge(s["turned"], g - 1)
                normalise_group(k, dve, normed[p], k.tmp_res, g, k.rstd, s["normed"])
                if not early(g, 1):
                    finish(g - 1, 1 - p)

            def finish(g, p):
                dve.wait_ge(s["back"], g + 1)
                for n in range(GROUP):
                    dve.bn_stats(k.stats[:, GROUP * g + n, :], back[p][:, n * P:(n + 1) * P]).then_inc(s["stats"], 1)
                dve.tensor_copy(group_of(k.tmp_res, g), back[p][:, :].rearrange("p (n d) -> p n d", d=D)).then_inc(s["kept"], 1)
            all_groups(dve, NB, step)
            finish(NB // GROUP - 1, 1)
            dve.wait_ge(s["kept"], NB // GROUP)


def build_context_residual(k):
    nc, NB = k.nc, k.NB
    with ExitStack() as ctx:
        normed = [k.sb(f"r_normed{p}", [P, GROUP, D], F32, ctx) for p in range(2)]
        s = {n: k.sem("r_" + n) for n in ("normed", "scaled", "moved", "added", "stats")}
        block = ctx.enter_context(nc.Block())

        def rows(t):
            return t[:, :].unsqueeze(1).broadcast_to([P, GROUP, D])

        @block.gpsimd
        def _(pool):
            def step(g, p):
                pool.wait_ge(s["normed"], GROUP * (g + 1))
                pool.tensor_tensor(normed[p][:, :, :], normed[p][:, :, :], rows(k.g1_rows), ALU.mult).then_inc(s["scaled"], 1)
                pool.wait_ge(s["scaled"], g + 1)
                pool.tensor_tensor(normed[p][:, :, :], normed[p][:, :, :], rows(k.beta1_rows), ALU.add).then_inc(s["moved"], 1)
            all_groups(pool, NB, step)

        @block.vector
        def _(dve):
            def step(g, p):
                if not early(g):
                    dve.wait_ge(s["added"], g - 1)
                normalise_group(k, dve, normed[p], k.tmp_res, g, k.rstd, s["normed"])
                if not early(g, 1):
                    finish(g - 1, 1 - p)

            def finish(g, p):
                dve.wait_ge(s["moved"], g + 1)
                dve.tensor_tensor(group_of(k.x_res, g), group_of(k.x_res, g), normed[p][:, :, :], ALU.add).then_inc(s["added"], 1)
                dve.wait_ge(s["added"], g + 1)
                for n in range(GROUP):
                    dve.bn_stats(k.stats[:, GROUP * g + n, :], k.x_res[:, GROUP * g + n, :]).then_inc(s["stats"], 1)
            all_groups(dve, NB, step)
            finish(NB // GROUP - 1, 1)
            dve.wait_ge(s["stats"], NB)



class Experts:

    def __init__(self, name, inner, down_chunks, top, act):
        self.name, self.inner, self.chunks, self.top, self.act = name, inner, down_chunks, top, act

    def tiles(self, NB):
        return self.top * NB + E


def build_prepare(k, m, columns, affine, gate_bias):
    nc, NB = k.nc, k.NB
    n_cols = columns.shape[1]
    source = k.tmp_res if affine else k.x_res
    with ExitStack() as ctx:
        sb = lambda n, s_, dt=F32: k.sb(m.name + n, s_, dt, ctx)
        xn = [sb(f"pn{p}", [P, D]) for p in range(2)]
        xa = [sb(f"pa{p}", [P, D]) for p in range(2)] if affine else xn
        x_t = [sb(f"pt{p}", [P, P]) for p in range(2)]
        turned = [k.psum(f"{m.name}pturn{p}", [P, 512], ctx) for p in range(2)]
        logit = [k.psum(f"{m.name}plogit{p}", [P, 512], ctx) for p in range(2)]
        s = {n: k.sem(m.name + "p_" + n) for n in ("normed", "scaled", "moved", "turned", "copied", "logits", "kept", "logits_kept", "bias")}
        stored = [k.sem(f"{m.name}p_stored{p}") for p in range(2)]
        block = ctx.enter_context(nc.Block())

        def each(eng, step):
            for b in (0, 1):
                step(b, b)
            with eng.Fori(1, NB // 2) as i:
                for p in (0, 1):
                    step(2 * i + p, p)

        @block.sync
        def _(sp):
            def step(b, p):
                sp.wait_ge(s["moved"] if affine else s["normed"], b + 1)
                sp.dma_start(k.xf_dram[bass.ds(b * P, P), :], xa[p][:, :]).then_inc(stored[p], 16)
            each(sp, step)
            for p in range(2):
                sp.wait_ge(stored[p], 8 * NB)

        @block.tensor
        def _(pe):
            def logits(b, p):
                pe.wait_ge(s["copied"], b + 1)
                if not early(b):
                    pe.wait_ge(s["logits_kept"], b - 1)
                pe.matmul(logit[p][:, 0:n_cols], x_t[p][:, :], columns, start=True, stop=True).then_inc(s["logits"], 1)

            def step(b, p):
                pe.wait_ge(s["normed"], b + 1)
                if not early(b):
                    pe.wait_ge(s["copied"], b - 1)
                pe.transpose(turned[p][:, 0:P], xn[p][:, :], k.ident[:, :]).then_inc(s["turned"], 1)
                if not early(b, 1):
                    logits(b - 1, 1 - p)
            each(pe, step)
            logits(NB - 1, 1)

        @block.scalar
        def _(act):
            def step(b, p):
                act.wait_ge(s["turned"], b + 1)
                if not early(b):
                    act.wait_ge(s["logits"], b - 1)
                    act.wait_ge(s["kept"], b - 1)
                if affine:
                    act.activation(x_t[p][:, :], turned[p][:, 0:P], ACT.Identity, bias=affine[1][:, 0:1],
                                   scale=affine[0][:, 0:1]).then_inc(s["copied"], 1)
                else:
                    act.activation(x_t[p][:, :], turned[p][:, 0:P], ACT.Copy).then_inc(s["copied"], 1)
            each(act, step)

        if affine:
            @block.gpsimd
            def _(pool):
                def step(b, p):
                    pool.wait_ge(s["normed"], b + 1)
                    if not early(b):
                        pool.wait_ge(stored[p], 8 * (b - p))
                    pool.tensor_tensor(xa[p][:, :], xn[p][:, :], affine[2][:, :], ALU.mult).then_inc(s["scaled"], 1)
                    pool.wait_ge(s["scaled"], b + 1)
                    pool.tensor_tensor(xa[p][:, :], xa[p][:, :], affine[3][:, :], ALU.add).then_inc(s["moved"], 1)
                each(pool, step)

        @block.vector
        def _(dve):
            def keep(b, p):
                dve.wait_ge(s["copied"], b + 1)
                dve.tensor_scalar(k.tmp_res[:, b, :], x_t[p][:, :], 1.0, None, ALU.mult).then_inc(s["kept"], 1)
                dve.wait_ge(s["logits"], b + 1)
                if gate_bias is None:
                    dve.tensor_scalar(k.logits[:, b, 0:n_cols], logit[p][:, 0:n_cols], k.rstd2[:, bass.ds(b, 1)], None,
                                      ALU.mult).then_inc(s["logits_kept"], 1)
                else:
                    dve.tensor_tensor(k.logits[:, b, 0:n_cols], logit[p][:, 0:n_cols], gate_bias[:, :],
                                      ALU.add).then_inc(s["logits_kept"], 1)

            def step(b, p):
                if not early(b):
                    dve.wait_ge(s["turned"], b - 1)
                    if affine:
                        dve.wait_ge(s["scaled"], b - 1)
                    else:
                        dve.wait_ge(stored[p], 8 * (b - p))
                dve.tensor_scalar(xn[p][:, :], source[:, b, :], k.mean[:, bass.ds(b, 1)], k.rstd[:, bass.ds(b, 1)],
                                  ALU.subtract, ALU.mult).then_inc(s["normed"], 1)
                if not early(b, 1):
                    keep(b - 1, 1 - p)
            each(dve, step)
            keep(NB - 1, 1)
            dve.wait_ge(s["logits_kept"], NB)


def build_route(k, m, logit_bias):
    nc, NB, NT = k.nc, k.NB, m.tiles(k.NB)
    with ExitStack() as ctx:
        sb = lambda n, s_, dt=F32: k.sb(m.name + n, s_, dt, ctx)
        t0, t1, probs, counts = (sb(n, [P, NB, E]) for n in ("rt0", "rt1", "rprobs", "rcounts"))
        chosen = [sb(f"rchosen{j}", [P, NB, E]) for j in range(2)]
        both = sb("rboth", [P, NB, E], BF16)
        triangle = sb("rtriangle", [P, P], BF16)
        ones = sb("rones", [P, P], BF16)
        v = [sb(f"rv{i}", [P, NB]) for i in range(3)]
        small = [sb(f"rs{i}", [P, E]) for i in range(4)]
        small_i = sb("rsi", [P, E], I32)
        tile_cmp = sb("rcmp", [P, NT, E])
        tile_of = sb("rtile", [P, NT])
        ranks = k.psum(m.name + "ranks", [P, NB * E], ctx)
        totals = k.psum(m.name + "totals", [P, NB * E], ctx)
        link = Chain(k.sem(m.name + "r_chain"))
        ready, exp_done, counted = (k.sem(m.name + "r_" + n) for n in ("shifted", "exp_done", "counted"))
        onehots = k.sem(m.name + "r_onehots")
        block = ctx.enter_context(nc.Block())

        def over_e(t):
            return t[:, :].unsqueeze(2).broadcast_to([P, NB, E])

        def over_b(t):
            return t[:, 0:E].unsqueeze(1).broadcast_to([P, NB, E])

        n_exp = 2 if m.top == 1 else 1

        @block.scalar
        def _(act):
            act.wait_ge(ready, 1)
            act.activation(probs[:, :, :], t0[:, :, :], ACT.Exp).then_inc(exp_done, 1)
            if n_exp == 2:
                act.wait_ge(ready, 2)
                act.activation(k.coef[:, :, :], k.coef[:, :, :], ACT.Exp).then_inc(exp_done, 1)

        @block.tensor
        def _(pe):
            pe.wait_ge(onehots, 1)
            pe.matmul(ranks[:, :], triangle[:, :], both[:, :, :], start=True, stop=True)
            pe.matmul(totals[:, :], ones[:, :], both[:, :, :], start=True, stop=True).then_inc(counted, 1)

        @block.vector
        def _(dve):
            def do(op):
                link(dve, op)

            TT, TS = dve.tensor_tensor, dve.tensor_scalar
            do(dve.tensor_copy(triangle[:, :], k.tables[:, 0:P]))
            do(dve.memset(ones[:, :], 1.0))
            L = k.logits[:, :, 0:E]
            if logit_bias is not None:
                do(TT(L, L, over_b(logit_bias), ALU.add))
            do(dve.tensor_reduce(v[0][:, :], L, AX.X, ALU.max))
            TT(t0[:, :, :], L, over_e(v[0]), ALU.subtract).then_inc(ready, 1)
            if n_exp == 2:
                C = k.logits[:, :, E:E + 2]
                do(dve.tensor_reduce(v[1][:, :], C, AX.X, ALU.max))
                TT(k.coef[:, :, :], C, v[1][:, :].unsqueeze(2).broadcast_to([P, NB, 2]), ALU.subtract).then_inc(ready, 1)
                dve.wait_ge(exp_done, 2)
                do(dve.tensor_reduce(v[1][:, :], k.coef[:, :, :], AX.X, ALU.add))
                do(dve.reciprocal(v[1][:, :], v[1][:, :]))
                do(TT(k.coef[:, :, :], k.coef[:, :, :], v[1][:, :].unsqueeze(2).broadcast_to([P, NB, 2]), ALU.mult))
            dve.wait_ge(exp_done, 1)
            do(dve.tensor_reduce(v[0][:, :], probs[:, :, :], AX.X, ALU.add))
            do(dve.reciprocal(v[0][:, :], v[0][:, :]))
            do(TT(probs[:, :, :], probs[:, :, :], over_e(v[0]), ALU.mult))
            for j in range(m.top):
                best = k.choice_w[j]
                do(dve.tensor_reduce(best[:, :], probs[:, :, :], AX.X, ALU.max))
                do(TT(t0[:, :, :], probs[:, :, :], over_e(best), ALU.is_equal))
                do(dve.scalar_tensor_tensor(out=t1[:, :, :], in0=t0[:, :, :], scalar=-float(E),
                                            in1=over_b(k.tables[:, P:P + E]), op0=ALU.mult, op1=ALU.add))
                do(dve.tensor_reduce(v[1][:, :], t1[:, :, :], AX.X, ALU.min))
                do(TS(v[1][:, :], v[1][:, :], float(E), None, ALU.add))
                do(TT(chosen[j][:, :, :], over_b(k.tables[:, P:P + E]), over_e(v[1]), ALU.is_equal))
                if j + 1 < m.top:
                    do(dve.scalar_tensor_tensor(out=probs[:, :, :], in0=chosen[j][:, :, :], scalar=-2.0,
                                                in1=probs[:, :, :], op0=ALU.mult, op1=ALU.add))
            if m.top == 2:
                TT(both[:, :, :], chosen[0][:, :, :], chosen[1][:, :, :], ALU.add).then_inc(onehots, 1)
                do(TT(v[0][:, :], k.choice_w[0][:, :], k.choice_w[1][:, :], ALU.add))
                do(TS(v[0][:, :], v[0][:, :], EPS, None, ALU.add))
                do(dve.reciprocal(v[0][:, :], v[0][:, :]))
                for j in range(2):
                    do(TT(k.choice_w[j][:, :], k.choice_w[j][:, :], v[0][:, :], ALU.mult))
            else:
                dve.tensor_copy(both[:, :, :], chosen[0][:, :, :]).then_inc(onehots, 1)
                do(TT(k.choice_w[0][:, :], k.choice_w[0][:, :], k.coef[:, :, 0], ALU.mult))
            dve.wait_ge(counted, 1)
            do(dve.tensor_copy(counts[:, :, :], totals[:, :].rearrange("p (b e) -> p b e", e=E)))
            a, b_, shift = counts, t0, 1
            while shift < NB:
                dve.tensor_copy(b_[:, 0:shift, :], a[:, 0:shift, :]).then_inc(link.sem, 1)
                link.n += 1
                do(TT(b_[:, shift:NB, :], a[:, shift:NB, :], a[:, 0:NB - shift, :], ALU.add))
                a, b_ = b_, (t1 if b_ is t0 else t0)
                shift *= 2
            do(TS(small_i[:, :], a[:, NB - 1, :], float(P - 1), None, ALU.add))
            do(TS(small_i[:, :], small_i[:, :], 7, None, ALU.arith_shift_right))
            do(dve.tensor_copy(small[0][:, :], small_i[:, :]))
            ea, eb, shift = small[0], small[1], 1
            while shift < E:
                dve.tensor_copy(eb[:, 0:shift], ea[:, 0:shift]).then_inc(link.sem, 1)
                link.n += 1
                do(TT(eb[:, shift:E], ea[:, shift:E], ea[:, 0:E - shift], ALU.add))
                ea, eb = eb, (small[2] if eb is small[1] else small[1])
                shift *= 2
            do(TT(small[3][:, :], ea[:, :], small[0][:, :], ALU.subtract))
            do(TS(small[3][:, :], small[3][:, :], float(P), None, ALU.mult))
            rest = t1 if a is t0 else t0
            do(TT(rest[:, :, :], a[:, :, :], counts[:, :, :], ALU.subtract))
            do(TT(rest[:, :, :], rest[:, :, :], over_b(small[3]), ALU.add))
            do(TT(rest[:, :, :], ranks[:, :].rearrange("p (b e) -> p b e", e=E), rest[:, :, :], ALU.add))
            for j in range(m.top):
                do(TT(chosen[j][:, :, :], chosen[j][:, :, :], rest[:, :, :], ALU.mult))
                do(dve.tensor_reduce(v[1][:, :], chosen[j][:, :, :], AX.X, ALU.add))
                do(dve.tensor_copy(k.place[j][:, :], v[1][:, :]))
            tile_no = k.tables[:, P + E:P + E + NT]
            do(TT(tile_cmp[:, :, :], tile_no.unsqueeze(2).broadcast_to([P, NT, E]),
                  ea[:, :].unsqueeze(1).broadcast_to([P, NT, E]), ALU.is_ge))
            do(dve.tensor_reduce(tile_of[:, :], tile_cmp[:, :, :], AX.X, ALU.add))
            do(TS(k.slot_expert[:, 0:NT], tile_of[:, :], float(E - 1), None, ALU.min))


def build_dispatch(k, m):
    nc, NB = k.nc, k.NB
    RING = 4
    with ExitStack() as ctx:
        rows = [k.sb(f"{m.name}drow{r}", [P, D], F32, ctx) for r in range(RING)]
        places = [[k.sb(f"{m.name}dplace{r}_{j}", [P, 1], I32, ctx) for j in range(m.top)] for r in range(RING)]
        loaded = [k.sem(f"{m.name}d_loaded{r}") for r in range(RING)]
        sent = [k.pool_dma_sem(f"{m.name}d_sent{r}") for r in range(RING)]
        placed = k.sem(m.name + "d_placed")
        go = k.sem(m.name + "d_go")
        block = ctx.enter_context(nc.Block())
        per = 16 * m.top

        @block.sync
        def _(sp):
            for r in range(RING):
                sp.dma_start(rows[r][:, :], k.xf_dram[r * P:(r + 1) * P, :]).then_inc(loaded[r], 16)
            with sp.Fori(1, NB // RING) as i:
                for r in range(RING):
                    sp.wait_ge(sent[r], per * i)
                    sp.dma_start(rows[r][:, :], k.xf_dram[bass.ds((RING * i + r) * P, P), :]).then_inc(loaded[r], 16)

        @block.gpsimd
        def _(pool):
            def step(i, r):
                b = RING * i + r
                if not early(i, 1):
                    pool.wait_ge(sent[r], per * i)
                for j in range(m.top):
                    pool.tensor_copy(places[r][j][:, :], k.place[j][:, bass.ds(b, 1)]).then_inc(placed, 1)
                pool.wait_ge(placed, m.top * (b + 1))
                pool.wait_ge(loaded[r], 16 * i + 16)
                pool.sem_inc(go, 1)
                for j in range(m.top):
                    pool.indirect_dma_start(k.slots, bass.IndirectOffsetOnAxis(places[r][j][:, 0:1], 0),
                                            rows[r][:, :], None).then_inc(sent[r], 16)
            for r in range(RING):
                step(0, r)
            with pool.Fori(1, NB // RING) as i:
                for r in range(RING):
                    step(i, r)
            for r in range(RING):
                pool.wait_ge(sent[r], per * (NB // RING))


def build_experts(k, m, up, down, up_bias=None, down_bias=None):
    nc, NT = k.nc, m.tiles(k.NB)
    C = m.chunks
    with ExitStack() as ctx:
        sb = lambda n, s_, dt=F32: k.sb(m.name + n, s_, dt, ctx)
        x_in = [sb(f"ex{p}", [P, D]) for p in range(2)]
        x_t = [sb(f"ext{p}", [P, P]) for p in range(2)]
        g = [sb(f"eg{p}", [P, 512]) for p in range(2)]
        h = [sb(f"eh{p}", [P, C * P]) for p in range(2)]
        h_t = [sb(f"eht{p}", [P, C * P]) for p in range(2)]
        y = [sb(f"ey{p}", [P, D]) for p in range(2)]
        turned = [k.psum(f"{m.name}eturn{p}", [P, 512], ctx) for p in range(2)]
        hidden = [k.psum(f"{m.name}ehid{p}", [P, 512], ctx) for p in range(2)]
        h_turned = [k.psum(f"{m.name}ehturn{p}", [P, 512], ctx) for p in range(2)]
        result = [k.psum(f"{m.name}eres{p}", [P, 512], ctx) for p in range(2)]
        loaded = [k.sem(f"{m.name}e_loaded{p}") for p in range(2)]
        stored = [k.sem(f"{m.name}e_stored{p}") for p in range(2)]
        s = {n: k.sem(m.name + "e_" + n) for n in
             ("turned", "x_ready", "hidden", "biased", "gated", "h_ready", "h_turned", "h_t_ready", "result", "y_ready")}
        block = ctx.enter_context(nc.Block())

        def each(eng, step):
            for i in (0, 1):
                step(i, i)
            with eng.Fori(1, NT // 2 - 1) as i:
                for p in (0, 1):
                    step(2 * i + p, p)
            for i in (NT - 2, NT - 1):
                step(i, i % 2)

        @block.sync
        def _(sp):
            def load(i, p):
                if not early(i):
                    sp.wait_ge(s["turned"], i - 1)
                sp.dma_start(x_in[p][:, :], k.slots[bass.ds(i * P, P), :]).then_inc(loaded[p], 16)

            def step(i, p):
                if not (isinstance(i, int) and i == NT - 1):
                    load(i + 1, 1 - p)
                if not early(i, 1):
                    store(i - 1, 1 - p)

            def store(i, p):
                sp.wait_ge(s["y_ready"], i + 1)
                sp.dma_start(k.results[bass.ds(i * P, P), :], y[p][:, :]).then_inc(stored[p], 16)
            load(0, 0)
            each(sp, step)
            store(NT - 1, 1)
            for p in range(2):
                sp.wait_ge(stored[p], 8 * NT)

        @block.tensor
        def _(pe):
            def turn_x(i, p):
                pe.wait_ge(loaded[p], 8 * (i - p) + 16)
                if not early(i):
                    pe.wait_ge(s["x_ready"], i - 1)
                pe.transpose(turned[p][:, 0:P], x_in[p][:, :], k.ident[:, :]).then_inc(s["turned"], 1)

            def turn_h(i, p):
                pe.wait_ge(s["h_ready"], i + 1)
                if not early(i):
                    pe.wait_ge(s["h_t_ready"], i - 1)
                for c in range(C):
                    mm = pe.transpose(h_turned[p][:, c * P:(c + 1) * P], h[p][:, c * P:(c + 1) * P], k.ident[:, :])
                mm.then_inc(s["h_turned"], 1)

            def go_down(i, p, e):
                pe.wait_ge(s["h_t_ready"], i + 1)
                if not early(i):
                    pe.wait_ge(s["y_ready"], i - 1)
                for c in range(C):
                    mm = pe.matmul(result[p][:, 0:D], h_t[p][:, c * P:(c + 1) * P], down[:, e, c, :],
                                   start=(c == 0), stop=(c == C - 1))
                mm.then_inc(s["result"], 1)

            def expert(i):
                return pe.value_load(k.slot_expert[0:1, bass.ds(i, 1)], min_val=0, max_val=E - 1)

            def go_up(i, p):
                pe.wait_ge(s["x_ready"], i + 1)
                if not early(i):
                    pe.wait_ge(s["biased" if up_bias is not None else "h_ready"], i - 1)
                pe.matmul(hidden[p][:, :], x_t[p][:, :], up[:, expert(i), :], start=True, stop=True).then_inc(s["hidden"], 1)

            def step(i, p):
                if not early(i, 1):
                    turn_h(i - 1, 1 - p)
                if not (isinstance(i, int) and i == NT - 1):
                    turn_x(i + 1, 1 - p)
                go_up(i, p)
                if not early(i, 1):
                    go_down(i - 1, 1 - p, expert(i - 1))
            turn_x(0, 0)
            each(pe, step)
            turn_h(NT - 1, 1)
            go_down(NT - 1, 1, expert(NT - 1))

        @block.scalar
        def _(act):
            def copy_x(i, p):
                act.wait_ge(s["turned"], i + 1)
                if not early(i):
                    act.wait_ge(s["hidden"], i - 1)
                act.activation(x_t[p][:, :], turned[p][:, 0:P], ACT.Copy).then_inc(s["x_ready"], 1)

            def step(i, p):
                if not (isinstance(i, int) and i == NT - 1):
                    copy_x(i + 1, 1 - p)
                if up_bias is not None:
                    act.wait_ge(s["biased"], i + 1)
                    if not early(i):
                        act.wait_ge(s["h_turned"], i - 1)
                    act.activation(h[p][:, :], g[p][:, :], m.act).then_inc(s["h_ready"], 1)
                else:
                    act.wait_ge(s["hidden"], i + 1)
                    if not early(i):
                        act.wait_ge(s["h_ready"], i - 1)
                    act.activation(g[p][:, 0:m.inner], hidden[p][:, 0:m.inner], m.act).then_inc(s["gated"], 1)
            copy_x(0, 0)
            each(act, step)

        @block.vector
        def _(dve):
            def expert(i):
                return dve.value_load(k.slot_expert[0:1, bass.ds(i, 1)], min_val=0, max_val=E - 1)

            def open_(i, p):
                if up_bias is not None:
                    e = expert(i)
                    dve.wait_ge(s["hidden"], i + 1)
                    if not early(i):
                        dve.wait_ge(s["h_ready"], i - 1)
                    dve.tensor_tensor(g[p][:, :], hidden[p][:, :], up_bias[:, e, :], ALU.add).then_inc(s["biased"], 1)
                else:
                    dve.wait_ge(s["gated"], i + 1)
                    if not early(i):
                        dve.wait_ge(s["h_turned"], i - 1)
                    dve.tensor_tensor(h[p][:, :], g[p][:, 0:m.inner], hidden[p][:, m.inner:2 * m.inner],
                                      ALU.mult).then_inc(s["h_ready"], 1)

            def copy_h(i, p):
                dve.wait_ge(s["h_turned"], i + 1)
                if not early(i):
                    dve.wait_ge(s["result"], i - 1)
                dve.tensor_copy(h_t[p][:, :], h_turned[p][:, 0:C * P]).then_inc(s["h_t_ready"], 1)

            def close(i, p):
                e = expert(i) if down_bias is not None else None
                dve.wait_ge(s["result"], i + 1)
                if not early(i):
                    dve.wait_ge(stored[p], 8 * (i - p))
                if down_bias is not None:
                    op = dve.tensor_tensor(y[p][:, :], result[p][:, 0:D], down_bias[:, e, :], ALU.add)
                else:
                    op = dve.tensor_copy(y[p][:, :], result[p][:, 0:D])
                op.then_inc(s["y_ready"], 1)

            def step(i, p):
                if not early(i, 1):
                    copy_h(i - 1, 1 - p)
                open_(i, p)
                if not early(i, 1):
                    close(i - 1, 1 - p)
            each(dve, step)
            copy_h(NT - 1, 1)
            close(NT - 1, 1)


def build_combine(k, m, s_up, s_down, shared_bias=None, stats=True):
    nc, NB = k.nc, k.NB
    N = GROUP * P
    UP = s_up.shape[1] // P
    C = m.chunks
    with ExitStack() as ctx:
        sb = lambda n, s_, dt=F32: k.sb(m.name + n, s_, dt, ctx)
        g = [sb(f"cg{c}", [P, N]) for c in range(2)]
        h_t = [[sb(f"ch{p}_{c}", [P, N]) for c in range(C)] for p in range(2)]
        rows = [[sb(f"crow{r}_{j}", [P, GROUP, D]) for j in range(m.top)] for r in range(2)]
        places = [[sb(f"cplace{r}_{j}", [P, GROUP], I32) for j in range(m.top)] for r in range(2)]
        single = [[[sb(f"cp{r}_{j}_{n}", [P, 1], I32) for n in range(GROUP)] for j in range(m.top)] for r in range(2)]
        extra = sb("cextra", [P, GROUP, D])
        hidden = [k.psum(f"{m.name}chid{c}", [P, N], ctx) for c in range(4)]
        result = [k.psum(f"{m.name}cres{p}", [P, N], ctx) for p in range(2)]
        gathered = [k.pool_dma_sem(f"{m.name}c_gathered{r}") for r in range(2)]
        s = {n: k.sem(m.name + "c_" + n) for n in
             ("placed", "go", "hidden", "gated", "h_ready", "result", "freed", "added", "first", "second", "stats", "scaled")}
        block = ctx.enter_context(nc.Block())

        @block.gpsimd
        def _(pool):
            def step(g_, p):
                if not early(g_):
                    pool.wait_ge(s["freed"], g_ - 1)
                for n in range(GROUP):
                    for j in range(m.top):
                        pool.tensor_copy(single[p][j][n][:, :], k.place[j][:, bass.ds(GROUP * g_ + n, 1)]).then_inc(s["placed"], 1)
                pool.wait_ge(s["placed"], GROUP * m.top * (g_ + 1))
                pool.sem_inc(s["go"], 1)
                for n in range(GROUP):
                    for j in range(m.top):
                        pool.indirect_dma_start(rows[p][j][:, n, :], None, k.results,
                                                bass.IndirectOffsetOnAxis(single[p][j][n][:, 0:1], 0)).then_inc(gathered[p], 16)
            all_groups(pool, NB, step)

        @block.tensor
        def _(pe):
            def go_up(g_, p):
                pe.wait_ge(s["h_ready"], C * g_)
                for c in range(UP):
                    pe.matmul(hidden[c][:, :], s_up[:, c * P:(c + 1) * P], group_of(k.tmp_res, g_),
                              start=True, stop=True).then_inc(s["hidden"], 1)

            def go_down(g_, p):
                pe.wait_ge(s["h_ready"], C * (g_ + 1))
                if not early(g_):
                    pe.wait_ge(s["added"], g_ - 1)
                for n in range(GROUP):
                    for c in range(C):
                        mm = pe.matmul(result[p][:, n * D:(n + 1) * D], h_t[p][c][:, n * P:(n + 1) * P], s_down[:, c, :],
                                       start=(c == 0), stop=(c == C - 1))
                mm.then_inc(s["result"], 1)

            def step(g_, p):
                go_up(g_, p)
                go_down(g_, p)
            all_groups(pe, NB, step)

        @block.scalar
        def _(act):
            def step(g_, p):
                for c in range(C):
                    if shared_bias is None:
                        act.wait_ge(s["hidden"], UP * g_ + c + 1)
                        if not early(g_, 1):
                            act.wait_ge(s["h_ready"], C * (g_ - 1) + c + 1)
                        act.activation(g[c][:, :], hidden[c][:, :], m.act).then_inc(s["gated"], 1)
                    else:
                        act.wait_ge(s["hidden"], UP * g_ + c + 1)
                        if c == 0 and not early(g_):
                            act.wait_ge(s["result"], g_ - 1)
                        act.activation(h_t[p][c][:, :], hidden[c][:, :], m.act,
                                       bias=shared_bias[0][:, c:c + 1]).then_inc(s["h_ready"], 1)
            all_groups(act, NB, step)

        @block.vector
        def _(dve):
            def hide(g_, p):
                if not early(g_):
                    dve.wait_ge(s["result"], g_ - 1)
                for c in range(C):
                    dve.wait_ge(s["gated"], C * g_ + c + 1)
                    dve.wait_ge(s["hidden"], UP * g_ + C + c + 1)
                    dve.tensor_tensor(h_t[p][c][:, :], g[c][:, :], hidden[C + c][:, :], ALU.mult).then_inc(s["h_ready"], 1)

            def step(g_, p):
                if shared_bias is None:
                    hide(g_, p)
                if not early(g_, 1):
                    finish(g_ - 1, 1 - p)

            def finish(g_, p):
                res = result[p][:, :].rearrange("p (n d) -> p n d", d=D)
                x4 = group_of(k.x_res, g_)
                dve.wait_ge(s["result"], g_ + 1)
                if shared_bias is None:
                    dve.tensor_tensor(x4, x4, res, ALU.add).then_inc(s["added"], 1)
                    dve.wait_ge(s["added"], g_ + 1)
                else:
                    dve.tensor_tensor(extra[:, :, :], res, shared_bias[1][:, :].unsqueeze(1).broadcast_to([P, GROUP, D]),
                                      ALU.add).then_inc(s["added"], 1)
                    dve.wait_ge(s["added"], g_ + 1)
                    for n in range(GROUP):
                        b = GROUP * g_ + n
                        dve.scalar_tensor_tensor(out=k.x_res[:, b, :], in0=extra[:, n, :], scalar=k.coef_shared[:, bass.ds(b, 1)],
                                                 in1=k.x_res[:, b, :], op0=ALU.mult, op1=ALU.add).then_inc(s["scaled"], 1)
                    dve.wait_ge(s["scaled"], GROUP * (g_ + 1))
                dve.wait_ge(gathered[p], 8 * m.top * GROUP * (g_ - p) + 16 * m.top * GROUP)
                for j in range(m.top):
                    done = s["first"] if j == 0 else s["second"]
                    for n in range(GROUP):
                        b = GROUP * g_ + n
                        dve.scalar_tensor_tensor(out=k.x_res[:, b, :], in0=rows[p][j][:, n, :],
                                                 scalar=k.choice_w[j][:, bass.ds(b, 1)], in1=k.x_res[:, b, :],
                                                 op0=ALU.mult, op1=ALU.add).then_inc(done, 1)
                    dve.wait_ge(done, GROUP * (g_ + 1))
                dve.sem_inc(s["freed"], 1)
                if stats:
                    for n in range(GROUP):
                        b = GROUP * g_ + n
                        dve.bn_stats(k.stats[:, b, :], k.x_res[:, b, :]).then_inc(s["stats"], 1)
            all_groups(dve, NB, step)
            finish(NB // GROUP - 1, 1)
            if stats:
                dve.wait_ge(s["stats"], NB)


def build_expert_layer_0(k):
    nc, ins = k.nc, k.ins
    m = Experts("m0_", 256, 2, 2, ACT.Silu)
    with ExitStack() as ctx:
        up = k.sb("m0_up", [P, E, 512], F32, ctx)
        down = k.sb("m0_down", [P, E, 2, D], F32, ctx)
        s_up = k.sb("m0_s_up", [P, 512], F32, ctx)
        s_down = k.sb("m0_s_down", [P, 2, D], F32, ctx)
        gate = k.sb("m0_gate", [P, E], F32, ctx)
        scale = k.sb("m0_scale", [P, 1], F32, ctx)
        bias = k.sb("m0_bias", [P, 1], F32, ctx)
        bias_wide = k.sb("m0_bias_wide", [P, P], F32, ctx)
        gate_scaled = k.sb("m0_gate_scaled", [P, E], F32, ctx)
        logit_bias = k.sb("m0_logit_bias", [P, E], F32, ctx)
        loaded = k.sem("m0_loaded")
        link = Chain(k.sem("m0_chain"))
        product = k.sem("m0_bias_product")
        loads = [(up[:, :, 0:256], ins["L0_ffn_Wg"].rearrange("e h i -> h e i")),
                 (up[:, :, 256:512], ins["L0_ffn_Wu"].rearrange("e h i -> h e i")),
                 (down[:, :, :, :], ins["L0_ffn_Wd"].rearrange("e (c p) h -> p e c h", p=P)),
                 (s_up[:, 0:256], ins["L0_ffn_sWg"]), (s_up[:, 256:512], ins["L0_ffn_sWu"]),
                 (s_down[:, :, :], ins["L0_ffn_sWd"].rearrange("(c p) h -> p c h", p=P)),
                 (gate[:, :], ins["L0_ffn_gate_w"].rearrange("e h -> h e")),
                 (scale[:, :], column(ins["L0_ffn_ln_scale"])), (bias[:, :], column(ins["L0_ffn_ln_bias"]))]
        with ExitStack() as inner:
            ps = k.psum("m0_bias_ps", [P, 512], inner)
            block = inner.enter_context(nc.Block())

            @block.sync
            def _(sp):
                for to, of in loads:
                    sp.dma_start(to, of, allow_slow_non_contiguous=True).then_inc(loaded, 16)

            @block.vector
            def _(dve):
                dve.wait_ge(loaded, 16 * len(loads))
                link(dve, dve.tensor_scalar(gate_scaled[:, :], gate[:, :], scale[:, 0:1], None, ALU.mult))
                link(dve, dve.tensor_copy(bias_wide[:, :], bias[:, 0:1].broadcast_to([P, P])))
                dve.wait_ge(product, 1)
                link(dve, dve.tensor_copy(logit_bias[:, :], ps[:, 0:E]))

            @block.tensor
            def _(pe):
                pe.wait_ge(link.sem, 2)
                pe.matmul(ps[:, 0:E], bias_wide[:, :], gate[:, :], start=True, stop=True).then_inc(product, 1)
        build_rstd(k, "m0_rstd", composed=True)
        build_prepare(k, m, gate_scaled[:, :], None, None)
        build_route(k, m, logit_bias)
        build_dispatch(k, m)
        build_experts(k, m, up, down)
        build_combine(k, m, s_up, s_down)



TOP_DELAYS = 9


def build_correlation(k):
    nc, ins, NB = k.nc, k.ins, k.NB
    N = GROUP * P
    with ExitStack() as ctx:
        sb = lambda n, s_, dt=F32: k.sb(n, s_, dt, ctx)
        wq, wk = sb("c_wq", [P, D]), sb("c_wk", [P, D])
        bq, bk = sb("c_bq", [1, D]), sb("c_bk", [1, D])
        dft, inverse, flip = sb("c_dft", [P, P]), sb("c_inverse", [P, P]), sb("c_flip", [P, 2 * P])
        dft_sums = sb("c_dft_sums", [1, 2, P])
        ones = sb("c_ones", [P, 1])
        xn = [sb(f"c_xn{p}", [P, GROUP, D]) for p in range(2)]
        cx = [sb(f"c_cx{p}", [P, GROUP, D]) for p in range(2)]
        xf = [sb(f"c_xf{p}", [P, N]) for p in range(2)]
        cf = [sb(f"c_cf{p}", [P, N]) for p in range(2)]
        kf = [sb(f"c_kf{p}", [P, N]) for p in range(2)]
        product = [sb(f"c_product{p}", [P, GROUP, P]) for p in range(2)]
        spectrum = sb("c_spectrum", [P, NB])
        corr, work, weight = sb("c_corr", [NB, P]), sb("c_work", [NB, P]), sb("c_weight", [NB, P])
        best, ninth = sb("c_best", [NB, 8]), sb("c_ninth", [NB, 8])
        total = sb("c_total", [NB, 1])
        weight_t = sb("c_weight_t", [P, NB])
        twice = sb("c_twice", [NB, 2 * P])
        x_spec, c_spec = k.psum("c_x_spec", [P, N], ctx), k.psum("c_c_spec", [P, N], ctx)
        q_spec, k_spec = k.psum("c_q_spec", [P, N], ctx), k.psum("c_k_spec", [P, N], ctx)
        power = k.psum("c_power", [P, 512], ctx)
        back = k.psum("c_back", [P, 512], ctx)
        loaded = k.sem("c_loaded")
        cx_loaded = [k.sem(f"c_cx_loaded{p}") for p in range(2)]
        link = Chain(k.sem("c_chain"))
        s = {n: k.sem("c_" + n) for n in ("ones_set", "normed", "x_spec", "c_spec", "xf", "cf", "q_spec", "k_spec", "kf",
                                          "product", "power", "spectrum", "corr", "shifted", "exp_done", "weighted", "turned", "turn_copied", "flipped", "twice", "stored")}
        loads = [(wq[:, :], ins["L1_xattn_Wq"]), (wk[:, :], ins["L1_xattn_Wk"]), (bq[:, :], ins["L1_xattn_bq"].unsqueeze(0)),
                 (bk[:, :], ins["L1_xattn_bk"].unsqueeze(0)), (dft[:, :], ins["c_dft"]), (inverse[:, :], ins["c_inverse"]),
                 (flip[:, :], ins["c_flip"]), (dft_sums[:, :, :], ins["c_dft_sums"].unsqueeze(0))]
        block = ctx.enter_context(nc.Block())
        NG = NB // GROUP

        @block.sync
        def _(sp):
            for to, of in loads:
                sp.dma_start(to, of).then_inc(loaded, 16)

            def step(g, p):
                if not early(g):
                    sp.wait_ge(s["c_spec"], g - 1)
                sp.dma_start(cx[p][0:S2, :, :], ins["ctx_1024"][bass.ds(GROUP * g, GROUP)].rearrange("b t d -> t b d")).then_inc(cx_loaded[p], 16)
            all_groups(sp, NB, step)
            sp.wait_ge(s["twice"], 1)
            sp.dma_start(k.circulant, twice[:, :]).then_inc(s["stored"], 16)
            sp.wait_ge(s["stored"], 16)

        @block.tensor
        def _(pe):
            def spectra(g, p):
                pe.wait_ge(s["normed"], GROUP * (g + 1))
                pe.wait_ge(s["xf"], g)
                for n in range(GROUP):
                    mm = pe.matmul(x_spec[:, n * P:(n + 1) * P], xn[p][:, n, :], dft[:, :], start=True, stop=True)
                mm.then_inc(s["x_spec"], 1)
                pe.wait_ge(cx_loaded[p], 8 * (g - p) + 16)
                pe.wait_ge(s["cf"], g)
                for n in range(GROUP):
                    mm = pe.matmul(c_spec[:, n * P:(n + 1) * P], cx[p][0:S2, n, :], dft[0:S2, :], start=True, stop=True)
                mm.then_inc(s["c_spec"], 1)

            def project(g, p):
                pe.wait_ge(s["cf"], g + 1)
                pe.wait_ge(s["kf"], g)
                pe.matmul(k_spec[:, :], wk[:, :], cf[p][:, :], start=True, stop=False)
                pe.matmul(k_spec[:, :], bk[:, :], dft_sums[:, 1, :].unsqueeze(1).broadcast_to([1, GROUP, P]),
                          start=False, stop=True).then_inc(s["k_spec"], 1)
                pe.wait_ge(s["xf"], g + 1)
                pe.wait_ge(s["product"], g)
                pe.matmul(q_spec[:, :], wq[:, :], xf[p][:, :], start=True, stop=False)
                pe.matmul(q_spec[:, :], bq[:, :], dft_sums[:, 0, :].unsqueeze(1).broadcast_to([1, GROUP, P]),
                          start=False, stop=True).then_inc(s["q_spec"], 1)

            def powers(g, p):
                pe.wait_ge(s["product"], g + 1)
                for n in range(GROUP):
                    mm = pe.matmul(power[:, bass.ds(GROUP * g + n, 1)], product[p][:, n, :], ones[:, :], start=True, stop=True)
                mm.then_inc(s["power"], 1)

            def step(g, p):
                spectra(g, p)
                if not early(g, 1):
                    powers(g - 1, 1 - p)
                project(g, p)
            pe.wait_ge(loaded, 16 * len(loads))
            pe.wait_ge(s["ones_set"], 1)
            all_groups(pe, NB, step)
            powers(NG - 1, 1)
            pe.wait_ge(s["spectrum"], 1)
            pe.matmul(back[0:NB, 0:P], spectrum[:, :], inverse[:, :], start=True, stop=True).then_inc(s["corr"], 1)
            pe.wait_ge(s["weighted"], 1)
            pe.transpose(power[:, 0:NB], weight[:, :], k.ident[0:NB, 0:NB]).then_inc(s["turned"], 1)
            pe.wait_ge(s["turn_copied"], 1)
            pe.matmul(back[0:NB, 0:2 * P], weight_t[:, :], flip[:, :], start=True, stop=True).then_inc(s["flipped"], 1)

        @block.scalar
        def _(act):
            def step(g, p):
                act.wait_ge(s["x_spec"], g + 1)
                if not early(g):
                    act.wait_ge(s["q_spec"], g - 1)
                act.activation(xf[p][:, :], x_spec[:, :], ACT.Copy).then_inc(s["xf"], 1)
                act.wait_ge(s["k_spec"], g + 1)
                if not early(g):
                    act.wait_ge(s["product"], g - 1)
                act.activation(kf[p][:, :], k_spec[:, :], ACT.Copy).then_inc(s["kf"], 1)
            all_groups(act, NB, step)
            act.wait_ge(s["shifted"], 1)
            act.activation(work[:, :], corr[:, :], ACT.Exp).then_inc(s["exp_done"], 1)

        @block.vector
        def _(dve):
            def multiply(g, p):
                dve.wait_ge(s["q_spec"], g + 1)
                dve.wait_ge(s["kf"], g + 1)
                if not early(g):
                    dve.wait_ge(s["power"], g - 1)
                dve.tensor_tensor(product[p][:, :, :], q_spec[:, :].rearrange("p (n d) -> p n d", d=P),
                                  kf[p][:, :].rearrange("p (n d) -> p n d", d=P), ALU.mult).then_inc(s["product"], 1)

            def step(g, p):
                if not early(g):
                    dve.wait_ge(s["x_spec"], g - 1)
                normalise_group(k, dve, xn[p], k.x_res, g, k.rstd, s["normed"])
                if not early(g, 1):
                    multiply(g - 1, 1 - p)
                dve.wait_ge(s["c_spec"], g + 1)
                if not early(g):
                    dve.wait_ge(s["k_spec"], g - 1)
                dve.tensor_copy(cf[p][:, :], c_spec[:, :]).then_inc(s["cf"], 1)
            dve.memset(ones[:, :], 1.0).then_inc(s["ones_set"], 1)
            all_groups(dve, NB, step)
            multiply(NG - 1, 1)
            dve.wait_ge(s["power"], NG)
            dve.tensor_copy(spectrum[:, :], power[:, 0:NB]).then_inc(s["spectrum"], 1)
            dve.wait_ge(s["corr"], 1)

            def do(op):
                link(dve, op)
            LOW = -3.0e38
            do(dve.tensor_copy(corr[:, :], back[0:NB, 0:P]))
            do(dve.max(best[:, :], corr[:, :]))
            do(dve.match_replace(work[:, :], best[:, :], corr[:, :], LOW))
            do(dve.max(ninth[:, :], work[:, :]))
            do(dve.memset(ninth[:, 1:8], LOW))
            do(dve.match_replace(weight[:, :], ninth[:, :], work[:, :], LOW))
            do(dve.tensor_scalar(weight[:, :], weight[:, :], LOW, None, ALU.is_equal))
            dve.tensor_scalar(corr[:, :], corr[:, :], best[:, 0:1], None, ALU.subtract).then_inc(s["shifted"], 1)
            dve.wait_ge(s["exp_done"], 1)
            do(dve.tensor_tensor(weight[:, :], weight[:, :], work[:, :], ALU.mult))
            do(dve.tensor_reduce(total[:, :], weight[:, :], AX.X, ALU.add))
            do(dve.reciprocal(total[:, :], total[:, :]))
            dve.tensor_scalar(weight[:, :], weight[:, :], total[:, 0:1], None, ALU.mult).then_inc(s["weighted"], 1)
            dve.wait_ge(s["turned"], 1)
            dve.tensor_copy(weight_t[:, :], power[:, 0:NB]).then_inc(s["turn_copied"], 1)
            dve.wait_ge(s["flipped"], 1)
            dve.tensor_copy(twice[:, :], back[0:NB, 0:2 * P]).then_inc(s["twice"], 1)


def build_roll(k):
    nc, ins, NB = k.nc, k.ins, k.NB
    N = GROUP * P
    with ExitStack() as ctx:
        roll = [k.sb(f"v_roll{p}", [P, GROUP, P], F32, ctx) for p in range(2)]
        bo_rows = k.sb("v_bo", [P, D], F32, ctx)
        rolled = [k.psum(f"v_rolled{p}", [P, N], ctx) for p in range(2)]
        loaded = [k.sem(f"v_loaded{p}") for p in range(2)]
        bo_loaded = k.sem("v_bo_loaded")
        s = {n: k.sem("v_" + n) for n in ("rolled", "biased", "added", "stats")}
        block = ctx.enter_context(nc.Block())

        @block.sync
        def _(sp):
            sp.dma_start(bo_rows[:, :], row_broadcast(ins["L1_xattn_bo"], P)).then_inc(bo_loaded, 16)

            def step(g, p):
                if not early(g):
                    sp.wait_ge(s["rolled"], g - 1)
                rows = k.circulant[bass.ds(GROUP * g, GROUP), P - S2 + 1:2 * P - S2 + 1]
                sp.dma_start(roll[p][0:S2, :, :],
                             bass.AP(tensor=rows.tensor, offset=rows.offset,
                                     ap=[[1, S2], [2 * P, GROUP], [1, P]])).then_inc(loaded[p], 16)
            all_groups(sp, NB, step)

        @block.tensor
        def _(pe):
            def step(g, p):
                pe.wait_ge(loaded[p], 8 * (g - p) + 16)
                if not early(g):
                    pe.wait_ge(s["biased"], g - 1)
                for n in range(GROUP):
                    mm = pe.matmul(rolled[p][:, n * D:(n + 1) * D], roll[p][0:S2, n, :], k.vo_res[0:S2, GROUP * g + n, :],
                                   start=True, stop=True)
                mm.then_inc(s["rolled"], 1)
            all_groups(pe, NB, step)

        @block.gpsimd
        def _(pool):
            def step(g, p):
                pool.tensor_tensor(group_of(k.x_res, g), group_of(k.x_res, g),
                                   bo_rows[:, :].unsqueeze(1).broadcast_to([P, GROUP, D]), ALU.add).then_inc(s["added"], 1)
            pool.wait_ge(bo_loaded, 16)
            all_groups(pool, NB, step)

        @block.vector
        def _(dve):
            def step(g, p):
                dve.wait_ge(s["rolled"], g + 1)
                dve.wait_ge(s["added"], g + 1)
                dve.tensor_tensor(group_of(k.x_res, g), rolled[p][:, :].rearrange("p (n d) -> p n d", d=D),
                                  group_of(k.x_res, g), ALU.add).then_inc(s["biased"], 1)
                dve.wait_ge(s["biased"], g + 1)
                for n in range(GROUP):
                    dve.bn_stats(k.stats[:, GROUP * g + n, :], k.x_res[:, GROUP * g + n, :]).then_inc(s["stats"], 1)
            all_groups(dve, NB, step)
            dve.wait_ge(s["stats"], NB)



def build_self_attention(k):
    nc, ins, NB = k.nc, k.ins, k.NB
    SCALE = 1.0 / float(DH) ** 0.5
    W = HQ * P
    CH = 2
    HC = H // 2
    COL = 2 * QUAD
    with ExitStack() as ctx:
        sb = lambda n, s_, dt=F32: k.sb(n, s_, dt, ctx)
        wqkv, wo = sb("s_wqkv", [P, 3 * D]), sb("s_wo", [P, D])
        gain, shift_ = sb("s_gain", [P, 1]), sb("s_shift", [P, 1])
        bq, bk = sb("s_bq", [P, 1]), sb("s_bk", [P, 1])
        bv_rows, bo_rows = sb("s_bv_rows", [P, D]), sb("s_bo_rows", [P, D])
        rstd12 = sb("s_rstd12", [P, NB])
        picks = sb("s_picks", [P, HQ, P], BF16)
        xn = [sb(f"s_xn{p}", [P, D]) for p in range(2)]
        xf = [sb(f"s_xf{p}", [P, D]) for p in range(2)]
        xn_t = [sb(f"s_xn_t{p}", [P, P]) for p in range(2)]
        q_t = [sb(f"s_q_t{p}", [P, P]) for p in range(2)]
        k_t = [sb(f"s_k_t{p}", [P, P]) for p in range(2)]
        q_wide = [sb(f"s_q_wide{p}", [P, HQ, P]) for p in range(2)]
        k_wide = [sb(f"s_k_wide{p}", [P, HQ, P]) for p in range(2)]
        v_heads = [sb(f"s_v_heads{p}", [P, H, COL]) for p in range(2)]
        probs = [sb(f"s_probs{p}", [P, H, P]) for p in range(2)]
        maxima = [sb(f"s_maxima{c}", [P, HC], BF16) for c in range(2)]
        maxima_t = sb("s_maxima_t", [P, P], BF16)
        o_t = sb("s_o_t", [P, 2 * P])
        rsum = sb("s_rsum", [P, H])
        mixed = sb("s_mixed", [P, D])
        mixed_t = sb("s_mixed_t", [P, P])

        scores = k.psum("s_scores", [P, 2, W], ctx)
        scores_t = k.psum("s_scores_t", [P, 2, W], ctx)
        turned = k.psum("s_turned", [P, 512], ctx)
        turned_b = k.psum("s_turned_b", [P, 1024], ctx, BF16)
        qkv = k.psum("s_qkv", [P, 512], ctx)
        out_ps = k.psum("s_out", [P, 512], ctx)
        loaded = k.sem("s_loaded")
        link = Chain(k.sem("s_chain"))
        s = {n: k.sem("s_" + n) for n in
             ("zeroed", "ones_set", "xn_ready", "xf_ready", "turned", "xn_t_ready", "qkv_done", "qk_ready", "v_ready", "wide_ready",
              "scores_done", "max_ready", "max_turned", "max_t_ready", "scores_t_done", "probs_ready", "pv_done",
              "o_ready", "o_turned", "recip", "mixed", "mixed_turned", "mixed_t_ready", "projected", "x2_ready",
              "x2_biased", "stats", "grown")}
        P_ = "L1_ffn_"
        loads = [(wqkv[:, :], ins[P_ + "Wqkv"]), (wo[:, :], ins[P_ + "Wo"]), (gain[:, :], column(ins[P_ + "ln1_g"])),
                 (shift_[:, :], column(ins[P_ + "ln1_b"])), (bq[:, :], column(ins[P_ + "bqkv"][0:D])),
                 (bk[:, :], column(ins[P_ + "bqkv"][D:2 * D])), (bv_rows[:, :], row_broadcast(ins[P_ + "bqkv"][2 * D:3 * D], P)),
                 (bo_rows[:, :], row_broadcast(ins[P_ + "bo"], P))]
        block = ctx.enter_context(nc.Block())

        def each(eng, step, last):
            for b in (0, 1):
                step(b, b)
            with eng.Fori(1, NB // 2 - 1) as i:
                for p in (0, 1):
                    step(2 * i + p, p)
            for b in (NB - 2, NB - 1):
                step(b, b % 2)
            last()

        def is_(b, n):
            return isinstance(b, int) and b == n

        @block.sync
        def _(sp):
            for to, of in loads:
                sp.dma_start(to, of).then_inc(loaded, 16)

        @block.tensor
        def _(pe):
            def turn_x(b, p):
                pe.wait_ge(s["xn_ready"], b + 1)
                pe.wait_ge(s["xn_t_ready"], b)
                if not early(b, 3):
                    pe.wait_ge(s["mixed_t_ready"], b - 2)
                pe.transpose(turned[:, 0:P], xn[p][:, :], k.ident[:, :]).then_inc(s["turned"], 1)

            def project(b, p):
                pe.wait_ge(s["xn_t_ready"], b + 1)
                pe.wait_ge(s["qk_ready"], b)
                pe.wait_ge(s["v_ready"], b)
                pe.matmul(qkv[:, 0:P], wqkv[:, 0:D], xn_t[p][:, :], start=True, stop=True)
                pe.matmul(qkv[:, P:2 * P], wqkv[:, D:2 * D], xn_t[p][:, :], start=True, stop=True)
                pe.matmul(qkv[:, 2 * P:3 * P], xn_t[p][:, :], wqkv[:, 2 * D:3 * D], start=True, stop=True).then_inc(s["qkv_done"], 1)

            def score(b, p, c):
                pe.wait_ge(s["wide_ready"], 2 * b + 2)
                pe.wait_ge(s["max_ready"], CH * b + c)
                for j in range(2):
                    q0 = QUAD * (2 * c + j)
                    mm = pe.matmul(scores[:, j, :], q_t[p][q0:q0 + QUAD, :], k_wide[p][q0:q0 + QUAD, :, :], start=True, stop=True)
                mm.then_inc(s["scores_done"], 1)

            def turn_max(b, c):
                pe.wait_ge(s["max_ready"], CH * b + c + 1)
                pe.wait_ge(s["max_t_ready"], CH * b + c)
                for j in range(2):
                    q0 = QUAD * (2 * c + j)
                    mm = pe.transpose(turned_b[q0:q0 + HQ, 0:P], maxima[c][:, HQ * j:HQ * (j + 1)], k.identb[:, :])
                mm.then_inc(s["max_turned"], 1)

            def score_t(b, p, c):
                pe.wait_ge(s["probs_ready"], CH * b + c)
                for j in range(2):
                    q0 = QUAD * (2 * c + j)
                    pe.matmul(scores_t[:, j, :], k_t[p][q0:q0 + QUAD, :], q_wide[p][q0:q0 + QUAD, :, :],
                              start=True, stop=False, skip_group_check=True)
                pe.wait_ge(s["max_t_ready"], CH * b + c + 1)
                for h in range(HQ):
                    for j in range(2):
                        q0 = QUAD * (2 * c + j)
                        mm = pe.matmul(scores_t[:, j, h * P:(h + 1) * P], picks[q0:q0 + HQ, h, :], maxima_t[q0:q0 + HQ, :],
                                       start=False, stop=(h == HQ - 1), skip_group_check=True)
                mm.then_inc(s["scores_t_done"], 1)

            def weigh(b, p):
                pe.wait_ge(s["probs_ready"], CH * b + CH)
                pe.wait_ge(s["v_ready"], b + 1)
                pe.wait_ge(s["x2_ready"], b)
                for jj in range(2):
                    for h in range(HQ):
                        for half in range(2):
                            head = HQ * (2 * jj + half) + h
                            mm = pe.matmul(out_ps[COL * half:COL * (half + 1), jj * P:(jj + 1) * P], v_heads[p][:, head, :],
                                           probs[p][:, head, :], start=(h == 0), stop=(h == HQ - 1), skip_group_check=True)
                mm.then_inc(s["pv_done"], 1)

            def turn_o(b):
                pe.wait_ge(s["o_ready"], b + 1)
                for jj in range(2):
                    mm = pe.transpose(out_ps[:, (2 + jj) * P:(3 + jj) * P], o_t[:, jj * P:(jj + 1) * P], k.ident[:, :])
                mm.then_inc(s["o_turned"], 1)

            def turn_mixed(b):
                pe.wait_ge(s["mixed"], b + 1)
                if is_(b, NB - 1):
                    pe.wait_ge(s["xn_t_ready"], NB)
                else:
                    pe.wait_ge(s["xn_t_ready"], b + 2)
                pe.transpose(turned[:, P:2 * P], mixed[:, :], k.ident[:, :]).then_inc(s["mixed_turned"], 1)

            def output(b):
                pe.wait_ge(s["mixed_t_ready"], b + 1)
                pe.matmul(out_ps[:, 0:D], mixed_t[:, :], wo[:, :], start=True, stop=True).then_inc(s["projected"], 1)

            def step(b, p):
                last, first = is_(b, NB - 1), is_(b, 0)
                turn_max(b, 0)
                score(b, p, 1)
                if not first:
                    weigh(b - 1, 1 - p)
                score_t(b, p, 0)
                if not last:
                    turn_x(b + 1, 1 - p)
                if not first:
                    turn_o(b - 1)
                turn_max(b, 1)
                if not last:
                    project(b + 1, 1 - p)
                if not first:
                    turn_mixed(b - 1)
                score_t(b, p, 1)
                if not last:
                    score(b + 1, 1 - p, 0)
                if not first:
                    output(b - 1)

            def last():
                weigh(NB - 1, 1)
                turn_o(NB - 1)
                turn_mixed(NB - 1)
                output(NB - 1)
            pe.wait_ge(loaded, 16 * len(loads))
            pe.wait_ge(link.sem, 1 + P // QUAD)
            turn_x(0, 0)
            project(0, 0)
            score(0, 0, 0)
            each(pe, step, last)

        @block.scalar
        def _(act):
            def affine(b, p):
                act.wait_ge(s["turned"], b + 1)
                if not early(b):
                    act.wait_ge(s["qkv_done"], b - 1)
                act.activation(xn_t[p][:, :], turned[:, 0:P], ACT.Identity, bias=shift_[:, 0:1],
                               scale=gain[:, 0:1]).then_inc(s["xn_t_ready"], 1)

            def bias_qk(b, p):
                act.wait_ge(s["qkv_done"], b + 1)
                if not early(b):
                    act.wait_ge(s["scores_done"], CH * (b - 1))
                    act.wait_ge(s["scores_t_done"], CH * (b - 1))
                    act.wait_ge(s["wide_ready"], 2 * (b - 1))
                act.activation(q_t[p][:, :], qkv[:, 0:P], ACT.Identity, bias=bq[:, 0:1])
                act.activation(k_t[p][:, :], qkv[:, P:2 * P], ACT.Identity, bias=bk[:, 0:1]).then_inc(s["qk_ready"], 1)

            def copy_max(b, c):
                act.wait_ge(s["max_turned"], CH * b + c + 1)
                if not is_(b, 0):
                    act.wait_ge(s["scores_t_done"], CH * (b - 1) + c + 1)
                for j in range(2):
                    q0 = QUAD * (2 * c + j)
                    op = act.activation(maxima_t[q0:q0 + HQ, :], turned_b[q0:q0 + HQ, 0:P], ACT.Copy)
                op.then_inc(s["max_t_ready"], 1)

            def exponent(b, p, c):
                act.wait_ge(s["scores_t_done"], CH * b + c + 1)
                if c == 0 and not early(b):
                    act.wait_ge(s["pv_done"], b - 1)
                act.activation(probs[p][:, HC * c:HC * (c + 1), :].rearrange("p h q -> p (h q)"),
                               scores_t[:, :, :].rearrange("p j q -> p (j q)"), ACT.Exp, scale=SCALE).then_inc(s["probs_ready"], 1)

            def copy_mixed(b):
                act.wait_ge(s["mixed_turned"], b + 1)
                act.wait_ge(s["projected"], b)
                act.activation(mixed_t[:, :], turned[:, P:2 * P], ACT.Copy).then_inc(s["mixed_t_ready"], 1)

            def step(b, p):
                last, first = is_(b, NB - 1), is_(b, 0)
                copy_max(b, 0)
                exponent(b, p, 0)
                if not last:
                    affine(b + 1, 1 - p)
                copy_max(b, 1)
                if not last:
                    bias_qk(b + 1, 1 - p)
                if not first:
                    copy_mixed(b - 1)
                exponent(b, p, 1)
            act.wait_ge(loaded, 16 * len(loads))
            affine(0, 0)
            bias_qk(0, 0)
            each(act, step, lambda: copy_mixed(NB - 1))

        @block.gpsimd
        def _(pool):
            def spread(b, p):
                pool.wait_ge(s["qk_ready"], b + 1)
                if not early(b):
                    pool.wait_ge(s["scores_done"], CH * (b - 1))
                    pool.wait_ge(s["scores_t_done"], CH * (b - 1))
                for to, of in ((k_wide, k_t), (q_wide, q_t)):
                    pool.tensor_tensor(to[p][:, :, :], of[p][:, :].unsqueeze(1).broadcast_to([P, HQ, P]),
                                       k.headmask[:, :].unsqueeze(2).broadcast_to([P, HQ, P]), ALU.mult).then_inc(s["wide_ready"], 1)

            def grow(b):
                pool.wait_ge(s["x2_ready"], b + 1)
                pool.tensor_tensor(k.x_res[:, b, :], k.x_res[:, b, :], k.tmp_res[:, b, :], ALU.add).then_inc(s["grown"], 1)

            def step(b, p):
                if not is_(b, NB - 1):
                    spread(b + 1, 1 - p)
                if not is_(b, 0):
                    grow(b - 1)
            for p in range(2):
                pool.memset(v_heads[p][:, :, :], 0.0).then_inc(s["zeroed"], 1)
            pool.wait_ge(s["zeroed"], 2)
            for p in range(2):
                t = v_heads[p]
                first = t[:, :, :]
                pool.memset(bass.AP(tensor=first.tensor, offset=first.offset + QUAD,
                                    ap=[list(first.ap[0]), [HQ * COL, H // HQ], [COL + 1, HQ]]), 1.0).then_inc(s["ones_set"], 1)
            pool.wait_ge(s["ones_set"], 2)
            spread(0, 0)
            each(pool, step, lambda: grow(NB - 1))
            pool.wait_ge(s["grown"], NB)

        @block.vector
        def _(dve):
            def normalise(b, p):
                if not early(b):
                    dve.wait_ge(s["turned"], b - 1)
                mean = k.mean[:, bass.ds(b, 1)]
                dve.tensor_scalar(xn[p][:, :], k.x_res[:, b, :], mean, rstd12[:, bass.ds(b, 1)], ALU.subtract, ALU.mult).then_inc(s["xn_ready"], 1)

            def bias_v(b, p):
                dve.wait_ge(s["qkv_done"], b + 1)
                dve.wait_ge(s["qk_ready"], b + 1)
                if not early(b):
                    dve.wait_ge(s["pv_done"], b - 1)
                first = v_heads[p][:, :, :]
                blocks = bass.AP(tensor=first.tensor, offset=first.offset,
                                 ap=[list(first.ap[0]), [HQ * COL, H // HQ], [COL + DH, HQ], [1, DH]])
                dve.tensor_tensor(blocks, qkv[:, 2 * P:3 * P].rearrange("p (j h d) -> p j h d", h=HQ, d=DH),
                                  bv_rows[:, :].rearrange("p (j h d) -> p j h d", h=HQ, d=DH), ALU.add).then_inc(s["v_ready"], 1)

            def maximum(b, c):
                dve.wait_ge(s["scores_done"], CH * b + c + 1)
                if not is_(b, 0):
                    dve.wait_ge(s["max_turned"], CH * (b - 1) + c + 1)
                dve.tensor_reduce(maxima[c][:, :], scores[:, :, :].rearrange("p j (h q) -> p (j h) q", q=P),
                                  AX.X, ALU.max).then_inc(s["max_ready"], 1)

            def copy_o(b):
                dve.wait_ge(s["pv_done"], b + 1)
                dve.wait_ge(s["o_turned"], b)
                dve.tensor_copy(o_t[:, :], out_ps[:, 0:2 * P]).then_inc(s["o_ready"], 1)

            def mix(b):
                dve.wait_ge(s["o_turned"], b + 1)
                both = out_ps[:, 2 * P:4 * P].rearrange("p (j c) -> p j c", c=COL)
                dve.reciprocal(rsum[:, :].rearrange("p (j h) -> p j h", h=HQ), both[:, :, QUAD:QUAD + HQ]).then_inc(s["recip"], 1)
                dve.wait_ge(s["recip"], b + 1)
                dve.wait_ge(s["mixed_turned"], b)
                dve.tensor_tensor(mixed[:, :].rearrange("p (j h d) -> p j h d", h=HQ, d=DH),
                                  both[:, :, 0:QUAD].rearrange("p j (h d) -> p j h d", d=DH),
                                  rsum[:, :].rearrange("p (j h) -> p j h", h=HQ).unsqueeze(3).broadcast_to([P, H // HQ, HQ, DH]),
                                  ALU.mult).then_inc(s["mixed"], 1)

            def close(b, p):
                dve.tensor_scalar(xf[p][:, :], k.x_res[:, b, :], k.mean[:, bass.ds(b, 1)], k.rstd[:, bass.ds(b, 1)],
                                  ALU.subtract, ALU.mult).then_inc(s["xf_ready"], 1)
                dve.wait_ge(s["xf_ready"], b + 1)
                dve.tensor_tensor(xf[p][:, :], xf[p][:, :], bo_rows[:, :], ALU.add).then_inc(s["x2_biased"], 1)
                dve.wait_ge(s["projected"], b + 1)
                dve.wait_ge(s["x2_biased"], b + 1)
                dve.tensor_tensor(k.tmp_res[:, b, :], out_ps[:, 0:D], xf[p][:, :], ALU.add).then_inc(s["x2_ready"], 1)
                dve.wait_ge(s["x2_ready"], b + 1)
                dve.bn_stats(k.stats[:, b, :], k.tmp_res[:, b, :]).then_inc(s["stats"], 1)

            def step(b, p):
                last, first = is_(b, NB - 1), is_(b, 0)
                maximum(b, 1)
                if not last:
                    normalise(b + 1, 1 - p)
                if not first:
                    copy_o(b - 1)
                    mix(b - 1)
                if not last:
                    bias_v(b + 1, 1 - p)
                    maximum(b + 1, 0)
                if not first:
                    close(b - 1, 1 - p)

            def last():
                copy_o(NB - 1)
                mix(NB - 1)
                close(NB - 1, 1)
                dve.wait_ge(s["stats"], NB)
            link(dve, dve.tensor_tensor(rstd12[:, :], k.rstd[:, :], k.rstd2[:, :], ALU.mult))
            for q0 in range(0, P, QUAD):
                link(dve, dve.tensor_scalar(picks[q0:q0 + HQ, :, :], k.ident[q0:q0 + HQ, q0:q0 + HQ].unsqueeze(2).broadcast_to([HQ, HQ, P]),
                                            -1.0, None, ALU.mult))
            dve.wait_ge(loaded, 16 * len(loads))
            dve.wait_ge(s["ones_set"], 2)
            normalise(0, 0)
            bias_v(0, 0)
            maximum(0, 0)
            each(dve, step, last)


def build_expert_layer_1(k):
    nc, ins, NB = k.nc, k.ins, k.NB
    m = Experts("m1_", 512, 4, 1, ACT.Gelu)
    N_ = "L1_ffn_"
    with ExitStack() as ctx:
        sb = lambda n, s_, dt=F32: k.sb("m1_" + n, s_, dt, ctx)
        columns = sb("columns", [P, E + 2])
        gain, shift_, gain_rows, shift_rows = sb("gain", [P, 1]), sb("shift", [P, 1]), sb("gain_rows", [P, D]), sb("shift_rows", [P, D])
        coef_bias = sb("coef_bias", [P, E + 2])
        up, down = sb("up", [P, E, 512]), sb("down", [P, E, 4, D])
        up_bias, down_bias = sb("up_bias", [P, E, 512]), sb("down_bias", [P, E, D])
        loaded = k.sem("m1_loaded")
        zeroed = k.sem("m1_zeroed")
        loads = [(columns[:, 0:E], ins[N_ + "gate_w"]), (columns[:, E:E + 2], ins[N_ + "coef_w"]),
                 (gain[:, :], column(ins[N_ + "ln2_g"])), (shift_[:, :], column(ins[N_ + "ln2_b"])),
                 (gain_rows[:, :], row_broadcast(ins[N_ + "ln2_g"], P)), (shift_rows[:, :], row_broadcast(ins[N_ + "ln2_b"], P)),
                 (coef_bias[:, E:E + 2], row_broadcast(ins[N_ + "coef_b"], P)),
                 (up[:, :, :], ins[N_ + "W1"].rearrange("e h i -> h e i")),
                 (down[:, :, :, :], ins[N_ + "W2"].rearrange("e (c p) h -> p e c h", p=P)),
                 (up_bias[:, :, :], row_broadcast(ins[N_ + "b1"], P)), (down_bias[:, :, :], row_broadcast(ins[N_ + "b2"], P))]
        with nc.Block() as block:
            @block.sync
            def _(sp):
                for to, of in loads:
                    sp.dma_start(to, of).then_inc(loaded, 16)
                sp.wait_ge(loaded, 16 * len(loads))

            @block.vector
            def _(dve):
                dve.memset(coef_bias[:, 0:E], 0.0).then_inc(zeroed, 1)
                dve.wait_ge(zeroed, 1)
        build_rstd(k, "m1_rstd")
        build_prepare(k, m, columns[:, :], (gain, shift_, gain_rows, shift_rows), coef_bias)
        build_route(k, m, None)
        build_dispatch(k, m)
        build_experts(k, m, up, down, up_bias, down_bias)
    with ExitStack() as ctx:
        sb = lambda n, s_, dt=F32: k.sb("m1s_" + n, s_, dt, ctx)
        s_up, s_down = sb("s_up", [P, 512]), sb("s_down", [P, 4, D])
        s_up_bias, s_down_rows = sb("s_up_bias", [P, 4]), sb("s_down_rows", [P, D])
        loaded = k.sem("m1s_loaded")
        copied = k.sem("m1s_copied")
        loads = [(s_up[:, :], ins[N_ + "rW1"]), (s_down[:, :, :], ins[N_ + "rW2"].rearrange("(c p) h -> p c h", p=P)),
                 (s_up_bias[:, :], ins[N_ + "rb1"].rearrange("(c p) -> p c", p=P)), (s_down_rows[:, :], row_broadcast(ins[N_ + "rb2"], P))]
        with nc.Block() as block:
            @block.sync
            def _(sp):
                for to, of in loads:
                    sp.dma_start(to, of, allow_slow_non_contiguous=True).then_inc(loaded, 16)
                sp.wait_ge(loaded, 16 * len(loads))

            @block.vector
            def _(dve):
                dve.tensor_copy(k.coef_shared[:, :], k.coef[:, :, 1]).then_inc(copied, 1)
                dve.wait_ge(copied, 1)
        build_combine(k, m, s_up, s_down, (s_up_bias, s_down_rows), stats=False)


def build_store(k):
    nc, NB = k.nc, k.NB
    stored = k.sem("out_stored")
    with nc.Block() as block:
        @block.sync
        def _(sp):
            for n in range(4):
                q = NB // 4
                sp.dma_start(k.out[n * q:(n + 1) * q].rearrange("b t d -> t b d"), k.x_res[:, n * q:(n + 1) * q, :]).then_inc(stored, 16)
            sp.wait_ge(stored, 64)


def build(nc, ins, out):
    with ExitStack() as ctx:
        k = Kernel(nc, ctx, ins, out)
        build_load(k)
        build_context_attention(k)
        build_rstd(k, "o0")
        build_context_output(k)
        build_rstd(k, "o1")
        build_context_residual(k)
        build_expert_layer_0(k)
        k.retire_semaphores()
        build_rstd(k, "c0")
        build_correlation(k)
        build_roll(k)
        build_rstd(k, "s0", composed=True)
        build_self_attention(k)
        build_expert_layer_1(k)
        build_store(k)
        k.sem_ctx.close()


def kernel(**inputs):
    import numpy as np
    import concourse.bacc as bacc
    from concourse import mybir as mb
    from concourse.bass_utils import run_bass_kernel_spmd as run

    nc = bacc.Bacc("TRN2", target_bir_lowering=False, num_devices=1)
    arrays = {"in_" + n: np.ascontiguousarray(a) for n, a in inputs.items()}
    rows = np.arange(P)
    arrays["in_c_ident"] = np.eye(P, dtype=np.float32)
    arrays["in_c_headmask"] = ((rows[:, None] % QUAD) // DH == np.arange(HQ)).astype(np.float32)
    NB = inputs["x"].shape[0]
    tables = np.concatenate([rows[:, None] < rows, np.tile(np.arange(E), (P, 1)), np.tile(np.arange(2 * NB + E), (P, 1))], 1)
    arrays["in_c_tables"] = tables.astype(np.float32)
    turns = 2 * np.pi * (np.outer(rows, np.concatenate([np.arange(65), np.arange(1, 64)])) % P) / P
    dft = np.where(np.arange(P) < 65, np.cos(turns), np.sin(turns))
    times = np.where((np.arange(P) == 0) | (np.arange(P) == 64), 1.0, 2.0)
    arrays["in_c_dft"] = dft.astype(np.float32)
    arrays["in_c_inverse"] = (dft.T * times[:, None] / P / P).astype(np.float32)
    arrays["in_c_dft_sums"] = np.stack([dft.sum(0), dft[:S2].sum(0)]).astype(np.float32)
    arrays["in_c_flip"] = (rows[:, None] == (-np.arange(2 * P)) % P).astype(np.float32)
    ins = {n[3:]: nc.dram_tensor(n, a.shape, mb.dt.from_np(a.dtype), kind="ExternalInput").ap()
           for n, a in arrays.items()}
    shape = inputs["x"].shape
    out = nc.dram_tensor("out", shape, mb.dt.float32, kind="ExternalOutput").ap()
    build(nc, ins, out)
    r = run(nc, [arrays], core_ids=[0])
    return r.results[0]["out"]
```

```python
from contextlib import ExitStack

import concourse.bass as bass
from concourse import mybir

F32 = mybir.dt.float32
BF16 = mybir.dt.bfloat16
I32 = mybir.dt.int32
ALU = mybir.AluOpType
ACT = mybir.ActivationFunctionType
AX = mybir.AxisListType

P = 128
D = 128
S2 = 120
H = 16
DH = D // H
QUAD = 32
HQ = QUAD // DH
EPS = 1e-5
E = 8
GROUP = 4


class Kernel:

    def __init__(self, nc, ctx, ins, out):
        self.nc, self.ctx, self.ins, self.out = nc, ctx, ins, out
        self.NB = ins["x"].shape[0]
        self.sems, self.sem_ctx = [], ExitStack()

    def sb(self, name, shape, dt=F32, ctx=None):
        return (ctx or self.ctx).enter_context(self.nc.sbuf_tensor(name, shape, dt))

    def psum(self, name, shape, ctx, dt=F32):
        return ctx.enter_context(self.nc.psum_tensor(name, shape, dt))

    def sem(self, name):
        self.sems.append(self.sem_ctx.enter_context(self.nc.semaphore(name)))
        return self.sems[-1]

    def pool_dma_sem(self, name):
        return self.ctx.enter_context(self.nc.semaphore(name))

    def retire_semaphores(self):
        with self.nc.Block() as block:
            @block.gpsimd
            def _(pool):
                for sem in self.sems:
                    pool.sem_clear(sem)
        self.sem_ctx.close()
        self.sems, self.sem_ctx = [], ExitStack()


def row_broadcast(vector, rows):
    return vector.partition_broadcast(rows)


def column(vector):
    return vector.rearrange("(d one) -> d one", one=1)


class Chain:

    def __init__(self, sem):
        self.sem, self.n = sem, 0

    def __call__(self, eng, op):
        self.n += 1
        op.then_inc(self.sem, 1)
        eng.wait_ge(self.sem, self.n)


def combine_stats(k, dve, link):
    mean_e, m2_e, mean_o, m2_o = (k.stats[:, :, i] for i in (1, 2, 4, 5))
    link(dve, dve.tensor_tensor(k.mean[:, :], mean_e, mean_o, ALU.subtract))
    link(dve, dve.scalar_tensor_tensor(out=k.var[:, :], in0=k.mean[:, :], scalar=0.25, in1=k.mean[:, :],
                                       op0=ALU.mult, op1=ALU.mult))
    link(dve, dve.tensor_tensor(k.mean[:, :], m2_e, m2_o, ALU.add))
    link(dve, dve.scalar_tensor_tensor(out=k.var[:, :], in0=k.mean[:, :], scalar=1.0 / D, in1=k.var[:, :],
                                       op0=ALU.mult, op1=ALU.add))
    link(dve, dve.tensor_tensor(k.mean[:, :], mean_e, mean_o, ALU.add))
    link(dve, dve.tensor_scalar(k.mean[:, :], k.mean[:, :], 0.5, None, ALU.mult))



def build_load(k):
    nc, ins, NB = k.nc, k.ins, k.NB
    k.x_res = k.sb("x_res", [P, NB, D])
    k.tmp_res = k.sb("tmp_res", [P, NB, D])
    k.vo_res = k.sb("vo_res", [P, NB, D])
    k.ident = k.sb("ident", [P, P])
    k.identb = k.sb("identb", [P, P], BF16)
    k.headmask = k.sb("headmask", [P, HQ])
    k.stats = k.sb("stats", [P, NB, 6])
    k.mean = k.sb("mean", [P, NB])
    k.var = k.sb("var", [P, NB])
    k.rstd = k.sb("rstd", [P, NB])
    k.rstd2 = k.sb("rstd2", [P, NB])
    k.logits = k.sb("logits", [P, NB, E + 2])
    k.coef = k.sb("coef", [P, NB, 2])
    k.coef_shared = k.sb("coef_shared", [P, NB])
    k.choice_w = [k.sb(f"choice_w{j}", [P, NB]) for j in range(2)]
    k.place = [k.sb(f"place{j}", [P, NB], I32) for j in range(2)]
    k.slot_expert = k.sb("slot_expert", [P, 2 * NB + E], I32)
    k.tables = k.sb("tables", [P, P + E + 2 * NB + E])
    k.zeros = k.sb("zeros", [P, 8 * D])
    k.slots = nc.dram_tensor("slots", [(2 * NB + E) * P, D], F32).ap()
    k.results = nc.dram_tensor("results", [(2 * NB + E) * P, D], F32).ap()
    k.xf_dram = nc.dram_tensor("xf_dram", [NB * P, D], F32).ap()
    k.circulant = nc.dram_tensor("circulant", [NB, 2 * P], F32).ap()
    k.w = {}
    for name in ("L0_xattn_Wq", "L0_xattn_Wk1", "L0_xattn_Wk2", "L0_xattn_Wv1", "L0_xattn_Wv2", "L0_xattn_Wo",
                 "L1_xattn_Wv", "L1_xattn_Wo"):
        k.w[name] = k.sb(name, [P, D])
    cols = ("L0_xattn_bq", "L0_xattn_bk1", "L0_xattn_bk2", "L0_xattn_bo", "L0_xattn_g0", "L0_xattn_beta0", "L1_xattn_bv")
    for name in cols:
        k.w[name] = k.sb(name, [P, 1])
    k.v_bias = k.sb("v_bias", [P, 2 * D])
    k.g1_rows = k.sb("g1_rows", [P, D])
    k.beta1_rows = k.sb("beta1_rows", [P, D])
    k.wvo = k.sb("wvo", [P, D])
    k.bvo = k.sb("bvo", [P, D])
    wv_t = k.sb("wv_t", [P, D])
    bv_wide = k.sb("bv_wide", [P, P])

    x_loaded = [k.sem(f"x_loaded{n}") for n in range(4)]
    weights_loaded = k.sem("weights_loaded")
    stats_done = k.sem("stats_done")
    chain = Chain(k.sem("load_chain"))
    ident_cast = k.sem("ident_cast")
    eps_added = k.sem("eps_added")
    root_done = k.sem("root_done")
    zeros_set = k.sem("zeros_set")
    slots_cleared = k.pool_dma_sem("slots_cleared")
    wv_turned = k.sem("wv_turned")
    wv_copied = k.sem("wv_copied")
    wvo_product = k.sem("wvo_product")
    PARTS = 4
    per = NB // PARTS
    loads = [(k.ident, ins["c_ident"]), (k.headmask, ins["c_headmask"]), (k.tables, ins["c_tables"])]
    loads += [(k.w[n], ins[n]) for n in k.w if n not in cols]
    loads += [(k.w[n], column(ins[n])) for n in cols]
    loads += [(k.v_bias[:, 0:D], row_broadcast(ins["L0_xattn_bv1"], P)),
              (k.v_bias[:, D:2 * D], row_broadcast(ins["L0_xattn_bv2"], P)),
              (k.g1_rows[:, :], row_broadcast(ins["L0_xattn_g1"], P)),
              (k.beta1_rows[:, :], row_broadcast(ins["L0_xattn_beta1"], P))]

    with ExitStack() as ctx:
        turn = k.psum("load_turn", [P, 512], ctx)
        prod = k.psum("load_prod", [P, 512], ctx)
        block = ctx.enter_context(nc.Block())

        @block.sync
        def _(sp):
            for n in range(PARTS):
                sp.dma_start(k.x_res[:, n * per:(n + 1) * per, :],
                             ins["x"][n * per:(n + 1) * per].rearrange("b t d -> t b d")).then_inc(x_loaded[n], 16)

        @block.scalar
        def _(act):
            for to, of in loads:
                act.dma_start(to if isinstance(to, bass.AP) else to[:, :], of).then_inc(weights_loaded, 16)
            act.wait_ge(eps_added, 1)
            act.activation(k.rstd[:, :], k.rstd[:, :], ACT.Sqrt).then_inc(root_done, 1)

        @block.gpsimd
        def _(pool):
            pool.memset(k.zeros[:, :], 0.0).then_inc(zeros_set, 1)
            pool.wait_ge(zeros_set, 1)
            for n in range((2 * NB + E) // 8):
                pool.dma_start(k.slots[n * 8 * P:(n + 1) * 8 * P, :].rearrange("(p r) d -> p (r d)", p=P),
                               k.zeros[:, :]).then_inc(slots_cleared, 16)
            pool.wait_ge(slots_cleared, 16 * ((2 * NB + E) // 8))

        @block.tensor
        def _(pe):
            pe.wait_ge(weights_loaded, 16 * len(loads))
            pe.transpose(turn[:, 0:D], k.w["L1_xattn_Wv"][:, :], k.ident[:, :]).then_inc(wv_turned, 1)
            pe.wait_ge(wv_copied, 2)
            pe.matmul(prod[:, 0:D], wv_t[:, :], k.w["L1_xattn_Wo"][:, :], start=True, stop=True)
            pe.matmul(prod[:, D:2 * D], bv_wide[:, :], k.w["L1_xattn_Wo"][:, :],
                      start=True, stop=True).then_inc(wvo_product, 1)

        @block.vector
        def _(dve):
            dve.wait_ge(weights_loaded, 16 * len(loads))
            dve.tensor_copy(k.identb[:, :], k.ident[:, :]).then_inc(ident_cast, 1)
            dve.tensor_copy(bv_wide[:, :], k.w["L1_xattn_bv"][:, 0:1].broadcast_to([P, P])).then_inc(wv_copied, 1)
            dve.wait_ge(wv_turned, 1)
            dve.tensor_copy(wv_t[:, :], turn[:, 0:D]).then_inc(wv_copied, 1)
            for n in range(PARTS):
                dve.wait_ge(x_loaded[n], 16)
                with dve.Fori(n * per, (n + 1) * per) as b:
                    dve.bn_stats(k.stats[:, b, :], k.x_res[:, b, :]).then_inc(stats_done, 1)
            dve.wait_ge(stats_done, NB)
            dve.wait_ge(wvo_product, 1)
            dve.tensor_copy(k.wvo[:, :], prod[:, 0:D]).then_inc(ident_cast, 1)
            dve.tensor_copy(k.bvo[:, :], prod[:, D:2 * D]).then_inc(ident_cast, 1)
            combine_stats(k, dve, chain)
            dve.tensor_scalar(k.rstd[:, :], k.var[:, :], EPS, None, ALU.add).then_inc(eps_added, 1)
            dve.wait_ge(root_done, 1)
            dve.reciprocal(k.rstd[:, :], k.rstd[:, :]).then_inc(ident_cast, 1)
            dve.wait_ge(ident_cast, 4)



def build_context_attention(k):
    nc, ins, NB, w = k.nc, k.ins, k.NB, k.w
    SCALE = 1.0 / float(D) ** 0.5
    W = HQ * P
    CH = 4
    HC = H // 2
    with ExitStack() as ctx:
        sb = lambda n, s, dt=F32: k.sb(n, s, dt, ctx)
        ctx_in = [sb(f"ctx_in{p}", [P, D]) for p in range(2)]
        xn = [sb(f"xn{p}", [P, D]) for p in range(2)]
        xc_t = [sb(f"xc_t{p}", [P, 2 * P]) for p in range(2)]
        q_t = [sb(f"q_t{p}", [P, P]) for p in range(2)]
        k_t = [sb(f"k_t{p}", [P, 2, S2]) for p in range(2)]
        q_wide = [sb(f"q_wide{p}", [P, HQ, P]) for p in range(2)]
        v_sb = [sb(f"v_sb{p}", [P, 2 * D]) for p in range(2)]
        v_heads = [sb(f"v_heads{p}", [P, 2, H, QUAD]) for p in range(2)]
        probs = [sb(f"probs{p}", [P, 2, H, P]) for p in range(2)]
        maxima = sb("maxima", [P, 2, HC], BF16)
        sums = sb("sums", [P, 2, HC])
        rsums = sb("rsums", [P, 4, HC])
        q_keep = [sb(f"q_keep{p}", [P, P]) for p in range(2)]
        o_t = sb("o_t", [P, P])

        scores = [k.psum(f"scores{i}", [P, 2, W], ctx) for i in range(2)]
        turned = k.psum("turned", [P, 512], ctx)
        qk = k.psum("qk", [P, 512], ctx)
        vv = k.psum("vv", [P, 512], ctx)
        pv = k.psum("pv", [P, 512], ctx)

        s = {n: k.sem("a_" + n) for n in
             ("zeroed", "xn_ready", "turned", "xc_ready", "qk_done", "q_ready", "wide_ready",
              "v_done", "v_ready", "vo_ready", "scores_done", "max_ready", "shifted", "probs_ready", "sums_ready",
              "rsums_ready", "v_heads_ready", "pv_part", "pv_done", "q_kept", "o_ready", "o_turned", "out_ready", "stats")}
        ctx_loaded = [k.sem(f"a_ctx_loaded{p}") for p in range(2)]
        block = ctx.enter_context(nc.Block())

        def all_sequences(eng, step, last):
            for b in (0, 1):
                step(b, b % 2)
            with eng.Fori(1, NB // 2 - 1) as i:
                for p in (0, 1):
                    step(2 * i + p, p)
            for b in (NB - 2, NB - 1):
                step(b, b % 2)
            last()

        def is_(b, n):
            return isinstance(b, int) and b == n

        @block.sync
        def _(sp):
            def step(b, p):
                if not (isinstance(b, int) and b < 2):
                    sp.wait_ge(s["turned"], b - 1)
                sp.dma_start(ctx_in[p][0:S2, :], ins["ctx_1024"][b]).then_inc(ctx_loaded[p], 16)
            all_sequences(sp, step, lambda: None)

        @block.tensor
        def _(pe):
            def turn_inputs(b, p):
                pe.wait_ge(s["xn_ready"], b + 1)
                pe.wait_ge(ctx_loaded[p], 8 * (b - p) + 16)
                pe.wait_ge(s["xc_ready"], b)
                pe.transpose(turned[:, 0:P], xn[p][:, :], k.ident[:, :])
                pe.transpose(turned[:, P:P + S2], ctx_in[p][0:S2, :], k.ident[0:S2, 0:S2]).then_inc(s["turned"], 1)

            def project(b, p):
                pe.wait_ge(s["xc_ready"], b + 1)
                pe.wait_ge(s["q_ready"], b)
                c_t = xc_t[p][:, P:P + S2]
                pe.matmul(qk[:, 0:P], w["L0_xattn_Wq"][:, :], xc_t[p][:, 0:P], start=True, stop=True)
                pe.matmul(qk[:, P:P + S2], w["L0_xattn_Wk1"][:, :], c_t, start=True, stop=True)
                pe.matmul(qk[:, 2 * P:2 * P + S2], w["L0_xattn_Wk2"][:, :], c_t,
                          start=True, stop=True).then_inc(s["qk_done"], 1)

            def values(b, p):
                pe.wait_ge(s["q_ready"], b + 1)
                pe.wait_ge(s["vo_ready"], b)
                if not early(b, 3):
                    pe.wait_ge(s["out_ready"], b - 2)
                pe.matmul(vv[0:S2, 0:D], k_t[p][:, 0, :], w["L0_xattn_Wv1"][:, :], start=True, stop=True)
                pe.matmul(vv[0:S2, D:2 * D], k_t[p][:, 1, :], w["L0_xattn_Wv2"][:, :], start=True, stop=True)
                pe.matmul(vv[0:S2, 2 * D:3 * D], xc_t[p][:, P:P + S2], k.wvo[:, :],
                          start=True, stop=True).then_inc(s["v_done"], 1)

            def score(b, p, c):
                if c == 0:
                    pe.wait_ge(s["wide_ready"], b + 1)
                if not (is_(b, 0) and c < 2):
                    pe.wait_ge(s["probs_ready"], CH * b + c - 1)
                for j in range(2):
                    q0 = QUAD * (2 * (c % 2) + j)
                    mm = pe.matmul(scores[c % 2][0:S2, j, :], k_t[p][q0:q0 + QUAD, c // 2, :],
                                   q_wide[p][q0:q0 + QUAD, :, :], start=True, stop=True)
                mm.then_inc(s["scores_done"], 1)

            def shift(b, c):
                pe.wait_ge(s["max_ready"], CH * b + c + 1)
                for j in range(2):
                    mm = pe.matmul(scores[c % 2][0:S2, j, :], k.identb[0:S2, 0:S2],
                                   maxima[0:S2, c % 2, HQ * j:HQ * (j + 1)].unsqueeze(2).broadcast_to([S2, HQ, P]),
                                   start=False, stop=True, skip_group_check=True)
                mm.then_inc(s["shifted"], 1)

            def weigh(b, p, part):
                if part == 0:
                    pe.wait_ge(s["o_ready"], b)
                pe.wait_ge(s["v_heads_ready"], CH * b + part // 2 * 2 + 2)
                for n in (2 * part, 2 * part + 1):
                    for j in range(H // HQ):
                        h = HQ * j + n % HQ
                        mm = pe.matmul(pv[QUAD * j:QUAD * (j + 1), 0:P], v_heads[p][0:S2, n // HQ, h, :],
                                       probs[p][0:S2, n // HQ, h, :], start=(n == 0), stop=(n == 2 * HQ - 1))
                mm.then_inc(s["pv_done"] if part == 3 else s["pv_part"], 1)

            def turn_output(b):
                pe.wait_ge(s["o_ready"], b + 1)
                if is_(b, NB - 2) or is_(b, NB - 1):
                    pe.wait_ge(s["vo_ready"], NB)
                else:
                    pe.wait_ge(s["vo_ready"], b + 3)
                pe.wait_ge(s["out_ready"], b)
                pe.transpose(vv[:, 3 * D:4 * D], o_t[:, :], k.ident[:, :]).then_inc(s["o_turned"], 1)

            def step(b, p):
                last, first = is_(b, NB - 1), is_(b, 0)
                score(b, p, 1)
                shift(b, 0)
                if not last:
                    turn_inputs(b + 1, 1 - p)
                if not (first or is_(b, 1)):
                    turn_output(b - 2)
                if not first:
                    weigh(b - 1, 1 - p, 0)
                score(b, p, 2)
                shift(b, 1)
                if not last:
                    project(b + 1, 1 - p)
                if not first:
                    weigh(b - 1, 1 - p, 1)
                score(b, p, 3)
                shift(b, 2)
                if not last:
                    values(b + 1, 1 - p)
                if not first:
                    weigh(b - 1, 1 - p, 2)
                if not last:
                    score(b + 1, 1 - p, 0)
                shift(b, 3)
                if not first:
                    weigh(b - 1, 1 - p, 3)

            def last():
                turn_output(NB - 2)
                for part in range(4):
                    weigh(NB - 1, 1, part)
                turn_output(NB - 1)

            turn_inputs(0, 0)
            project(0, 0)
            values(0, 0)
            score(0, 0, 0)
            all_sequences(pe, step, last)

        @block.scalar
        def _(act):
            def copy_turned(b, p):
                pe_done = s["turned"]
                act.wait_ge(pe_done, b + 1)
                if not (isinstance(b, int) and b < 2):
                    act.wait_ge(s["v_done"], b - 1)
                act.activation(xc_t[p][:, 0:P], turned[:, 0:P], ACT.Copy)
                act.activation(xc_t[p][:, P:P + S2], turned[:, P + S2 - 1:P - 1:-1], ACT.Copy).then_inc(s["xc_ready"], 1)

            def bias_qk(b, p):
                act.wait_ge(s["qk_done"], b + 1)
                if not (isinstance(b, int) and b < 2):
                    act.wait_ge(s["scores_done"], CH * b - CH)
                    act.wait_ge(s["v_done"], b - 1)
                    act.wait_ge(s["wide_ready"], b - 1)
                    act.wait_ge(s["q_kept"], b - 1)
                act.activation(q_t[p][:, :], qk[:, 0:P], ACT.Identity, bias=w["L0_xattn_bq"][:, 0:1])
                act.activation(k_t[p][:, 0, :], qk[:, P:P + S2], ACT.Identity, bias=w["L0_xattn_bk1"][:, 0:1])
                act.activation(k_t[p][:, 1, :], qk[:, 2 * P:2 * P + S2], ACT.Identity,
                               bias=w["L0_xattn_bk2"][:, 0:1]).then_inc(s["q_ready"], 1)

            def exponent(b, p, c):
                act.wait_ge(s["shifted"], CH * b + c + 1)
                if c == 0 and not (isinstance(b, int) and b < 2):
                    act.wait_ge(s["pv_done"], b - 1)
                h0 = HC * (c % 2)
                act.activation(probs[p][0:S2, c // 2, h0:h0 + HC, :].rearrange("p h q -> p (h q)"),
                               scores[c % 2][0:S2, :, :].rearrange("p j q -> p (j q)"),
                               ACT.Exp, scale=SCALE).then_inc(s["probs_ready"], 1)

            def step(b, p):
                last = is_(b, NB - 1)
                exponent(b, p, 0)
                if not last:
                    copy_turned(b + 1, 1 - p)
                exponent(b, p, 1)
                if not last:
                    bias_qk(b + 1, 1 - p)
                exponent(b, p, 2)
                exponent(b, p, 3)

            copy_turned(0, 0)
            bias_qk(0, 0)
            all_sequences(act, step, lambda: None)

        @block.gpsimd
        def _(pool):
            def spread(b, p):
                pool.wait_ge(s["q_ready"], b + 1)
                if not (isinstance(b, int) and b < 2):
                    pool.wait_ge(s["scores_done"], CH * b - CH)
                pool.tensor_tensor(q_wide[p][:, :, :], q_t[p][:, :].unsqueeze(1).broadcast_to([P, HQ, P]),
                                   k.headmask[:, :].unsqueeze(2).broadcast_to([P, HQ, P]),
                                   ALU.mult).then_inc(s["wide_ready"], 1)

            def scale_values(b, p, c):
                pool.wait_ge(s["rsums_ready"], CH * b + c + 1)
                if c == 0:
                    pool.wait_ge(s["v_ready"], b + 1)
                    if not (isinstance(b, int) and b < 2):
                        pool.wait_ge(s["pv_done"], b - 1)
                for j in range(2):
                    jj = 2 * (c % 2) + j
                    own = v_heads[p][0:S2, c // 2, HQ * jj:HQ * (jj + 1), :].rearrange("p h c -> p (h c)")
                    own = own.rearrange("p (h c) -> p h c", c=QUAD)
                    v0 = D * (c // 2) + QUAD * jj
                    t = v_heads[p][0:S2, c // 2, HQ * jj:HQ * (jj + 1), :]
                    diag = bass.AP(tensor=t.tensor, offset=t.offset,
                                   ap=[list(t.ap[0]), [QUAD + DH, HQ], [1, DH]])
                    op = pool.tensor_tensor(
                        diag, v_sb[p][0:S2, v0:v0 + QUAD].rearrange("p (h d) -> p h d", d=DH),
                        rsums[0:S2, c, HQ * j:HQ * (j + 1)].unsqueeze(2).broadcast_to([S2, HQ, DH]), ALU.mult)
                op.then_inc(s["v_heads_ready"], 1)

            def keep_queries(b, p):
                if not early(b):
                    pool.wait_ge(s["o_ready"], b - 1)
                pool.tensor_tensor(q_keep[p][:, :], q_t[p][:, :], k.zeros[:, 0:P], ALU.add).then_inc(s["q_kept"], 1)

            def step(b, p):
                last = is_(b, NB - 1)
                if not is_(b, 0):
                    scale_values(b - 1, 1 - p, 3)
                    keep_queries(b - 1, 1 - p)
                scale_values(b, p, 0)
                if not last:
                    spread(b + 1, 1 - p)
                scale_values(b, p, 1)
                scale_values(b, p, 2)

            for p in range(2):
                pool.memset(v_heads[p][:, :, :, :], 0.0).then_inc(s["zeroed"], 1)
            pool.wait_ge(s["zeroed"], 2)
            spread(0, 0)
            def last():
                scale_values(NB - 1, 1, 3)
                keep_queries(NB - 1, 1)
            all_sequences(pool, step, last)

        @block.vector
        def _(dve):
            def normalise(b, p):
                if not (isinstance(b, int) and b < 2):
                    dve.wait_ge(s["turned"], b - 1)
                dve.tensor_scalar(xn[p][:, :], k.x_res[:, b, :], k.mean[:, bass.ds(b, 1)], k.rstd[:, bass.ds(b, 1)],
                                  ALU.subtract, ALU.mult).then_inc(s["xn_ready"], 1)

            def bias_values(b, p):
                dve.wait_ge(s["v_done"], b + 1)
                if not (isinstance(b, int) and b < 2):
                    dve.wait_ge(s["v_heads_ready"], CH * b - CH)
                dve.tensor_tensor(v_sb[p][0:S2, :], vv[0:S2, 0:2 * D], k.v_bias[0:S2, :],
                                  ALU.add).then_inc(s["v_ready"], 1)
                dve.tensor_tensor(k.vo_res[0:S2, b, :], vv[0:S2, 2 * D:3 * D], k.bvo[0:S2, :],
                                  ALU.add).then_inc(s["vo_ready"], 1)

            def maximum(b, c):
                dve.wait_ge(s["scores_done"], CH * b + c + 1)
                if not (is_(b, 0) and c < 2):
                    dve.wait_ge(s["shifted"], CH * b + c - 1)
                dve.tensor_reduce(maxima[0:S2, c % 2, :],
                                  scores[c % 2][0:S2, :, :].rearrange("p j (h q) -> p (j h) q", q=P),
                                  AX.X, ALU.max, negate=True).then_inc(s["max_ready"], 1)

            def total(b, p, c):
                dve.wait_ge(s["probs_ready"], CH * b + c + 1)
                h0 = HC * (c % 2)
                dve.tensor_reduce(sums[0:S2, c % 2, :], probs[p][0:S2, c // 2, h0:h0 + HC, :],
                                  AX.X, ALU.add).then_inc(s["sums_ready"], 1)
                dve.wait_ge(s["sums_ready"], CH * b + c + 1)
                if not is_(b, 0):
                    dve.wait_ge(s["v_heads_ready"], CH * b + c - CH + 1)
                dve.reciprocal(rsums[0:S2, c, :], sums[0:S2, c % 2, :]).then_inc(s["rsums_ready"], 1)

            def add_queries(b, p):
                dve.wait_ge(s["pv_done"], b + 1)
                dve.wait_ge(s["o_turned"], b)
                dve.wait_ge(s["q_kept"], b + 1)
                dve.tensor_tensor(o_t[:, :], pv[:, 0:P], q_keep[p][:, :], ALU.add).then_inc(s["o_ready"], 1)

            def keep_output(b):
                dve.wait_ge(s["o_turned"], b + 1)
                dve.bn_stats(k.stats[:, b, :], vv[:, 3 * D:4 * D]).then_inc(s["stats"], 1)
                dve.tensor_copy(k.tmp_res[:, b, :], vv[:, 3 * D:4 * D]).then_inc(s["out_ready"], 1)

            def step(b, p):
                first, last = is_(b, 0), is_(b, NB - 1)
                old = not (first or is_(b, 1))
                maximum(b, 0)
                if not first:
                    total(b - 1, 1 - p, 3)
                if old:
                    add_queries(b - 2, p)
                if not last:
                    normalise(b + 1, 1 - p)
                maximum(b, 1)
                total(b, p, 0)
                if old:
                    keep_output(b - 2)
                maximum(b, 2)
                total(b, p, 1)
                maximum(b, 3)
                total(b, p, 2)
                if not last:
                    bias_values(b + 1, 1 - p)

            def last():
                total(NB - 1, 1, 3)
                add_queries(NB - 2, 0)
                keep_output(NB - 2)
                add_queries(NB - 1, 1)
                keep_output(NB - 1)
                dve.wait_ge(s["out_ready"], NB)
                dve.wait_ge(s["stats"], NB)

            normalise(0, 0)
            bias_values(0, 0)
            all_sequences(dve, step, last)



def build_rstd(k, name, composed=False):
    nc = k.nc
    link = Chain(k.sem(name + "_chain"))
    eps_added = k.sem(name + "_eps_added")
    root_done = k.sem(name + "_root_done")
    with nc.Block() as block:
        @block.scalar
        def _(act):
            act.wait_ge(eps_added, 1)
            act.activation(k.rstd[:, :], k.rstd[:, :], ACT.Sqrt).then_inc(root_done, 1)
            if composed:
                act.wait_ge(eps_added, 2)
                act.activation(k.rstd2[:, :], k.rstd2[:, :], ACT.Sqrt).then_inc(root_done, 1)

        @block.vector
        def _(dve):
            combine_stats(k, dve, link)
            dve.tensor_scalar(k.rstd[:, :], k.var[:, :], EPS, None, ALU.add).then_inc(eps_added, 1)
            dve.wait_ge(root_done, 1)
            link(dve, dve.reciprocal(k.rstd[:, :], k.rstd[:, :]))
            if composed:
                link(dve, dve.tensor_tensor(k.rstd2[:, :], k.rstd[:, :], k.rstd[:, :], ALU.mult))
                link(dve, dve.tensor_tensor(k.rstd2[:, :], k.rstd2[:, :], k.var[:, :], ALU.mult))
                dve.tensor_scalar(k.rstd2[:, :], k.rstd2[:, :], EPS, None, ALU.add).then_inc(eps_added, 1)
                dve.wait_ge(root_done, 2)
                link(dve, dve.reciprocal(k.rstd2[:, :], k.rstd2[:, :]))


def normalise_group(k, dve, to, of, g, rstd, done):
    for n in range(GROUP):
        b = GROUP * g + n
        dve.tensor_scalar(to[:, n, :], of[:, b, :], k.mean[:, bass.ds(b, 1)], rstd[:, bass.ds(b, 1)],
                          ALU.subtract, ALU.mult).then_inc(done, 1)


def group_of(tensor, g):
    return tensor[:, bass.ds(GROUP * g, GROUP), :]


def all_groups(eng, NB, step):
    NG = NB // GROUP
    for g in (0, 1):
        step(g, g)
    if NG > 2:
        with eng.Fori(1, NG // 2) as i:
            for p in (0, 1):
                step(2 * i + p, p)


def early(g, n=2):
    return isinstance(g, int) and g < n



def build_context_output(k):
    nc, NB, w = k.nc, k.NB, k.w
    N = GROUP * D
    with ExitStack() as ctx:
        sb = lambda n, s, dt=F32: k.sb(n, s, dt, ctx)
        normed = [sb(f"normed{p}", [P, GROUP, D]) for p in range(2)]
        o_t = [sb(f"out_t{p}", [P, N]) for p in range(2)]
        r_t = [sb(f"relu_t{p}", [P, N]) for p in range(2)]
        turned = [k.psum(f"bo_turned{p}", [P, N], ctx) for p in range(2)]
        product = [k.psum(f"bo_product{p}", [P, N], ctx) for p in range(2)]
        back = [k.psum(f"bo_back{p}", [P, N], ctx) for p in range(2)]
        s = {n: k.sem("o_" + n) for n in ("normed", "turned", "affine", "product", "relu", "sum", "back", "kept", "stats")}
        block = ctx.enter_context(nc.Block())

        @block.tensor
        def _(pe):
            def step(g, p):
                pe.wait_ge(s["normed"], GROUP * (g + 1))
                if not early(g):
                    pe.wait_ge(s["affine"], g - 1)
                for n in range(GROUP):
                    mm = pe.transpose(turned[p][:, n * P:(n + 1) * P], normed[p][:, n, :], k.ident[:, :])
                mm.then_inc(s["turned"], 1)
                pe.wait_ge(s["affine"], g + 1)
                if not early(g):
                    pe.wait_ge(s["relu"], g - 1)
                pe.matmul(product[p][:, :], w["L0_xattn_Wo"][:, :], o_t[p][:, :], start=True, stop=True).then_inc(s["product"], 1)
                pe.wait_ge(s["sum"], g + 1)
                if not early(g):
                    pe.wait_ge(s["kept"], g - 1)
                    pe.wait_ge(s["stats"], GROUP * (g - 1))
                for n in range(GROUP):
                    mm = pe.transpose(back[p][:, n * P:(n + 1) * P], r_t[p][:, n * P:(n + 1) * P], k.ident[:, :])
                mm.then_inc(s["back"], 1)
            all_groups(pe, NB, step)

        @block.scalar
        def _(act):
            def step(g, p):
                act.wait_ge(s["turned"], g + 1)
                if not early(g):
                    act.wait_ge(s["sum"], g - 1)
                act.activation(o_t[p][:, :], turned[p][:, :], ACT.Identity, bias=w["L0_xattn_beta0"][:, 0:1],
                               scale=w["L0_xattn_g0"][:, 0:1]).then_inc(s["affine"], 1)
                act.wait_ge(s["product"], g + 1)
                if not early(g):
                    act.wait_ge(s["back"], g - 1)
                act.activation(r_t[p][:, :], product[p][:, :], ACT.Relu,
                               bias=w["L0_xattn_bo"][:, 0:1]).then_inc(s["relu"], 1)
            all_groups(act, NB, step)

        @block.gpsimd
        def _(pool):
            def step(g, p):
                pool.wait_ge(s["relu"], g + 1)
                pool.tensor_tensor(r_t[p][:, :], r_t[p][:, :], o_t[p][:, :], ALU.add).then_inc(s["sum"], 1)
            all_groups(pool, NB, step)

        @block.vector
        def _(dve):
            def step(g, p):
                if not early(g):
                    dve.wait_ge(s["turned"], g - 1)
                normalise_group(k, dve, normed[p], k.tmp_res, g, k.rstd, s["normed"])
                if not early(g, 1):
                    finish(g - 1, 1 - p)

            def finish(g, p):
                dve.wait_ge(s["back"], g + 1)
                for n in range(GROUP):
                    dve.bn_stats(k.stats[:, GROUP * g + n, :], back[p][:, n * P:(n + 1) * P]).then_inc(s["stats"], 1)
                dve.tensor_copy(group_of(k.tmp_res, g), back[p][:, :].rearrange("p (n d) -> p n d", d=D)).then_inc(s["kept"], 1)
            all_groups(dve, NB, step)
            finish(NB // GROUP - 1, 1)
            dve.wait_ge(s["kept"], NB // GROUP)


def build_context_residual(k):
    nc, NB = k.nc, k.NB
    with ExitStack() as ctx:
        normed = [k.sb(f"r_normed{p}", [P, GROUP, D], F32, ctx) for p in range(2)]
        s = {n: k.sem("r_" + n) for n in ("normed", "scaled", "moved", "added", "stats")}
        block = ctx.enter_context(nc.Block())

        def rows(t):
            return t[:, :].unsqueeze(1).broadcast_to([P, GROUP, D])

        @block.gpsimd
        def _(pool):
            def step(g, p):
                pool.wait_ge(s["normed"], GROUP * (g + 1))
                pool.tensor_tensor(normed[p][:, :, :], normed[p][:, :, :], rows(k.g1_rows), ALU.mult).then_inc(s["scaled"], 1)
                pool.wait_ge(s["scaled"], g + 1)
                pool.tensor_tensor(normed[p][:, :, :], normed[p][:, :, :], rows(k.beta1_rows), ALU.add).then_inc(s["moved"], 1)
            all_groups(pool, NB, step)

        @block.vector
        def _(dve):
            def step(g, p):
                if not early(g):
                    dve.wait_ge(s["added"], g - 1)
                normalise_group(k, dve, normed[p], k.tmp_res, g, k.rstd, s["normed"])
                if not early(g, 1):
                    finish(g - 1, 1 - p)

            def finish(g, p):
                dve.wait_ge(s["moved"], g + 1)
                dve.tensor_tensor(group_of(k.x_res, g), group_of(k.x_res, g), normed[p][:, :, :], ALU.add).then_inc(s["added"], 1)
                dve.wait_ge(s["added"], g + 1)
                for n in range(GROUP):
                    dve.bn_stats(k.stats[:, GROUP * g + n, :], k.x_res[:, GROUP * g + n, :]).then_inc(s["stats"], 1)
            all_groups(dve, NB, step)
            finish(NB // GROUP - 1, 1)
            dve.wait_ge(s["stats"], NB)



class Experts:

    def __init__(self, name, inner, down_chunks, top, act):
        self.name, self.inner, self.chunks, self.top, self.act = name, inner, down_chunks, top, act

    def tiles(self, NB):
        return self.top * NB + E


def build_prepare(k, m, columns, affine, gate_bias):
    nc, NB = k.nc, k.NB
    n_cols = columns.shape[1]
    source = k.tmp_res if affine else k.x_res
    with ExitStack() as ctx:
        sb = lambda n, s_, dt=F32: k.sb(m.name + n, s_, dt, ctx)
        xn = [sb(f"pn{p}", [P, D]) for p in range(2)]
        xa = [sb(f"pa{p}", [P, D]) for p in range(2)] if affine else xn
        x_t = [sb(f"pt{p}", [P, P]) for p in range(2)]
        turned = [k.psum(f"{m.name}pturn{p}", [P, 512], ctx) for p in range(2)]
        logit = [k.psum(f"{m.name}plogit{p}", [P, 512], ctx) for p in range(2)]
        s = {n: k.sem(m.name + "p_" + n) for n in ("normed", "scaled", "moved", "turned", "copied", "logits", "kept", "logits_kept", "bias")}
        stored = [k.sem(f"{m.name}p_stored{p}") for p in range(2)]
        block = ctx.enter_context(nc.Block())

        def each(eng, step):
            for b in (0, 1):
                step(b, b)
            with eng.Fori(1, NB // 2) as i:
                for p in (0, 1):
                    step(2 * i + p, p)

        @block.sync
        def _(sp):
            def step(b, p):
                sp.wait_ge(s["moved"] if affine else s["normed"], b + 1)
                sp.dma_start(k.xf_dram[bass.ds(b * P, P), :], xa[p][:, :]).then_inc(stored[p], 16)
            each(sp, step)
            for p in range(2):
                sp.wait_ge(stored[p], 8 * NB)

        @block.tensor
        def _(pe):
            def logits(b, p):
                pe.wait_ge(s["copied"], b + 1)
                if not early(b):
                    pe.wait_ge(s["logits_kept"], b - 1)
                pe.matmul(logit[p][:, 0:n_cols], x_t[p][:, :], columns, start=True, stop=True).then_inc(s["logits"], 1)

            def step(b, p):
                pe.wait_ge(s["normed"], b + 1)
                if not early(b):
                    pe.wait_ge(s["copied"], b - 1)
                pe.transpose(turned[p][:, 0:P], xn[p][:, :], k.ident[:, :]).then_inc(s["turned"], 1)
                if not early(b, 1):
                    logits(b - 1, 1 - p)
            each(pe, step)
            logits(NB - 1, 1)

        @block.scalar
        def _(act):
            def step(b, p):
                act.wait_ge(s["turned"], b + 1)
                if not early(b):
                    act.wait_ge(s["logits"], b - 1)
                    act.wait_ge(s["kept"], b - 1)
                if affine:
                    act.activation(x_t[p][:, :], turned[p][:, 0:P], ACT.Identity, bias=affine[1][:, 0:1],
                                   scale=affine[0][:, 0:1]).then_inc(s["copied"], 1)
                else:
                    act.activation(x_t[p][:, :], turned[p][:, 0:P], ACT.Copy).then_inc(s["copied"], 1)
            each(act, step)

        if affine:
            @block.gpsimd
            def _(pool):
                def step(b, p):
                    pool.wait_ge(s["normed"], b + 1)
                    if not early(b):
                        pool.wait_ge(stored[p], 8 * (b - p))
                    pool.tensor_tensor(xa[p][:, :], xn[p][:, :], affine[2][:, :], ALU.mult).then_inc(s["scaled"], 1)
                    pool.wait_ge(s["scaled"], b + 1)
                    pool.tensor_tensor(xa[p][:, :], xa[p][:, :], affine[3][:, :], ALU.add).then_inc(s["moved"], 1)
                each(pool, step)

        @block.vector
        def _(dve):
            def keep(b, p):
                dve.wait_ge(s["copied"], b + 1)
                dve.tensor_scalar(k.tmp_res[:, b, :], x_t[p][:, :], 1.0, None, ALU.mult).then_inc(s["kept"], 1)
                dve.wait_ge(s["logits"], b + 1)
                if gate_bias is None:
                    dve.tensor_scalar(k.logits[:, b, 0:n_cols], logit[p][:, 0:n_cols], k.rstd2[:, bass.ds(b, 1)], None,
                                      ALU.mult).then_inc(s["logits_kept"], 1)
                else:
                    dve.tensor_tensor(k.logits[:, b, 0:n_cols], logit[p][:, 0:n_cols], gate_bias[:, :],
                                      ALU.add).then_inc(s["logits_kept"], 1)

            def step(b, p):
                if not early(b):
                    dve.wait_ge(s["turned"], b - 1)
                    if affine:
                        dve.wait_ge(s["scaled"], b - 1)
                    else:
                        dve.wait_ge(stored[p], 8 * (b - p))
                dve.tensor_scalar(xn[p][:, :], source[:, b, :], k.mean[:, bass.ds(b, 1)], k.rstd[:, bass.ds(b, 1)],
                                  ALU.subtract, ALU.mult).then_inc(s["normed"], 1)
                if not early(b, 1):
                    keep(b - 1, 1 - p)
            each(dve, step)
            keep(NB - 1, 1)
            dve.wait_ge(s["logits_kept"], NB)


def build_route(k, m, logit_bias):
    nc, NB, NT = k.nc, k.NB, m.tiles(k.NB)
    with ExitStack() as ctx:
        sb = lambda n, s_, dt=F32: k.sb(m.name + n, s_, dt, ctx)
        t0, t1, probs, counts = (sb(n, [P, NB, E]) for n in ("rt0", "rt1", "rprobs", "rcounts"))
        chosen = [sb(f"rchosen{j}", [P, NB, E]) for j in range(2)]
        both = sb("rboth", [P, NB, E], BF16)
        triangle = sb("rtriangle", [P, P], BF16)
        ones = sb("rones", [P, P], BF16)
        v = [sb(f"rv{i}", [P, NB]) for i in range(3)]
        small = [sb(f"rs{i}", [P, E]) for i in range(4)]
        small_i = sb("rsi", [P, E], I32)
        tile_cmp = sb("rcmp", [P, NT, E])
        tile_of = sb("rtile", [P, NT])
        ranks = k.psum(m.name + "ranks", [P, NB * E], ctx)
        totals = k.psum(m.name + "totals", [P, NB * E], ctx)
        link = Chain(k.sem(m.name + "r_chain"))
        ready, exp_done, counted = (k.sem(m.name + "r_" + n) for n in ("shifted", "exp_done", "counted"))
        onehots = k.sem(m.name + "r_onehots")
        block = ctx.enter_context(nc.Block())

        def over_e(t):
            return t[:, :].unsqueeze(2).broadcast_to([P, NB, E])

        def over_b(t):
            return t[:, 0:E].unsqueeze(1).broadcast_to([P, NB, E])

        n_exp = 2 if m.top == 1 else 1

        @block.scalar
        def _(act):
            act.wait_ge(ready, 1)
            act.activation(probs[:, :, :], t0[:, :, :], ACT.Exp).then_inc(exp_done, 1)
            if n_exp == 2:
                act.wait_ge(ready, 2)
                act.activation(k.coef[:, :, :], k.coef[:, :, :], ACT.Exp).then_inc(exp_done, 1)

        @block.tensor
        def _(pe):
            pe.wait_ge(onehots, 1)
            pe.matmul(ranks[:, :], triangle[:, :], both[:, :, :], start=True, stop=True)
            pe.matmul(totals[:, :], ones[:, :], both[:, :, :], start=True, stop=True).then_inc(counted, 1)

        @block.vector
        def _(dve):
            def do(op):
                link(dve, op)

            TT, TS = dve.tensor_tensor, dve.tensor_scalar
            do(dve.tensor_copy(triangle[:, :], k.tables[:, 0:P]))
            do(dve.memset(ones[:, :], 1.0))
            L = k.logits[:, :, 0:E]
            if logit_bias is not None:
                do(TT(L, L, over_b(logit_bias), ALU.add))
            do(dve.tensor_reduce(v[0][:, :], L, AX.X, ALU.max))
            TT(t0[:, :, :], L, over_e(v[0]), ALU.subtract).then_inc(ready, 1)
            if n_exp == 2:
                C = k.logits[:, :, E:E + 2]
                do(dve.tensor_reduce(v[1][:, :], C, AX.X, ALU.max))
                TT(k.coef[:, :, :], C, v[1][:, :].unsqueeze(2).broadcast_to([P, NB, 2]), ALU.subtract).then_inc(ready, 1)
                dve.wait_ge(exp_done, 2)
                do(dve.tensor_reduce(v[1][:, :], k.coef[:, :, :], AX.X, ALU.add))
                do(dve.reciprocal(v[1][:, :], v[1][:, :]))
                do(TT(k.coef[:, :, :], k.coef[:, :, :], v[1][:, :].unsqueeze(2).broadcast_to([P, NB, 2]), ALU.mult))
            dve.wait_ge(exp_done, 1)
            do(dve.tensor_reduce(v[0][:, :], probs[:, :, :], AX.X, ALU.add))
            do(dve.reciprocal(v[0][:, :], v[0][:, :]))
            do(TT(probs[:, :, :], probs[:, :, :], over_e(v[0]), ALU.mult))
            for j in range(m.top):
                best = k.choice_w[j]
                do(dve.tensor_reduce(best[:, :], probs[:, :, :], AX.X, ALU.max))
                do(TT(t0[:, :, :], probs[:, :, :], over_e(best), ALU.is_equal))
                do(dve.scalar_tensor_tensor(out=t1[:, :, :], in0=t0[:, :, :], scalar=-float(E),
                                            in1=over_b(k.tables[:, P:P + E]), op0=ALU.mult, op1=ALU.add))
                do(dve.tensor_reduce(v[1][:, :], t1[:, :, :], AX.X, ALU.min))
                do(TS(v[1][:, :], v[1][:, :], float(E), None, ALU.add))
                do(TT(chosen[j][:, :, :], over_b(k.tables[:, P:P + E]), over_e(v[1]), ALU.is_equal))
                if j + 1 < m.top:
                    do(dve.scalar_tensor_tensor(out=probs[:, :, :], in0=chosen[j][:, :, :], scalar=-2.0,
                                                in1=probs[:, :, :], op0=ALU.mult, op1=ALU.add))
            if m.top == 2:
                TT(both[:, :, :], chosen[0][:, :, :], chosen[1][:, :, :], ALU.add).then_inc(onehots, 1)
                do(TT(v[0][:, :], k.choice_w[0][:, :], k.choice_w[1][:, :], ALU.add))
                do(TS(v[0][:, :], v[0][:, :], EPS, None, ALU.add))
                do(dve.reciprocal(v[0][:, :], v[0][:, :]))
                for j in range(2):
                    do(TT(k.choice_w[j][:, :], k.choice_w[j][:, :], v[0][:, :], ALU.mult))
            else:
                dve.tensor_copy(both[:, :, :], chosen[0][:, :, :]).then_inc(onehots, 1)
                do(TT(k.choice_w[0][:, :], k.choice_w[0][:, :], k.coef[:, :, 0], ALU.mult))
            dve.wait_ge(counted, 1)
            do(dve.tensor_copy(counts[:, :, :], totals[:, :].rearrange("p (b e) -> p b e", e=E)))
            a, b_, shift = counts, t0, 1
            while shift < NB:
                dve.tensor_copy(b_[:, 0:shift, :], a[:, 0:shift, :]).then_inc(link.sem, 1)
                link.n += 1
                do(TT(b_[:, shift:NB, :], a[:, shift:NB, :], a[:, 0:NB - shift, :], ALU.add))
                a, b_ = b_, (t1 if b_ is t0 else t0)
                shift *= 2
            do(TS(small_i[:, :], a[:, NB - 1, :], float(P - 1), None, ALU.add))
            do(TS(small_i[:, :], small_i[:, :], 7, None, ALU.arith_shift_right))
            do(dve.tensor_copy(small[0][:, :], small_i[:, :]))
            ea, eb, shift = small[0], small[1], 1
            while shift < E:
                dve.tensor_copy(eb[:, 0:shift], ea[:, 0:shift]).then_inc(link.sem, 1)
                link.n += 1
                do(TT(eb[:, shift:E], ea[:, shift:E], ea[:, 0:E - shift], ALU.add))
                ea, eb = eb, (small[2] if eb is small[1] else small[1])
                shift *= 2
            do(TT(small[3][:, :], ea[:, :], small[0][:, :], ALU.subtract))
            do(TS(small[3][:, :], small[3][:, :], float(P), None, ALU.mult))
            rest = t1 if a is t0 else t0
            do(TT(rest[:, :, :], a[:, :, :], counts[:, :, :], ALU.subtract))
            do(TT(rest[:, :, :], rest[:, :, :], over_b(small[3]), ALU.add))
            do(TT(rest[:, :, :], ranks[:, :].rearrange("p (b e) -> p b e", e=E), rest[:, :, :], ALU.add))
            for j in range(m.top):
                do(TT(chosen[j][:, :, :], chosen[j][:, :, :], rest[:, :, :], ALU.mult))
                do(dve.tensor_reduce(v[1][:, :], chosen[j][:, :, :], AX.X, ALU.add))
                do(dve.tensor_copy(k.place[j][:, :], v[1][:, :]))
            tile_no = k.tables[:, P + E:P + E + NT]
            do(TT(tile_cmp[:, :, :], tile_no.unsqueeze(2).broadcast_to([P, NT, E]),
                  ea[:, :].unsqueeze(1).broadcast_to([P, NT, E]), ALU.is_ge))
            do(dve.tensor_reduce(tile_of[:, :], tile_cmp[:, :, :], AX.X, ALU.add))
            do(TS(k.slot_expert[:, 0:NT], tile_of[:, :], float(E - 1), None, ALU.min))


def build_dispatch(k, m):
    nc, NB = k.nc, k.NB
    RING = 4
    with ExitStack() as ctx:
        rows = [k.sb(f"{m.name}drow{r}", [P, D], F32, ctx) for r in range(RING)]
        places = [[k.sb(f"{m.name}dplace{r}_{j}", [P, 1], I32, ctx) for j in range(m.top)] for r in range(RING)]
        loaded = [k.sem(f"{m.name}d_loaded{r}") for r in range(RING)]
        sent = [k.pool_dma_sem(f"{m.name}d_sent{r}") for r in range(RING)]
        placed = k.sem(m.name + "d_placed")
        go = k.sem(m.name + "d_go")
        block = ctx.enter_context(nc.Block())
        per = 16 * m.top

        @block.sync
        def _(sp):
            for r in range(RING):
                sp.dma_start(rows[r][:, :], k.xf_dram[r * P:(r + 1) * P, :]).then_inc(loaded[r], 16)
            with sp.Fori(1, NB // RING) as i:
                for r in range(RING):
                    sp.wait_ge(sent[r], per * i)
                    sp.dma_start(rows[r][:, :], k.xf_dram[bass.ds((RING * i + r) * P, P), :]).then_inc(loaded[r], 16)

        @block.gpsimd
        def _(pool):
            def step(i, r):
                b = RING * i + r
                if not early(i, 1):
                    pool.wait_ge(sent[r], per * i)
                for j in range(m.top):
                    pool.tensor_copy(places[r][j][:, :], k.place[j][:, bass.ds(b, 1)]).then_inc(placed, 1)
                pool.wait_ge(placed, m.top * (b + 1))
                pool.wait_ge(loaded[r], 16 * i + 16)
                pool.sem_inc(go, 1)
                for j in range(m.top):
                    pool.indirect_dma_start(k.slots, bass.IndirectOffsetOnAxis(places[r][j][:, 0:1], 0),
                                            rows[r][:, :], None).then_inc(sent[r], 16)
            for r in range(RING):
                step(0, r)
            with pool.Fori(1, NB // RING) as i:
                for r in range(RING):
                    step(i, r)
            for r in range(RING):
                pool.wait_ge(sent[r], per * (NB // RING))


def build_experts(k, m, up, down, up_bias=None, down_bias=None):
    nc, NT = k.nc, m.tiles(k.NB)
    C = m.chunks
    R, QD = 8, 4
    NR = NT // R
    with ExitStack() as ctx:
        sb = lambda n, s_, dt=F32: k.sb(m.name + n, s_, dt, ctx)
        x_in = [sb(f"ex{q}", [P, QD, D]) for q in range(2)]
        x_t = [sb(f"ext{p}", [P, P]) for p in range(2)]
        g = [sb(f"eg{p}", [P, 512]) for p in range(2)]
        h = [sb(f"eh{p}", [P, C * P]) for p in range(2)]
        h_t = [sb(f"eht{p}", [P, C * P]) for p in range(2)]
        y = [sb(f"ey{q}", [P, QD, D]) for q in range(2)]
        turned = [k.psum(f"{m.name}eturn{p}", [P, 512], ctx) for p in range(2)]
        hidden = [k.psum(f"{m.name}ehid{p}", [P, 512], ctx) for p in range(2)]
        h_turned = [k.psum(f"{m.name}ehturn{p}", [P, 512], ctx) for p in range(2)]
        result = [k.psum(f"{m.name}eres{p}", [P, 512], ctx) for p in range(2)]
        loaded = [k.sem(f"{m.name}e_loaded{q}") for q in range(2)]
        stored = [k.pool_dma_sem(f"{m.name}e_stored{q}") for q in range(2)]
        s = {n: k.sem(m.name + "e_" + n) for n in
             ("turned", "x_ready", "hidden", "biased", "gated", "h_ready", "h_turned", "h_t_ready", "result", "y_ready")}
        block = ctx.enter_context(nc.Block())

        def rows_of(t, quad):
            return t[bass.ds(quad * QD * P, QD * P), :].rearrange("(n p) d -> p n d", p=P)

        def each(eng, step):
            for r in range(R):
                step(0, r)
            with eng.Fori(1, NR - 1) as n:
                for r in range(R):
                    step(n, r)
            for r in range(R):
                step(NR - 1, r)

        def off(n, r, d):
            n, r = n + (r + d) // R, (r + d) % R
            return None if isinstance(n, int) and not 0 <= n < NR else (n, r)

        def slot(at):
            return R * at[0] + at[1]

        def back2(at):
            return off(*at, -2) is not None

        @block.sync
        def _(sp):
            def load(n, q):
                if not early(n, 1):
                    sp.wait_ge(s["turned"], R * (n - 1) + QD * (q + 1))
                sp.dma_start(x_in[q][:, :, :], rows_of(k.slots, 2 * n + q)).then_inc(loaded[q], 16)

            for q in range(2):
                load(0, q)
            with sp.Fori(1, NR) as n:
                for q in range(2):
                    load(n, q)

        @block.gpsimd
        def _(pool):
            def store(n, q):
                pool.wait_ge(s["y_ready"], R * n + QD * (q + 1))
                pool.dma_start(rows_of(k.results, 2 * n + q), y[q][:, :, :]).then_inc(stored[q], 16)

            with pool.Fori(0, NR) as n:
                for q in range(2):
                    store(n, q)
            for q in range(2):
                pool.wait_ge(stored[q], 16 * NR)

        @block.tensor
        def _(pe):
            def expert(at):
                return pe.value_load(k.slot_expert[0:1, bass.ds(slot(at), 1)], min_val=0, max_val=E - 1)

            def turn_x(at):
                n, r = at
                if r % QD == 0:
                    pe.wait_ge(loaded[r // QD], 16 * n + 16)
                if back2(at):
                    pe.wait_ge(s["x_ready"], slot(at) - 1)
                pe.transpose(turned[r % 2][:, 0:P], x_in[r // QD][:, r % QD, :], k.ident[:, :]).then_inc(s["turned"], 1)

            def go_up(at):
                p = at[1] % 2
                e = expert(at)
                pe.wait_ge(s["x_ready"], slot(at) + 1)
                if back2(at):
                    pe.wait_ge(s["biased" if up_bias is not None else "h_ready"], slot(at) - 1)
                pe.matmul(hidden[p][:, :], x_t[p][:, :], up[:, e, :], start=True, stop=True).then_inc(s["hidden"], 1)

            def turn_h(at):
                p = at[1] % 2
                pe.wait_ge(s["h_ready"], slot(at) + 1)
                if back2(at):
                    pe.wait_ge(s["h_t_ready"], slot(at) - 1)
                for c in range(C):
                    mm = pe.transpose(h_turned[p][:, c * P:(c + 1) * P], h[p][:, c * P:(c + 1) * P], k.ident[:, :])
                mm.then_inc(s["h_turned"], 1)

            def go_down(at):
                p = at[1] % 2
                e = expert(at)
                pe.wait_ge(s["h_t_ready"], slot(at) + 1)
                if back2(at):
                    pe.wait_ge(s["y_ready"], slot(at) - 1)
                for c in range(C):
                    mm = pe.matmul(result[p][:, 0:D], h_t[p][:, c * P:(c + 1) * P], down[:, e, c, :],
                                   start=(c == 0), stop=(c == C - 1))
                mm.then_inc(s["result"], 1)

            def step(n, r):
                for d, work in ((1, turn_x), (0, go_up), (-1, turn_h), (-2, go_down)):
                    at = off(n, r, d)
                    if at is not None:
                        work(at)
            turn_x((0, 0))
            each(pe, step)
            turn_h((NR - 1, R - 1))
            go_down((NR - 1, R - 2))
            go_down((NR - 1, R - 1))

        @block.scalar
        def _(act):
            def copy_x(at):
                p = at[1] % 2
                act.wait_ge(s["turned"], slot(at) + 1)
                if back2(at):
                    act.wait_ge(s["hidden"], slot(at) - 1)
                act.activation(x_t[p][:, :], turned[p][:, 0:P], ACT.Copy).then_inc(s["x_ready"], 1)

            def gate(at):
                p = at[1] % 2
                if up_bias is not None:
                    act.wait_ge(s["biased"], slot(at) + 1)
                    if back2(at):
                        act.wait_ge(s["h_turned"], slot(at) - 1)
                    act.activation(h[p][:, :], g[p][:, :], m.act).then_inc(s["h_ready"], 1)
                else:
                    act.wait_ge(s["hidden"], slot(at) + 1)
                    if back2(at):
                        act.wait_ge(s["h_ready"], slot(at) - 1)
                    act.activation(g[p][:, 0:m.inner], hidden[p][:, 0:m.inner], m.act).then_inc(s["gated"], 1)

            def step(n, r):
                nxt = off(n, r, 1)
                if nxt is not None:
                    copy_x(nxt)
                gate((n, r))
            copy_x((0, 0))
            each(act, step)

        @block.vector
        def _(dve):
            def expert(at):
                return dve.value_load(k.slot_expert[0:1, bass.ds(slot(at), 1)], min_val=0, max_val=E - 1)

            def open_(at):
                p = at[1] % 2
                if up_bias is not None:
                    e = expert(at)
                    dve.wait_ge(s["hidden"], slot(at) + 1)
                    if back2(at):
                        dve.wait_ge(s["h_ready"], slot(at) - 1)
                    dve.tensor_tensor(g[p][:, :], hidden[p][:, :], up_bias[:, e, :], ALU.add).then_inc(s["biased"], 1)
                else:
                    dve.wait_ge(s["gated"], slot(at) + 1)
                    if back2(at):
                        dve.wait_ge(s["h_turned"], slot(at) - 1)
                    dve.tensor_tensor(h[p][:, :], g[p][:, 0:m.inner], hidden[p][:, m.inner:2 * m.inner],
                                      ALU.mult).then_inc(s["h_ready"], 1)

            def copy_h(at):
                p = at[1] % 2
                dve.wait_ge(s["h_turned"], slot(at) + 1)
                if back2(at):
                    dve.wait_ge(s["result"], slot(at) - 1)
                dve.tensor_copy(h_t[p][:, :], h_turned[p][:, 0:C * P]).then_inc(s["h_t_ready"], 1)

            def close(at):
                n, r = at
                p, q = r % 2, r // QD
                e = expert(at) if down_bias is not None else None
                dve.wait_ge(s["result"], slot(at) + 1)
                if r % QD == 0 and not early(n, 1):
                    dve.wait_ge(stored[q], 16 * n)
                if down_bias is not None:
                    op = dve.tensor_tensor(y[q][:, r % QD, :], result[p][:, 0:D], down_bias[:, e, :], ALU.add)
                else:
                    op = dve.tensor_copy(y[q][:, r % QD, :], result[p][:, 0:D])
                op.then_inc(s["y_ready"], 1)

            def step(n, r):
                for d, work in ((-1, copy_h), (0, open_), (-2, close)):
                    at = off(n, r, d)
                    if at is not None:
                        work(at)
            each(dve, step)
            copy_h((NR - 1, R - 1))
            close((NR - 1, R - 2))
            close((NR - 1, R - 1))


def build_combine(k, m, s_up, s_down, shared_bias=None, stats=True):
    nc, NB = k.nc, k.NB
    N = GROUP * P
    UP = s_up.shape[1] // P
    C = m.chunks
    with ExitStack() as ctx:
        sb = lambda n, s_, dt=F32: k.sb(m.name + n, s_, dt, ctx)
        g = [sb(f"cg{c}", [P, N]) for c in range(2)]
        h_t = [[sb(f"ch{p}_{c}", [P, N]) for c in range(C)] for p in range(2)]
        rows = [[sb(f"crow{r}_{j}", [P, GROUP, D]) for j in range(m.top)] for r in range(2)]
        places = [[sb(f"cplace{r}_{j}", [P, GROUP], I32) for j in range(m.top)] for r in range(2)]
        single = [[[sb(f"cp{r}_{j}_{n}", [P, 1], I32) for n in range(GROUP)] for j in range(m.top)] for r in range(2)]
        extra = sb("cextra", [P, GROUP, D])
        hidden = [k.psum(f"{m.name}chid{c}", [P, N], ctx) for c in range(4)]
        result = [k.psum(f"{m.name}cres{p}", [P, N], ctx) for p in range(2)]
        gathered = [k.pool_dma_sem(f"{m.name}c_gathered{r}") for r in range(2)]
        s = {n: k.sem(m.name + "c_" + n) for n in
             ("placed", "go", "hidden", "gated", "h_ready", "result", "freed", "added", "first", "second", "stats", "scaled")}
        block = ctx.enter_context(nc.Block())

        @block.gpsimd
        def _(pool):
            def step(g_, p):
                if not early(g_):
                    pool.wait_ge(s["freed"], g_ - 1)
                for n in range(GROUP):
                    for j in range(m.top):
                        pool.tensor_copy(single[p][j][n][:, :], k.place[j][:, bass.ds(GROUP * g_ + n, 1)]).then_inc(s["placed"], 1)
                pool.wait_ge(s["placed"], GROUP * m.top * (g_ + 1))
                pool.sem_inc(s["go"], 1)
                for n in range(GROUP):
                    for j in range(m.top):
                        pool.indirect_dma_start(rows[p][j][:, n, :], None, k.results,
                                                bass.IndirectOffsetOnAxis(single[p][j][n][:, 0:1], 0)).then_inc(gathered[p], 16)
            all_groups(pool, NB, step)

        @block.tensor
        def _(pe):
            def go_up(g_, p):
                pe.wait_ge(s["h_ready"], C * g_)
                for c in range(UP):
                    pe.matmul(hidden[c][:, :], s_up[:, c * P:(c + 1) * P], group_of(k.tmp_res, g_),
                              start=True, stop=True).then_inc(s["hidden"], 1)

            def go_down(g_, p):
                pe.wait_ge(s["h_ready"], C * (g_ + 1))
                if not early(g_):
                    pe.wait_ge(s["added"], g_ - 1)
                for n in range(GROUP):
                    for c in range(C):
                        mm = pe.matmul(result[p][:, n * D:(n + 1) * D], h_t[p][c][:, n * P:(n + 1) * P], s_down[:, c, :],
                                       start=(c == 0), stop=(c == C - 1))
                mm.then_inc(s["result"], 1)

            def step(g_, p):
                go_up(g_, p)
                go_down(g_, p)
            all_groups(pe, NB, step)

        @block.scalar
        def _(act):
            def step(g_, p):
                for c in range(C):
                    if shared_bias is None:
                        act.wait_ge(s["hidden"], UP * g_ + c + 1)
                        if not early(g_, 1):
                            act.wait_ge(s["h_ready"], C * (g_ - 1) + c + 1)
                        act.activation(g[c][:, :], hidden[c][:, :], m.act).then_inc(s["gated"], 1)
                    else:
                        act.wait_ge(s["hidden"], UP * g_ + c + 1)
                        if c == 0 and not early(g_):
                            act.wait_ge(s["result"], g_ - 1)
                        act.activation(h_t[p][c][:, :], hidden[c][:, :], m.act,
                                       bias=shared_bias[0][:, c:c + 1]).then_inc(s["h_ready"], 1)
            all_groups(act, NB, step)

        @block.vector
        def _(dve):
            def hide(g_, p):
                if not early(g_):
                    dve.wait_ge(s["result"], g_ - 1)
                for c in range(C):
                    dve.wait_ge(s["gated"], C * g_ + c + 1)
                    dve.wait_ge(s["hidden"], UP * g_ + C + c + 1)
                    dve.tensor_tensor(h_t[p][c][:, :], g[c][:, :], hidden[C + c][:, :], ALU.mult).then_inc(s["h_ready"], 1)

            def step(g_, p):
                if shared_bias is None:
                    hide(g_, p)
                if not early(g_, 1):
                    finish(g_ - 1, 1 - p)

            def finish(g_, p):
                res = result[p][:, :].rearrange("p (n d) -> p n d", d=D)
                x4 = group_of(k.x_res, g_)
                dve.wait_ge(s["result"], g_ + 1)
                if shared_bias is None:
                    dve.tensor_tensor(x4, x4, res, ALU.add).then_inc(s["added"], 1)
                    dve.wait_ge(s["added"], g_ + 1)
                else:
                    dve.tensor_tensor(extra[:, :, :], res, shared_bias[1][:, :].unsqueeze(1).broadcast_to([P, GROUP, D]),
                                      ALU.add).then_inc(s["added"], 1)
                    dve.wait_ge(s["added"], g_ + 1)
                    for n in range(GROUP):
                        b = GROUP * g_ + n
                        dve.scalar_tensor_tensor(out=k.x_res[:, b, :], in0=extra[:, n, :], scalar=k.coef_shared[:, bass.ds(b, 1)],
                                                 in1=k.x_res[:, b, :], op0=ALU.mult, op1=ALU.add).then_inc(s["scaled"], 1)
                    dve.wait_ge(s["scaled"], GROUP * (g_ + 1))
                dve.wait_ge(gathered[p], 8 * m.top * GROUP * (g_ - p) + 16 * m.top * GROUP)
                for j in range(m.top):
                    done = s["first"] if j == 0 else s["second"]
                    for n in range(GROUP):
                        b = GROUP * g_ + n
                        dve.scalar_tensor_tensor(out=k.x_res[:, b, :], in0=rows[p][j][:, n, :],
                                                 scalar=k.choice_w[j][:, bass.ds(b, 1)], in1=k.x_res[:, b, :],
                                                 op0=ALU.mult, op1=ALU.add).then_inc(done, 1)
                    dve.wait_ge(done, GROUP * (g_ + 1))
                dve.sem_inc(s["freed"], 1)
                if stats:
                    for n in range(GROUP):
                        b = GROUP * g_ + n
                        dve.bn_stats(k.stats[:, b, :], k.x_res[:, b, :]).then_inc(s["stats"], 1)
            all_groups(dve, NB, step)
            finish(NB // GROUP - 1, 1)
            if stats:
                dve.wait_ge(s["stats"], NB)


def build_expert_layer_0(k):
    nc, ins = k.nc, k.ins
    m = Experts("m0_", 256, 2, 2, ACT.Silu)
    with ExitStack() as ctx:
        up = k.sb("m0_up", [P, E, 512], F32, ctx)
        down = k.sb("m0_down", [P, E, 2, D], F32, ctx)
        s_up = k.sb("m0_s_up", [P, 512], F32, ctx)
        s_down = k.sb("m0_s_down", [P, 2, D], F32, ctx)
        gate = k.sb("m0_gate", [P, E], F32, ctx)
        scale = k.sb("m0_scale", [P, 1], F32, ctx)
        bias = k.sb("m0_bias", [P, 1], F32, ctx)
        bias_wide = k.sb("m0_bias_wide", [P, P], F32, ctx)
        gate_scaled = k.sb("m0_gate_scaled", [P, E], F32, ctx)
        logit_bias = k.sb("m0_logit_bias", [P, E], F32, ctx)
        loaded = k.sem("m0_loaded")
        link = Chain(k.sem("m0_chain"))
        product = k.sem("m0_bias_product")
        loads = [(up[:, :, 0:256], ins["L0_ffn_Wg"].rearrange("e h i -> h e i")),
                 (up[:, :, 256:512], ins["L0_ffn_Wu"].rearrange("e h i -> h e i")),
                 (down[:, :, :, :], ins["L0_ffn_Wd"].rearrange("e (c p) h -> p e c h", p=P)),
                 (s_up[:, 0:256], ins["L0_ffn_sWg"]), (s_up[:, 256:512], ins["L0_ffn_sWu"]),
                 (s_down[:, :, :], ins["L0_ffn_sWd"].rearrange("(c p) h -> p c h", p=P)),
                 (gate[:, :], ins["L0_ffn_gate_w"].rearrange("e h -> h e")),
                 (scale[:, :], column(ins["L0_ffn_ln_scale"])), (bias[:, :], column(ins["L0_ffn_ln_bias"]))]
        with ExitStack() as inner:
            ps = k.psum("m0_bias_ps", [P, 512], inner)
            block = inner.enter_context(nc.Block())

            @block.sync
            def _(sp):
                for to, of in loads:
                    sp.dma_start(to, of, allow_slow_non_contiguous=True).then_inc(loaded, 16)

            @block.vector
            def _(dve):
                dve.wait_ge(loaded, 16 * len(loads))
                link(dve, dve.tensor_scalar(gate_scaled[:, :], gate[:, :], scale[:, 0:1], None, ALU.mult))
                link(dve, dve.tensor_copy(bias_wide[:, :], bias[:, 0:1].broadcast_to([P, P])))
                dve.wait_ge(product, 1)
                link(dve, dve.tensor_copy(logit_bias[:, :], ps[:, 0:E]))

            @block.tensor
            def _(pe):
                pe.wait_ge(link.sem, 2)
                pe.matmul(ps[:, 0:E], bias_wide[:, :], gate[:, :], start=True, stop=True).then_inc(product, 1)
        build_rstd(k, "m0_rstd", composed=True)
        build_prepare(k, m, gate_scaled[:, :], None, None)
        build_route(k, m, logit_bias)
        build_dispatch(k, m)
        build_experts(k, m, up, down)
        build_combine(k, m, s_up, s_down)



TOP_DELAYS = 9


def build_correlation(k):
    nc, ins, NB = k.nc, k.ins, k.NB
    N = GROUP * P
    with ExitStack() as ctx:
        sb = lambda n, s_, dt=F32: k.sb(n, s_, dt, ctx)
        wq, wk = sb("c_wq", [P, D]), sb("c_wk", [P, D])
        bq, bk = sb("c_bq", [1, D]), sb("c_bk", [1, D])
        dft, inverse, flip = sb("c_dft", [P, P]), sb("c_inverse", [P, P]), sb("c_flip", [P, 2 * P])
        dft_sums = sb("c_dft_sums", [1, 2, P])
        ones = sb("c_ones", [P, 1])
        xn = [sb(f"c_xn{p}", [P, GROUP, D]) for p in range(2)]
        cx = [sb(f"c_cx{p}", [P, GROUP, D]) for p in range(2)]
        xf = [sb(f"c_xf{p}", [P, N]) for p in range(2)]
        cf = [sb(f"c_cf{p}", [P, N]) for p in range(2)]
        kf = [sb(f"c_kf{p}", [P, N]) for p in range(2)]
        product = [sb(f"c_product{p}", [P, GROUP, P]) for p in range(2)]
        spectrum = sb("c_spectrum", [P, NB])
        corr, work, weight = sb("c_corr", [NB, P]), sb("c_work", [NB, P]), sb("c_weight", [NB, P])
        best, ninth = sb("c_best", [NB, 8]), sb("c_ninth", [NB, 8])
        total = sb("c_total", [NB, 1])
        weight_t = sb("c_weight_t", [P, NB])
        twice = sb("c_twice", [NB, 2 * P])
        x_spec, c_spec = k.psum("c_x_spec", [P, N], ctx), k.psum("c_c_spec", [P, N], ctx)
        q_spec, k_spec = k.psum("c_q_spec", [P, N], ctx), k.psum("c_k_spec", [P, N], ctx)
        power = k.psum("c_power", [P, 512], ctx)
        back = k.psum("c_back", [P, 512], ctx)
        loaded = k.sem("c_loaded")
        cx_loaded = [k.sem(f"c_cx_loaded{p}") for p in range(2)]
        link = Chain(k.sem("c_chain"))
        s = {n: k.sem("c_" + n) for n in ("ones_set", "normed", "x_spec", "c_spec", "xf", "cf", "q_spec", "k_spec", "kf",
                                          "product", "power", "spectrum", "corr", "shifted", "exp_done", "weighted", "turned", "turn_copied", "flipped", "twice", "stored")}
        loads = [(wq[:, :], ins["L1_xattn_Wq"]), (wk[:, :], ins["L1_xattn_Wk"]), (bq[:, :], ins["L1_xattn_bq"].unsqueeze(0)),
                 (bk[:, :], ins["L1_xattn_bk"].unsqueeze(0)), (dft[:, :], ins["c_dft"]), (inverse[:, :], ins["c_inverse"]),
                 (flip[:, :], ins["c_flip"]), (dft_sums[:, :, :], ins["c_dft_sums"].unsqueeze(0))]
        block = ctx.enter_context(nc.Block())
        NG = NB // GROUP

        @block.sync
        def _(sp):
            for to, of in loads:
                sp.dma_start(to, of).then_inc(loaded, 16)

            def step(g, p):
                if not early(g):
                    sp.wait_ge(s["c_spec"], g - 1)
                sp.dma_start(cx[p][0:S2, :, :], ins["ctx_1024"][bass.ds(GROUP * g, GROUP)].rearrange("b t d -> t b d")).then_inc(cx_loaded[p], 16)
            all_groups(sp, NB, step)
            sp.wait_ge(s["twice"], 1)
            sp.dma_start(k.circulant, twice[:, :]).then_inc(s["stored"], 16)
            sp.wait_ge(s["stored"], 16)

        @block.tensor
        def _(pe):
            def spectra(g, p):
                pe.wait_ge(s["normed"], GROUP * (g + 1))
                pe.wait_ge(s["xf"], g)
                for n in range(GROUP):
                    mm = pe.matmul(x_spec[:, n * P:(n + 1) * P], xn[p][:, n, :], dft[:, :], start=True, stop=True)
                mm.then_inc(s["x_spec"], 1)
                pe.wait_ge(cx_loaded[p], 8 * (g - p) + 16)
                pe.wait_ge(s["cf"], g)
                for n in range(GROUP):
                    mm = pe.matmul(c_spec[:, n * P:(n + 1) * P], cx[p][0:S2, n, :], dft[0:S2, :], start=True, stop=True)
                mm.then_inc(s["c_spec"], 1)

            def project(g, p):
                pe.wait_ge(s["cf"], g + 1)
                pe.wait_ge(s["kf"], g)
                pe.matmul(k_spec[:, :], wk[:, :], cf[p][:, :], start=True, stop=False)
                pe.matmul(k_spec[:, :], bk[:, :], dft_sums[:, 1, :].unsqueeze(1).broadcast_to([1, GROUP, P]),
                          start=False, stop=True).then_inc(s["k_spec"], 1)
                pe.wait_ge(s["xf"], g + 1)
                pe.wait_ge(s["product"], g)
                pe.matmul(q_spec[:, :], wq[:, :], xf[p][:, :], start=True, stop=False)
                pe.matmul(q_spec[:, :], bq[:, :], dft_sums[:, 0, :].unsqueeze(1).broadcast_to([1, GROUP, P]),
                          start=False, stop=True).then_inc(s["q_spec"], 1)

            def powers(g, p):
                pe.wait_ge(s["product"], g + 1)
                for n in range(GROUP):
                    mm = pe.matmul(power[:, bass.ds(GROUP * g + n, 1)], product[p][:, n, :], ones[:, :], start=True, stop=True)
                mm.then_inc(s["power"], 1)

            def step(g, p):
                spectra(g, p)
                if not early(g, 1):
                    powers(g - 1, 1 - p)
                project(g, p)
            pe.wait_ge(loaded, 16 * len(loads))
            pe.wait_ge(s["ones_set"], 1)
            all_groups(pe, NB, step)
            powers(NG - 1, 1)
            pe.wait_ge(s["spectrum"], 1)
            pe.matmul(back[0:NB, 0:P], spectrum[:, :], inverse[:, :], start=True, stop=True).then_inc(s["corr"], 1)
            pe.wait_ge(s["weighted"], 1)
            pe.transpose(power[:, 0:NB], weight[:, :], k.ident[0:NB, 0:NB]).then_inc(s["turned"], 1)
            pe.wait_ge(s["turn_copied"], 1)
            pe.matmul(back[0:NB, 0:2 * P], weight_t[:, :], flip[:, :], start=True, stop=True).then_inc(s["flipped"], 1)

        @block.scalar
        def _(act):
            def step(g, p):
                act.wait_ge(s["x_spec"], g + 1)
                if not early(g):
                    act.wait_ge(s["q_spec"], g - 1)
                act.activation(xf[p][:, :], x_spec[:, :], ACT.Copy).then_inc(s["xf"], 1)
                act.wait_ge(s["k_spec"], g + 1)
                if not early(g):
                    act.wait_ge(s["product"], g - 1)
                act.activation(kf[p][:, :], k_spec[:, :], ACT.Copy).then_inc(s["kf"], 1)
            all_groups(act, NB, step)
            act.wait_ge(s["shifted"], 1)
            act.activation(work[:, :], corr[:, :], ACT.Exp).then_inc(s["exp_done"], 1)

        @block.vector
        def _(dve):
            def multiply(g, p):
                dve.wait_ge(s["q_spec"], g + 1)
                dve.wait_ge(s["kf"], g + 1)
                if not early(g):
                    dve.wait_ge(s["power"], g - 1)
                dve.tensor_tensor(product[p][:, :, :], q_spec[:, :].rearrange("p (n d) -> p n d", d=P),
                                  kf[p][:, :].rearrange("p (n d) -> p n d", d=P), ALU.mult).then_inc(s["product"], 1)

            def step(g, p):
                if not early(g):
                    dve.wait_ge(s["x_spec"], g - 1)
                normalise_group(k, dve, xn[p], k.x_res, g, k.rstd, s["normed"])
                if not early(g, 1):
                    multiply(g - 1, 1 - p)
                dve.wait_ge(s["c_spec"], g + 1)
                if not early(g):
                    dve.wait_ge(s["k_spec"], g - 1)
                dve.tensor_copy(cf[p][:, :], c_spec[:, :]).then_inc(s["cf"], 1)
            dve.memset(ones[:, :], 1.0).then_inc(s["ones_set"], 1)
            all_groups(dve, NB, step)
            multiply(NG - 1, 1)
            dve.wait_ge(s["power"], NG)
            dve.tensor_copy(spectrum[:, :], power[:, 0:NB]).then_inc(s["spectrum"], 1)
            dve.wait_ge(s["corr"], 1)

            def do(op):
                link(dve, op)
            LOW = -3.0e38
            do(dve.tensor_copy(corr[:, :], back[0:NB, 0:P]))
            do(dve.max(best[:, :], corr[:, :]))
            do(dve.match_replace(work[:, :], best[:, :], corr[:, :], LOW))
            do(dve.max(ninth[:, :], work[:, :]))
            do(dve.memset(ninth[:, 1:8], LOW))
            do(dve.match_replace(weight[:, :], ninth[:, :], work[:, :], LOW))
            do(dve.tensor_scalar(weight[:, :], weight[:, :], LOW, None, ALU.is_equal))
            dve.tensor_scalar(corr[:, :], corr[:, :], best[:, 0:1], None, ALU.subtract).then_inc(s["shifted"], 1)
            dve.wait_ge(s["exp_done"], 1)
            do(dve.tensor_tensor(weight[:, :], weight[:, :], work[:, :], ALU.mult))
            do(dve.tensor_reduce(total[:, :], weight[:, :], AX.X, ALU.add))
            do(dve.reciprocal(total[:, :], total[:, :]))
            dve.tensor_scalar(weight[:, :], weight[:, :], total[:, 0:1], None, ALU.mult).then_inc(s["weighted"], 1)
            dve.wait_ge(s["turned"], 1)
            dve.tensor_copy(weight_t[:, :], power[:, 0:NB]).then_inc(s["turn_copied"], 1)
            dve.wait_ge(s["flipped"], 1)
            dve.tensor_copy(twice[:, :], back[0:NB, 0:2 * P]).then_inc(s["twice"], 1)


def build_roll(k):
    nc, ins, NB = k.nc, k.ins, k.NB
    N = GROUP * P
    with ExitStack() as ctx:
        roll = [k.sb(f"v_roll{p}", [P, GROUP, P], F32, ctx) for p in range(2)]
        bo_rows = k.sb("v_bo", [P, D], F32, ctx)
        rolled = [k.psum(f"v_rolled{p}", [P, N], ctx) for p in range(2)]
        loaded = [k.sem(f"v_loaded{p}") for p in range(2)]
        bo_loaded = k.sem("v_bo_loaded")
        s = {n: k.sem("v_" + n) for n in ("rolled", "biased", "added", "stats")}
        block = ctx.enter_context(nc.Block())

        @block.sync
        def _(sp):
            sp.dma_start(bo_rows[:, :], row_broadcast(ins["L1_xattn_bo"], P)).then_inc(bo_loaded, 16)

            def step(g, p):
                if not early(g):
                    sp.wait_ge(s["rolled"], g - 1)
                rows = k.circulant[bass.ds(GROUP * g, GROUP), P - S2 + 1:2 * P - S2 + 1]
                sp.dma_start(roll[p][0:S2, :, :],
                             bass.AP(tensor=rows.tensor, offset=rows.offset,
                                     ap=[[1, S2], [2 * P, GROUP], [1, P]])).then_inc(loaded[p], 16)
            all_groups(sp, NB, step)

        @block.tensor
        def _(pe):
            def step(g, p):
                pe.wait_ge(loaded[p], 8 * (g - p) + 16)
                if not early(g):
                    pe.wait_ge(s["biased"], g - 1)
                for n in range(GROUP):
                    mm = pe.matmul(rolled[p][:, n * D:(n + 1) * D], roll[p][0:S2, n, :], k.vo_res[0:S2, GROUP * g + n, :],
                                   start=True, stop=True)
                mm.then_inc(s["rolled"], 1)
            all_groups(pe, NB, step)

        @block.gpsimd
        def _(pool):
            def step(g, p):
                pool.tensor_tensor(group_of(k.x_res, g), group_of(k.x_res, g),
                                   bo_rows[:, :].unsqueeze(1).broadcast_to([P, GROUP, D]), ALU.add).then_inc(s["added"], 1)
            pool.wait_ge(bo_loaded, 16)
            all_groups(pool, NB, step)

        @block.vector
        def _(dve):
            def step(g, p):
                dve.wait_ge(s["rolled"], g + 1)
                dve.wait_ge(s["added"], g + 1)
                dve.tensor_tensor(group_of(k.x_res, g), rolled[p][:, :].rearrange("p (n d) -> p n d", d=D),
                                  group_of(k.x_res, g), ALU.add).then_inc(s["biased"], 1)
                dve.wait_ge(s["biased"], g + 1)
                for n in range(GROUP):
                    dve.bn_stats(k.stats[:, GROUP * g + n, :], k.x_res[:, GROUP * g + n, :]).then_inc(s["stats"], 1)
            all_groups(dve, NB, step)
            dve.wait_ge(s["stats"], NB)



def build_self_attention(k):
    nc, ins, NB = k.nc, k.ins, k.NB
    SCALE = 1.0 / float(DH) ** 0.5
    W = HQ * P
    CH = 2
    HC = H // 2
    COL = 2 * QUAD
    with ExitStack() as ctx:
        sb = lambda n, s_, dt=F32: k.sb(n, s_, dt, ctx)
        wqkv, wo = sb("s_wqkv", [P, 3 * D]), sb("s_wo", [P, D])
        gain, shift_ = sb("s_gain", [P, 1]), sb("s_shift", [P, 1])
        bq, bk = sb("s_bq", [P, 1]), sb("s_bk", [P, 1])
        bv_rows, bo_rows = sb("s_bv_rows", [P, D]), sb("s_bo_rows", [P, D])
        rstd12 = sb("s_rstd12", [P, NB])
        xn = [sb(f"s_xn{p}", [P, D]) for p in range(2)]
        xf = sb("s_xf", [P, D])
        xn_t = [sb(f"s_xn_t{p}", [P, P]) for p in range(2)]
        q_t = [sb(f"s_q_t{p}", [P, P]) for p in range(2)]
        k_t = [sb(f"s_k_t{p}", [P, P]) for p in range(2)]
        k_wide = [sb(f"s_k_wide{p}", [P, HQ, P]) for p in range(2)]
        v_heads = [sb(f"s_v_heads{p}", [P, H, COL]) for p in range(2)]
        maxima = [sb(f"s_maxima{c}", [P, HC], BF16) for c in range(2)]
        probs = [sb(f"s_probs{c}", [P, HC, P]) for c in range(2)]
        probs_t = [sb(f"s_probs_t{c}", [P, HC, P]) for c in range(2)]
        o_t = sb("s_o_t", [P, 2 * P])
        rsum = sb("s_rsum", [P, H])
        mixed = sb("s_mixed", [P, D])
        mixed_t = sb("s_mixed_t", [P, P])

        scores = [k.psum(f"s_scores{c}", [P, 2, W], ctx) for c in range(2)]
        p_turned = k.psum("s_p_turned", [P, 2, W], ctx)
        front = k.psum("s_front", [P, 512], ctx)
        out_ps = k.psum("s_out", [P, 512], ctx)
        loaded = k.sem("s_loaded")
        link = Chain(k.sem("s_chain"))
        s = {n: k.sem("s_" + n) for n in
             ("zeroed", "ones_set", "xn_ready", "xf_ready", "turned", "xn_t_ready", "qkv_done", "qk_ready", "v_ready", "wide_ready",
              "scores_done", "max_ready", "shifted", "probs_ready", "p_turned", "p_copied_a", "p_copied_b", "pv_part", "pv_done",
              "o_ready", "o_turned", "recip", "mixed", "mixed_turned", "mixed_t_ready", "projected", "x2_ready",
              "x2_biased", "stats", "grown")}
        P_ = "L1_ffn_"
        loads = [(wqkv[:, :], ins[P_ + "Wqkv"]), (wo[:, :], ins[P_ + "Wo"]), (gain[:, :], column(ins[P_ + "ln1_g"])),
                 (shift_[:, :], column(ins[P_ + "ln1_b"])), (bq[:, :], column(ins[P_ + "bqkv"][0:D])),
                 (bk[:, :], column(ins[P_ + "bqkv"][D:2 * D])), (bv_rows[:, :], row_broadcast(ins[P_ + "bqkv"][2 * D:3 * D], P)),
                 (bo_rows[:, :], row_broadcast(ins[P_ + "bo"], P))]
        block = ctx.enter_context(nc.Block())

        def each(eng, step, last):
            for b in (0, 1):
                step(b, b)
            with eng.Fori(1, NB // 2 - 1) as i:
                for p in (0, 1):
                    step(2 * i + p, p)
            for b in (NB - 2, NB - 1):
                step(b, b % 2)
            last()

        def is_(b, n):
            return isinstance(b, int) and b == n

        def before(b, c):
            return (b, c - 1) if c else None if is_(b, 0) else (b - 1, CH - 1)

        @block.sync
        def _(sp):
            for to, of in loads:
                sp.dma_start(to, of).then_inc(loaded, 16)

        @block.tensor
        def _(pe):
            def turn_x(b, p):
                pe.wait_ge(s["xn_ready"], b + 1)
                pe.wait_ge(s["v_ready"], b)
                pe.transpose(front[:, 3 * P:4 * P], xn[p][:, :], k.ident[:, :]).then_inc(s["turned"], 1)

            def project(b, p):
                pe.wait_ge(s["xn_t_ready"], b + 1)
                pe.matmul(front[:, 0:P], wqkv[:, 0:D], xn_t[p][:, :], start=True, stop=True)
                pe.matmul(front[:, P:2 * P], wqkv[:, D:2 * D], xn_t[p][:, :], start=True, stop=True)
                pe.matmul(front[:, 2 * P:3 * P], xn_t[p][:, :], wqkv[:, 2 * D:3 * D], start=True, stop=True).then_inc(s["qkv_done"], 1)

            def score(b, p, c):
                pe.wait_ge(s["wide_ready"], b + 1)
                if not is_(b, 0):
                    pe.wait_ge(s["probs_ready"], CH * (b - 1) + c + 1)
                for j in range(2):
                    q0 = QUAD * (2 * c + j)
                    mm = pe.matmul(scores[c][:, j, :], q_t[p][q0:q0 + QUAD, :], k_wide[p][q0:q0 + QUAD, :, :], start=True, stop=True)
                mm.then_inc(s["scores_done"], 1)

            def shift(b, c):
                pe.wait_ge(s["max_ready"], CH * b + c + 1)
                for j in range(2):
                    mm = pe.matmul(scores[c][:, j, :], k.identb[:, :],
                                   maxima[c][:, HQ * j:HQ * (j + 1)].unsqueeze(2).broadcast_to([P, HQ, P]),
                                   start=False, stop=True, skip_group_check=True)
                mm.then_inc(s["shifted"], 1)

            def turn_p(b, c):
                pe.wait_ge(s["probs_ready"], CH * b + c + 1)
                pe.wait_ge(s["p_copied_a"], CH * b + c)
                pe.wait_ge(s["p_copied_b"], CH * b + c)
                for h in range(HC):
                    mm = pe.transpose(p_turned[:, h // HQ, h % HQ * P:(h % HQ + 1) * P], probs[c][:, h, :], k.ident[:, :])
                mm.then_inc(s["p_turned"], 1)

            def weigh(b, p, c):
                pe.wait_ge(s["p_copied_a"], CH * b + c + 1)
                pe.wait_ge(s["p_copied_b"], CH * b + c + 1)
                if c == 0:
                    pe.wait_ge(s["v_ready"], b + 1)
                    pe.wait_ge(s["x2_ready"], b)
                for h in range(HQ):
                    for half in range(2):
                        mm = pe.matmul(out_ps[COL * half:COL * (half + 1), c * P:(c + 1) * P],
                                       v_heads[p][:, HQ * (2 * c + half) + h, :], probs_t[c][:, HQ * half + h, :],
                                       start=(h == 0), stop=(h == HQ - 1))
                mm.then_inc(s["pv_done"] if c else s["pv_part"], 1)

            def turn_o(b):
                pe.wait_ge(s["o_ready"], b + 1)
                for jj in range(2):
                    mm = pe.transpose(out_ps[:, (2 + jj) * P:(3 + jj) * P], o_t[:, jj * P:(jj + 1) * P], k.ident[:, :])
                mm.then_inc(s["o_turned"], 1)

            def turn_mixed(b):
                pe.wait_ge(s["mixed"], b + 1)
                pe.transpose(out_ps[:, 0:P], mixed[:, :], k.ident[:, :]).then_inc(s["mixed_turned"], 1)

            def output(b):
                pe.wait_ge(s["mixed_t_ready"], b + 1)
                pe.matmul(out_ps[:, P:2 * P], mixed_t[:, :], wo[:, :], start=True, stop=True).then_inc(s["projected"], 1)

            def step(b, p):
                last, first = is_(b, NB - 1), is_(b, 0)
                score(b, p, 1)
                if not first:
                    turn_p(b - 1, 1)
                shift(b, 0)
                if not last:
                    turn_x(b + 1, 1 - p)
                if not first:
                    weigh(b - 1, 1 - p, 1)
                if not last:
                    project(b + 1, 1 - p)
                turn_p(b, 0)
                if not first:
                    turn_o(b - 1)
                shift(b, 1)
                if not first:
                    turn_mixed(b - 1)
                if not last:
                    score(b + 1, 1 - p, 0)
                if not first:
                    output(b - 1)
                weigh(b, p, 0)

            def last():
                turn_p(NB - 1, 1)
                weigh(NB - 1, 1, 1)
                turn_o(NB - 1)
                turn_mixed(NB - 1)
                output(NB - 1)
            pe.wait_ge(loaded, 16 * len(loads))
            turn_x(0, 0)
            project(0, 0)
            score(0, 0, 0)
            each(pe, step, last)

        @block.scalar
        def _(act):
            def affine(b, p):
                act.wait_ge(s["turned"], b + 1)
                if not early(b):
                    act.wait_ge(s["qkv_done"], b - 1)
                act.activation(xn_t[p][:, :], front[:, 3 * P:4 * P], ACT.Identity, bias=shift_[:, 0:1],
                               scale=gain[:, 0:1]).then_inc(s["xn_t_ready"], 1)

            def bias_qk(b, p):
                act.wait_ge(s["qkv_done"], b + 1)
                if not early(b):
                    act.wait_ge(s["scores_done"], CH * (b - 1))
                    act.wait_ge(s["wide_ready"], b - 1)
                act.activation(q_t[p][:, :], front[:, 0:P], ACT.Identity, bias=bq[:, 0:1])
                act.activation(k_t[p][:, :], front[:, P:2 * P], ACT.Identity, bias=bk[:, 0:1]).then_inc(s["qk_ready"], 1)

            def exponent(b, c):
                act.wait_ge(s["shifted"], CH * b + c + 1)
                if not is_(b, 0):
                    act.wait_ge(s["p_turned"], CH * (b - 1) + c + 1)
                act.activation(probs[c][:, :, :].rearrange("p h k -> p (h k)"),
                               scores[c][:, :, :].rearrange("p j k -> p (j k)"), ACT.Exp, scale=SCALE).then_inc(s["probs_ready"], 1)

            def copy_p(b, c):
                act.wait_ge(s["p_turned"], CH * b + c + 1)
                if not is_(b, 0):
                    act.wait_ge(s["pv_done"] if c else s["pv_part"], b)
                act.activation(probs_t[c][:, 0:HQ, :].rearrange("p h k -> p (h k)"), p_turned[:, 0, :], ACT.Copy).then_inc(s["p_copied_a"], 1)

            def copy_mixed(b):
                act.wait_ge(s["mixed_turned"], b + 1)
                act.wait_ge(s["projected"], b)
                act.activation(mixed_t[:, :], out_ps[:, 0:P], ACT.Copy).then_inc(s["mixed_t_ready"], 1)

            def step(b, p):
                last, first = is_(b, NB - 1), is_(b, 0)
                if not first:
                    copy_p(b - 1, 1)
                exponent(b, 0)
                if not last:
                    affine(b + 1, 1 - p)
                    bias_qk(b + 1, 1 - p)
                copy_p(b, 0)
                exponent(b, 1)
                if not first:
                    copy_mixed(b - 1)

            def last():
                copy_p(NB - 1, 1)
                copy_mixed(NB - 1)
            act.wait_ge(loaded, 16 * len(loads))
            affine(0, 0)
            bias_qk(0, 0)
            each(act, step, last)

        @block.gpsimd
        def _(pool):
            def spread(b, p):
                pool.wait_ge(s["qk_ready"], b + 1)
                if not early(b):
                    pool.wait_ge(s["scores_done"], CH * (b - 1))
                pool.tensor_tensor(k_wide[p][:, :, :], k_t[p][:, :].unsqueeze(1).broadcast_to([P, HQ, P]),
                                   k.headmask[:, :].unsqueeze(2).broadcast_to([P, HQ, P]), ALU.mult).then_inc(s["wide_ready"], 1)

            def grow(b):
                pool.wait_ge(s["x2_ready"], b + 1)
                pool.tensor_tensor(k.x_res[:, b, :], k.x_res[:, b, :], k.tmp_res[:, b, :], ALU.add).then_inc(s["grown"], 1)

            def step(b, p):
                if not is_(b, NB - 1):
                    spread(b + 1, 1 - p)
                if not is_(b, 0):
                    grow(b - 1)
            for p in range(2):
                pool.memset(v_heads[p][:, :, :], 0.0).then_inc(s["zeroed"], 1)
            pool.wait_ge(s["zeroed"], 2)
            for p in range(2):
                first = v_heads[p][:, :, :]
                pool.memset(bass.AP(tensor=first.tensor, offset=first.offset + QUAD,
                                    ap=[list(first.ap[0]), [HQ * COL, H // HQ], [COL + 1, HQ]]), 1.0).then_inc(s["ones_set"], 1)
            pool.wait_ge(s["ones_set"], 2)
            spread(0, 0)
            each(pool, step, lambda: grow(NB - 1))
            pool.wait_ge(s["grown"], NB)

        @block.vector
        def _(dve):
            def normalise(b, p):
                if not early(b):
                    dve.wait_ge(s["turned"], b - 1)
                dve.tensor_scalar(xn[p][:, :], k.x_res[:, b, :], k.mean[:, bass.ds(b, 1)], rstd12[:, bass.ds(b, 1)],
                                  ALU.subtract, ALU.mult).then_inc(s["xn_ready"], 1)

            def bias_v(b, p):
                dve.wait_ge(s["qk_ready"], b + 1)
                if not early(b):
                    dve.wait_ge(s["pv_done"], b - 1)
                first = v_heads[p][:, :, :]
                blocks = bass.AP(tensor=first.tensor, offset=first.offset,
                                 ap=[list(first.ap[0]), [HQ * COL, H // HQ], [COL + DH, HQ], [1, DH]])
                dve.tensor_tensor(blocks, front[:, 2 * P:3 * P].rearrange("p (j h d) -> p j h d", h=HQ, d=DH),
                                  bv_rows[:, :].rearrange("p (j h d) -> p j h d", h=HQ, d=DH), ALU.add).then_inc(s["v_ready"], 1)

            def maximum(b, c):
                dve.wait_ge(s["scores_done"], CH * b + c + 1)
                if not is_(b, 0):
                    dve.wait_ge(s["shifted"], CH * (b - 1) + c + 1)
                dve.tensor_reduce(maxima[c][:, :], scores[c][:, :, :].rearrange("p j (h q) -> p (j h) q", q=P),
                                  AX.X, ALU.max, negate=True).then_inc(s["max_ready"], 1)

            def copy_p(b, c):
                dve.wait_ge(s["p_turned"], CH * b + c + 1)
                if not is_(b, 0):
                    dve.wait_ge(s["pv_done"] if c else s["pv_part"], b)
                dve.tensor_copy(probs_t[c][:, HQ:HC, :].rearrange("p h k -> p (h k)"), p_turned[:, 1, :]).then_inc(s["p_copied_b"], 1)

            def copy_o(b):
                dve.wait_ge(s["pv_done"], b + 1)
                dve.wait_ge(s["o_turned"], b)
                dve.tensor_copy(o_t[:, :], out_ps[:, 0:2 * P]).then_inc(s["o_ready"], 1)

            def mix(b):
                dve.wait_ge(s["o_turned"], b + 1)
                both = out_ps[:, 2 * P:4 * P].rearrange("p (j c) -> p j c", c=COL)
                dve.reciprocal(rsum[:, :].rearrange("p (j h) -> p j h", h=HQ), both[:, :, QUAD:QUAD + HQ]).then_inc(s["recip"], 1)
                dve.wait_ge(s["recip"], b + 1)
                dve.wait_ge(s["mixed_turned"], b)
                dve.tensor_tensor(mixed[:, :].rearrange("p (j h d) -> p j h d", h=HQ, d=DH),
                                  both[:, :, 0:QUAD].rearrange("p j (h d) -> p j h d", d=DH),
                                  rsum[:, :].rearrange("p (j h) -> p j h", h=HQ).unsqueeze(3).broadcast_to([P, H // HQ, HQ, DH]),
                                  ALU.mult).then_inc(s["mixed"], 1)

            def base(b):
                dve.tensor_scalar(xf[:, :], k.x_res[:, b, :], k.mean[:, bass.ds(b, 1)], k.rstd[:, bass.ds(b, 1)],
                                  ALU.subtract, ALU.mult).then_inc(s["xf_ready"], 1)
                dve.wait_ge(s["xf_ready"], b + 1)
                dve.tensor_tensor(xf[:, :], xf[:, :], bo_rows[:, :], ALU.add).then_inc(s["x2_biased"], 1)

            def close(b):
                dve.wait_ge(s["projected"], b + 1)
                dve.wait_ge(s["x2_biased"], b + 1)
                dve.tensor_tensor(k.tmp_res[:, b, :], out_ps[:, P:2 * P], xf[:, :], ALU.add).then_inc(s["x2_ready"], 1)
                dve.wait_ge(s["x2_ready"], b + 1)
                dve.bn_stats(k.stats[:, b, :], k.tmp_res[:, b, :]).then_inc(s["stats"], 1)

            def step(b, p):
                last, first = is_(b, NB - 1), is_(b, 0)
                if not first:
                    copy_p(b - 1, 1)
                maximum(b, 1)
                if not first:
                    copy_o(b - 1)
                if not last:
                    bias_v(b + 1, 1 - p)
                if not first:
                    mix(b - 1)
                    base(b - 1)
                copy_p(b, 0)
                if not first:
                    close(b - 1)
                if not last:
                    if not is_(b, NB - 2):
                        normalise(b + 2, p)
                    maximum(b + 1, 0)

            def last():
                copy_p(NB - 1, 1)
                copy_o(NB - 1)
                mix(NB - 1)
                base(NB - 1)
                close(NB - 1)
                dve.wait_ge(s["stats"], NB)
            link(dve, dve.tensor_tensor(rstd12[:, :], k.rstd[:, :], k.rstd2[:, :], ALU.mult))
            dve.wait_ge(loaded, 16 * len(loads))
            dve.wait_ge(s["ones_set"], 2)
            normalise(0, 0)
            bias_v(0, 0)
            normalise(1, 1)
            maximum(0, 0)
            each(dve, step, last)


def build_expert_layer_1(k):
    nc, ins, NB = k.nc, k.ins, k.NB
    m = Experts("m1_", 512, 4, 1, ACT.Gelu)
    N_ = "L1_ffn_"
    with ExitStack() as ctx:
        sb = lambda n, s_, dt=F32: k.sb("m1_" + n, s_, dt, ctx)
        columns = sb("columns", [P, E + 2])
        gain, shift_, gain_rows, shift_rows = sb("gain", [P, 1]), sb("shift", [P, 1]), sb("gain_rows", [P, D]), sb("shift_rows", [P, D])
        coef_bias = sb("coef_bias", [P, E + 2])
        up, down = sb("up", [P, E, 512]), sb("down", [P, E, 4, D])
        up_bias, down_bias = sb("up_bias", [P, E, 512]), sb("down_bias", [P, E, D])
        loaded = k.sem("m1_loaded")
        zeroed = k.sem("m1_zeroed")
        loads = [(columns[:, 0:E], ins[N_ + "gate_w"]), (columns[:, E:E + 2], ins[N_ + "coef_w"]),
                 (gain[:, :], column(ins[N_ + "ln2_g"])), (shift_[:, :], column(ins[N_ + "ln2_b"])),
                 (gain_rows[:, :], row_broadcast(ins[N_ + "ln2_g"], P)), (shift_rows[:, :], row_broadcast(ins[N_ + "ln2_b"], P)),
                 (coef_bias[:, E:E + 2], row_broadcast(ins[N_ + "coef_b"], P)),
                 (up[:, :, :], ins[N_ + "W1"].rearrange("e h i -> h e i")),
                 (down[:, :, :, :], ins[N_ + "W2"].rearrange("e (c p) h -> p e c h", p=P)),
                 (up_bias[:, :, :], row_broadcast(ins[N_ + "b1"], P)), (down_bias[:, :, :], row_broadcast(ins[N_ + "b2"], P))]
        with nc.Block() as block:
            @block.sync
            def _(sp):
                for to, of in loads:
                    sp.dma_start(to, of).then_inc(loaded, 16)
                sp.wait_ge(loaded, 16 * len(loads))

            @block.vector
            def _(dve):
                dve.memset(coef_bias[:, 0:E], 0.0).then_inc(zeroed, 1)
                dve.wait_ge(zeroed, 1)
        build_rstd(k, "m1_rstd")
        build_prepare(k, m, columns[:, :], (gain, shift_, gain_rows, shift_rows), coef_bias)
        build_route(k, m, None)
        build_dispatch(k, m)
        build_experts(k, m, up, down, up_bias, down_bias)
    with ExitStack() as ctx:
        sb = lambda n, s_, dt=F32: k.sb("m1s_" + n, s_, dt, ctx)
        s_up, s_down = sb("s_up", [P, 512]), sb("s_down", [P, 4, D])
        s_up_bias, s_down_rows = sb("s_up_bias", [P, 4]), sb("s_down_rows", [P, D])
        loaded = k.sem("m1s_loaded")
        copied = k.sem("m1s_copied")
        loads = [(s_up[:, :], ins[N_ + "rW1"]), (s_down[:, :, :], ins[N_ + "rW2"].rearrange("(c p) h -> p c h", p=P)),
                 (s_up_bias[:, :], ins[N_ + "rb1"].rearrange("(c p) -> p c", p=P)), (s_down_rows[:, :], row_broadcast(ins[N_ + "rb2"], P))]
        with nc.Block() as block:
            @block.sync
            def _(sp):
                for to, of in loads:
                    sp.dma_start(to, of, allow_slow_non_contiguous=True).then_inc(loaded, 16)
                sp.wait_ge(loaded, 16 * len(loads))

            @block.vector
            def _(dve):
                dve.tensor_copy(k.coef_shared[:, :], k.coef[:, :, 1]).then_inc(copied, 1)
                dve.wait_ge(copied, 1)
        build_combine(k, m, s_up, s_down, (s_up_bias, s_down_rows), stats=False)


def build_store(k):
    nc, NB = k.nc, k.NB
    stored = k.sem("out_stored")
    with nc.Block() as block:
        @block.sync
        def _(sp):
            for n in range(4):
                q = NB // 4
                sp.dma_start(k.out[n * q:(n + 1) * q].rearrange("b t d -> t b d"), k.x_res[:, n * q:(n + 1) * q, :]).then_inc(stored, 16)
            sp.wait_ge(stored, 64)


def build(nc, ins, out):
    with ExitStack() as ctx:
        k = Kernel(nc, ctx, ins, out)
        build_load(k)
        build_context_attention(k)
        build_rstd(k, "o0")
        build_context_output(k)
        build_rstd(k, "o1")
        build_context_residual(k)
        build_expert_layer_0(k)
        k.retire_semaphores()
        build_rstd(k, "c0")
        build_correlation(k)
        build_roll(k)
        build_rstd(k, "s0", composed=True)
        build_self_attention(k)
        build_expert_layer_1(k)
        build_store(k)
        k.sem_ctx.close()


def kernel(**inputs):
    import numpy as np
    import concourse.bacc as bacc
    from concourse import mybir as mb
    from concourse.bass_utils import run_bass_kernel_spmd as run

    nc = bacc.Bacc("TRN2", target_bir_lowering=False, num_devices=1)
    arrays = {"in_" + n: np.ascontiguousarray(a) for n, a in inputs.items()}
    rows = np.arange(P)
    arrays["in_c_ident"] = np.eye(P, dtype=np.float32)
    arrays["in_c_headmask"] = ((rows[:, None] % QUAD) // DH == np.arange(HQ)).astype(np.float32)
    NB = inputs["x"].shape[0]
    tables = np.concatenate([rows[:, None] < rows, np.tile(np.arange(E), (P, 1)), np.tile(np.arange(2 * NB + E), (P, 1))], 1)
    arrays["in_c_tables"] = tables.astype(np.float32)
    turns = 2 * np.pi * (np.outer(rows, np.concatenate([np.arange(65), np.arange(1, 64)])) % P) / P
    dft = np.where(np.arange(P) < 65, np.cos(turns), np.sin(turns))
    times = np.where((np.arange(P) == 0) | (np.arange(P) == 64), 1.0, 2.0)
    arrays["in_c_dft"] = dft.astype(np.float32)
    arrays["in_c_inverse"] = (dft.T * times[:, None] / P / P).astype(np.float32)
    arrays["in_c_dft_sums"] = np.stack([dft.sum(0), dft[:S2].sum(0)]).astype(np.float32)
    arrays["in_c_flip"] = (rows[:, None] == (-np.arange(2 * P)) % P).astype(np.float32)
    ins = {n[3:]: nc.dram_tensor(n, a.shape, mb.dt.from_np(a.dtype), kind="ExternalInput").ap()
           for n, a in arrays.items()}
    shape = inputs["x"].shape
    out = nc.dram_tensor("out", shape, mb.dt.float32, kind="ExternalOutput").ap()
    build(nc, ins, out)
    r = run(nc, [arrays], core_ids=[0])
    return r.results[0]["out"]
```

```python
from contextlib import ExitStack

import concourse.bass as bass
from concourse import mybir

F32 = mybir.dt.float32
BF16 = mybir.dt.bfloat16
I32 = mybir.dt.int32
ALU = mybir.AluOpType
ACT = mybir.ActivationFunctionType
AX = mybir.AxisListType

P = 128
D = 128
S2 = 120
H = 16
DH = D // H
QUAD = 32
HQ = QUAD // DH
EPS = 1e-5
E = 8
GROUP = 4
SLOT = D + 4


FILL = 8


def filled_slots(NB):
    assert FILL * (NB // 2 - 1) >= 3 * NB + 2 * E
    return FILL * (NB // 2 - 1)


class Kernel:

    def __init__(self, nc, ctx, ins, out):
        self.nc, self.ctx, self.ins, self.out = nc, ctx, ins, out
        self.NB = ins["x"].shape[0]
        self.sems, self.sem_ctx = [], ExitStack()

    def sb(self, name, shape, dt=F32, ctx=None):
        return (ctx or self.ctx).enter_context(self.nc.sbuf_tensor(name, shape, dt))

    def psum(self, name, shape, ctx, dt=F32):
        return ctx.enter_context(self.nc.psum_tensor(name, shape, dt))

    def sem(self, name):
        self.sems.append(self.sem_ctx.enter_context(self.nc.semaphore(name)))
        return self.sems[-1]

    def pool_dma_sem(self, name):
        return self.ctx.enter_context(self.nc.semaphore(name))

    def retire_semaphores(self):
        with self.nc.Block() as block:
            @block.gpsimd
            def _(pool):
                for sem in self.sems:
                    pool.sem_clear(sem)
        self.sem_ctx.close()
        self.sems, self.sem_ctx = [], ExitStack()


def row_broadcast(vector, rows):
    return vector.partition_broadcast(rows)


def column(vector):
    return vector.rearrange("(d one) -> d one", one=1)


class Chain:

    def __init__(self, sem):
        self.sem, self.n = sem, 0

    def __call__(self, eng, op):
        self.n += 1
        op.then_inc(self.sem, 1)
        eng.wait_ge(self.sem, self.n)


def combine_stats(k, dve, link):
    mean_e, m2_e, mean_o, m2_o = (k.stats[:, :, i] for i in (1, 2, 4, 5))
    link(dve, dve.tensor_tensor(k.mean[:, :], mean_e, mean_o, ALU.subtract))
    link(dve, dve.scalar_tensor_tensor(out=k.var[:, :], in0=k.mean[:, :], scalar=0.25, in1=k.mean[:, :],
                                       op0=ALU.mult, op1=ALU.mult))
    link(dve, dve.tensor_tensor(k.mean[:, :], m2_e, m2_o, ALU.add))
    link(dve, dve.scalar_tensor_tensor(out=k.var[:, :], in0=k.mean[:, :], scalar=1.0 / D, in1=k.var[:, :],
                                       op0=ALU.mult, op1=ALU.add))
    link(dve, dve.tensor_tensor(k.mean[:, :], mean_e, mean_o, ALU.add))
    link(dve, dve.tensor_scalar(k.mean[:, :], k.mean[:, :], 0.5, None, ALU.mult))



def build_load(k):
    nc, ins, NB = k.nc, k.ins, k.NB
    k.x_res = k.sb("x_res", [P, NB, D])
    k.tmp_res = k.sb("tmp_res", [P, NB, D])
    k.vo_res = k.sb("vo_res", [P, NB, D])
    k.ident = k.sb("ident", [P, P])
    k.identb = k.sb("identb", [P, P], BF16)
    k.headmask = k.sb("headmask", [P, 2, HQ])
    k.stats = k.sb("stats", [P, NB, 6])
    k.mean = k.sb("mean", [P, NB])
    k.var = k.sb("var", [P, NB])
    k.rstd = k.sb("rstd", [P, NB])
    k.rstd2 = k.sb("rstd2", [P, NB])
    k.logits = k.sb("logits", [P, NB, E + 2])
    k.coef = k.sb("coef", [P, NB, 2])
    k.coef_shared = k.sb("coef_shared", [P, NB])
    k.choice_w = [k.sb(f"choice_w{j}", [P, NB]) for j in range(2)]
    k.place = [k.sb(f"place{j}", [P, NB], I32) for j in range(2)]
    k.slot_expert = k.sb("slot_expert", [P, 2 + 2 * NB + E + 2], I32)
    k.tables = k.sb("tables", [P, P + E + 2 * NB + E])
    k.zeros = k.sb("zeros", [P, P])
    k.slots = nc.dram_tensor("slots", [filled_slots(NB) * P, SLOT], F32).ap()
    k.results = nc.dram_tensor("results", [(filled_slots(NB) + 2 * NB) * P, D], F32).ap()
    k.fill_rows = k.sb("fill_rows", [P, filled_slots(NB)])
    k.token_rows = k.sb("token_rows", [P, 2, NB])
    k.xf_dram = nc.dram_tensor("xf_dram", [NB * P, D], F32).ap()
    k.circulant = nc.dram_tensor("circulant", [NB, 2 * P], F32).ap()
    k.w = {}
    for name in ("L0_xattn_Wq", "L0_xattn_Wk1", "L0_xattn_Wk2", "L0_xattn_Wv1", "L0_xattn_Wv2", "L0_xattn_Wo",
                 "L1_xattn_Wv", "L1_xattn_Wo"):
        k.w[name] = k.sb(name, [P, D])
    cols = ("L0_xattn_bq", "L0_xattn_bk1", "L0_xattn_bk2", "L0_xattn_bo", "L0_xattn_g0", "L0_xattn_beta0", "L1_xattn_bv")
    for name in cols:
        k.w[name] = k.sb(name, [P, 1])
    k.v_bias = k.sb("v_bias", [P, 2 * D])
    k.g1_rows = k.sb("g1_rows", [P, D])
    k.beta1_rows = k.sb("beta1_rows", [P, D])
    k.wvo = k.sb("wvo", [P, D])
    k.bvo = k.sb("bvo", [P, D])
    wv_t = k.sb("wv_t", [P, D])
    bv_wide = k.sb("bv_wide", [P, P])

    x_loaded = [k.sem(f"x_loaded{n}") for n in range(4)]
    weights_loaded = k.sem("weights_loaded")
    stats_done = k.sem("stats_done")
    chain = Chain(k.sem("load_chain"))
    ident_cast = k.sem("ident_cast")
    eps_added = k.sem("eps_added")
    root_done = k.sem("root_done")
    zeros_set = k.sem("zeros_set")
    wv_turned = k.sem("wv_turned")
    wv_copied = k.sem("wv_copied")
    wvo_product = k.sem("wvo_product")
    PARTS = 4
    per = NB // PARTS
    loads = [(k.token_rows[:, :, :], ins["c_token_rows"]), (k.fill_rows, ins["c_fill_rows"]), (k.ident, ins["c_ident"]), (k.headmask, ins["c_headmask"]), (k.tables, ins["c_tables"])]
    loads += [(k.w[n], ins[n]) for n in k.w if n not in cols]
    loads += [(k.w[n], column(ins[n])) for n in cols]
    loads += [(k.v_bias[:, 0:D], row_broadcast(ins["L0_xattn_bv1"], P)),
              (k.v_bias[:, D:2 * D], row_broadcast(ins["L0_xattn_bv2"], P)),
              (k.g1_rows[:, :], row_broadcast(ins["L0_xattn_g1"], P)),
              (k.beta1_rows[:, :], row_broadcast(ins["L0_xattn_beta1"], P))]

    with ExitStack() as ctx:
        turn = k.psum("load_turn", [P, 512], ctx)
        prod = k.psum("load_prod", [P, 512], ctx)
        block = ctx.enter_context(nc.Block())

        @block.sync
        def _(sp):
            for n in range(PARTS):
                sp.dma_start(k.x_res[:, n * per:(n + 1) * per, :],
                             ins["x"][n * per:(n + 1) * per].rearrange("b t d -> t b d")).then_inc(x_loaded[n], 16)

        @block.scalar
        def _(act):
            for to, of in loads:
                act.dma_start(to if isinstance(to, bass.AP) else to[:, :], of).then_inc(weights_loaded, 16)
            act.wait_ge(eps_added, 1)
            act.activation(k.rstd[:, :], k.rstd[:, :], ACT.Sqrt).then_inc(root_done, 1)

        @block.gpsimd
        def _(pool):
            pool.memset(k.zeros[:, :], 0.0).then_inc(zeros_set, 1)
            pool.wait_ge(zeros_set, 1)

        @block.tensor
        def _(pe):
            pe.wait_ge(weights_loaded, 16 * len(loads))
            pe.transpose(turn[:, 0:D], k.w["L1_xattn_Wv"][:, :], k.ident[:, :]).then_inc(wv_turned, 1)
            pe.wait_ge(wv_copied, 2)
            pe.matmul(prod[:, 0:D], wv_t[:, :], k.w["L1_xattn_Wo"][:, :], start=True, stop=True)
            pe.matmul(prod[:, D:2 * D], bv_wide[:, :], k.w["L1_xattn_Wo"][:, :],
                      start=True, stop=True).then_inc(wvo_product, 1)

        @block.vector
        def _(dve):
            dve.wait_ge(weights_loaded, 16 * len(loads))
            dve.tensor_copy(k.identb[:, :], k.ident[:, :]).then_inc(ident_cast, 1)
            dve.memset(k.slot_expert[:, :], 0).then_inc(ident_cast, 1)
            dve.tensor_copy(bv_wide[:, :], k.w["L1_xattn_bv"][:, 0:1].broadcast_to([P, P])).then_inc(wv_copied, 1)
            dve.wait_ge(wv_turned, 1)
            dve.tensor_copy(wv_t[:, :], turn[:, 0:D]).then_inc(wv_copied, 1)
            for n in range(PARTS):
                dve.wait_ge(x_loaded[n], 16)
                with dve.Fori(n * per // GROUP, (n + 1) * per // GROUP) as g:
                    for m in range(GROUP):
                        dve.bn_stats(k.stats[:, GROUP * g + m, :], k.x_res[:, GROUP * g + m, :]).then_inc(stats_done, 1)
            dve.wait_ge(stats_done, NB)
            dve.wait_ge(wvo_product, 1)
            dve.tensor_copy(k.wvo[:, :], prod[:, 0:D]).then_inc(ident_cast, 1)
            dve.tensor_copy(k.bvo[:, :], prod[:, D:2 * D]).then_inc(ident_cast, 1)
            combine_stats(k, dve, chain)
            dve.tensor_scalar(k.rstd[:, :], k.var[:, :], EPS, None, ALU.add).then_inc(eps_added, 1)
            dve.wait_ge(root_done, 1)
            dve.reciprocal(k.rstd[:, :], k.rstd[:, :]).then_inc(ident_cast, 1)
            dve.wait_ge(ident_cast, 5)



def build_context_attention(k):
    nc, ins, NB, w = k.nc, k.ins, k.NB, k.w
    W = HQ * P
    CH = 4
    HC = H // 2
    HALF = 2 * CH
    with ExitStack() as ctx:
        sb = lambda n, s, dt=F32: k.sb(n, s, dt, ctx)
        ctx_in = [sb(f"ctx_in{p}", [P, D]) for p in range(2)]
        xn = [sb(f"xn{p}", [P, D]) for p in range(2)]
        xc_t = [sb(f"xc_t{p}", [P, 2 * P]) for p in range(2)]
        q_t = [sb(f"q_t{p}", [P, P]) for p in range(2)]
        k_t = [sb(f"k_t{p}", [P, 2, S2]) for p in range(2)]
        q_wide = [sb(f"q_wide{p}", [P, HQ, P]) for p in range(2)]
        v_sb = [sb(f"v_sb{p}", [P, 2 * D]) for p in range(2)]
        v_heads = [sb(f"v_heads{p}", [P, 2, H, QUAD]) for p in range(2)]
        probs = [sb(f"probs{p}", [P, 2, H, P]) for p in range(2)]
        maxima = sb("maxima", [P, 4, HQ], BF16)
        sums = sb("sums", [P, 2, HC])
        rsums = sb("rsums", [P, 4, HC])
        q_keep = [sb(f"q_keep{p}", [P, P]) for p in range(2)]
        fill = sb("fill", [P, FILL, SLOT])
        o_t = sb("o_t", [P, P])

        scores = [k.psum(f"scores{i}", [P, 2, W], ctx) for i in range(2)]
        turned = k.psum("turned", [P, 512], ctx)
        qk = k.psum("qk", [P, 512], ctx)
        vv = k.psum("vv", [P, 512], ctx)
        pv = k.psum("pv", [P, 512], ctx)

        s = {n: k.sem("a_" + n) for n in
             ("zeroed", "xn_ready", "turned", "xc_ready", "qk_done", "q_ready", "wide_ready",
              "v_done", "v_ready", "vo_ready", "scores_done", "max_ready", "shifted", "probs_ready", "sums_ready",
              "rsums_ready", "v_heads_ready", "pv_part", "pv_done", "q_kept", "o_ready", "o_turned", "out_ready", "stats")}
        ctx_loaded = [k.sem(f"a_ctx_loaded{p}") for p in range(2)]
        fill_go, fill_ready, filled = k.sem("a_fill_go"), k.sem("a_fill_ready"), k.pool_dma_sem("a_filled")
        block = ctx.enter_context(nc.Block())

        def all_sequences(eng, step, last):
            for b in (0, 1):
                step(b, b % 2)
            with eng.Fori(1, NB // 2 - 1) as i:
                for p in (0, 1):
                    step(2 * i + p, p)
            for b in (NB - 2, NB - 1):
                step(b, b % 2)
            last()

        def is_(b, n):
            return isinstance(b, int) and b == n

        def bank(i):
            return scores[i // 2 % 2][0:S2, i % 2, :]

        @block.sync
        def _(sp):
            def step(b, p):
                if not (isinstance(b, int) and b < 2):
                    sp.wait_ge(s["turned"], b - 1)
                sp.dma_start(ctx_in[p][0:S2, :], ins["ctx_1024"][b]).then_inc(ctx_loaded[p], 16)
            all_sequences(sp, step, lambda: None)

        @block.tensor
        def _(pe):
            def turn_inputs(b, p):
                pe.wait_ge(s["xn_ready"], b + 1)
                pe.wait_ge(ctx_loaded[p], 8 * (b - p) + 16)
                pe.wait_ge(s["xc_ready"], b)
                pe.transpose(turned[:, 0:P], xn[p][:, :], k.ident[:, :])
                pe.transpose(turned[:, P:P + S2], ctx_in[p][0:S2, :], k.ident[0:S2, 0:S2]).then_inc(s["turned"], 1)

            def project(b, p):
                pe.wait_ge(s["xc_ready"], b + 1)
                pe.wait_ge(s["q_ready"], b)
                c_t = xc_t[p][:, P:P + S2]
                pe.matmul(qk[:, 0:P], w["L0_xattn_Wq"][:, :], xc_t[p][:, 0:P], start=True, stop=True)
                pe.matmul(qk[:, P:P + S2], w["L0_xattn_Wk1"][:, :], c_t, start=True, stop=True)
                pe.matmul(qk[:, 2 * P:2 * P + S2], w["L0_xattn_Wk2"][:, :], c_t,
                          start=True, stop=True).then_inc(s["qk_done"], 1)

            def values(b, p):
                pe.wait_ge(s["q_ready"], b + 1)
                pe.wait_ge(s["vo_ready"], b)
                if not early(b, 3):
                    pe.wait_ge(s["out_ready"], b - 2)
                pe.matmul(vv[0:S2, 0:D], k_t[p][:, 0, :], w["L0_xattn_Wv1"][:, :], start=True, stop=True)
                pe.matmul(vv[0:S2, D:2 * D], k_t[p][:, 1, :], w["L0_xattn_Wv2"][:, :], start=True, stop=True)
                pe.matmul(vv[0:S2, 2 * D:3 * D], xc_t[p][:, P:P + S2], k.wvo[:, :],
                          start=True, stop=True).then_inc(s["v_done"], 1)

            def score(b, p, i):
                if i == 0:
                    pe.wait_ge(s["wide_ready"], b + 1)
                if not (is_(b, 0) and i < 4):
                    pe.wait_ge(s["probs_ready"], HALF * b + i - 3)
                q0 = QUAD * (i % 4)
                pe.matmul(bank(i), k_t[p][q0:q0 + QUAD, i // 4, :], q_wide[p][q0:q0 + QUAD, :, :],
                          start=True, stop=True).then_inc(s["scores_done"], 1)

            def shift(b, i):
                pe.wait_ge(s["max_ready"], HALF * b + i + 1)
                pe.matmul(bank(i), k.identb[0:S2, 0:S2],
                          maxima[0:S2, i % 4, :].unsqueeze(2).broadcast_to([S2, HQ, P]),
                          start=False, stop=True, skip_group_check=True).then_inc(s["shifted"], 1)

            def weigh(b, p, part):
                if part == 0:
                    pe.wait_ge(s["o_ready"], b)
                pe.wait_ge(s["v_heads_ready"], CH * b + part // 2 * 2 + 2)
                for n in (2 * part, 2 * part + 1):
                    for j in range(H // HQ):
                        h = HQ * j + n % HQ
                        mm = pe.matmul(pv[QUAD * j:QUAD * (j + 1), 0:P], v_heads[p][0:S2, n // HQ, h, :],
                                       probs[p][0:S2, n // HQ, h, :], start=(n == 0), stop=(n == 2 * HQ - 1))
                mm.then_inc(s["pv_done"] if part == 3 else s["pv_part"], 1)

            def turn_output(b):
                pe.wait_ge(s["o_ready"], b + 1)
                if is_(b, NB - 2) or is_(b, NB - 1):
                    pe.wait_ge(s["vo_ready"], NB)
                else:
                    pe.wait_ge(s["vo_ready"], b + 3)
                pe.wait_ge(s["out_ready"], b)
                pe.transpose(vv[:, 3 * D:4 * D], o_t[:, :], k.ident[:, :]).then_inc(s["o_turned"], 1)

            def step(b, p):
                last, first = is_(b, NB - 1), is_(b, 0)
                for i in range(HALF):
                    if i + 2 < HALF:
                        score(b, p, i + 2)
                    elif not last:
                        score(b + 1, 1 - p, i + 2 - HALF)
                    shift(b, i)
                    if i == 0 and not last:
                        turn_inputs(b + 1, 1 - p)
                    if i == 2 and not last:
                        project(b + 1, 1 - p)
                    if i == 2 and not (first or is_(b, 1)):
                        turn_output(b - 2)
                    if i == 5 and not last:
                        values(b + 1, 1 - p)
                    if i % 2 == 1 and not first:
                        weigh(b - 1, 1 - p, i // 2)

            def last():
                turn_output(NB - 2)
                for part in range(4):
                    weigh(NB - 1, 1, part)
                turn_output(NB - 1)

            turn_inputs(0, 0)
            project(0, 0)
            values(0, 0)
            score(0, 0, 0)
            score(0, 0, 1)
            for _ in range(8):
                pe.matmul(pv[:, :], k.identb[:, :], k.identb[:, :].unsqueeze(1).broadcast_to([P, 4, P]), start=True, stop=True)
            all_sequences(pe, step, last)

        @block.scalar
        def _(act):
            def copy_turned(b, p):
                pe_done = s["turned"]
                act.wait_ge(pe_done, b + 1)
                if not (isinstance(b, int) and b < 2):
                    act.wait_ge(s["v_done"], b - 1)
                act.activation(xc_t[p][:, 0:P], turned[:, 0:P], ACT.Copy)
                act.activation(xc_t[p][:, P:P + S2], turned[:, P + S2 - 1:P - 1:-1], ACT.Copy).then_inc(s["xc_ready"], 1)

            def bias_qk(b, p):
                act.wait_ge(s["qk_done"], b + 1)
                if not (isinstance(b, int) and b < 2):
                    act.wait_ge(s["scores_done"], HALF * b - HALF)
                    act.wait_ge(s["v_done"], b - 1)
                    act.wait_ge(s["wide_ready"], b - 1)
                    act.wait_ge(s["q_kept"], b - 1)
                act.activation(q_t[p][:, :], qk[:, 0:P], ACT.Identity, bias=w["L0_xattn_bq"][:, 0:1])
                act.activation(k_t[p][:, 0, :], qk[:, P:P + S2], ACT.Identity, bias=w["L0_xattn_bk1"][:, 0:1])
                act.activation(k_t[p][:, 1, :], qk[:, 2 * P:2 * P + S2], ACT.Identity,
                               bias=w["L0_xattn_bk2"][:, 0:1]).then_inc(s["q_ready"], 1)

            def exponent(b, p, i):
                act.wait_ge(s["shifted"], HALF * b + i + 1)
                if i == 0 and not (isinstance(b, int) and b < 2):
                    act.wait_ge(s["pv_done"], b - 1)
                h0 = HQ * (i % 4)
                act.activation(probs[p][0:S2, i // 4, h0:h0 + HQ, :].rearrange("p h q -> p (h q)"), bank(i),
                               ACT.Exp).then_inc(s["probs_ready"], 1)

            def step(b, p):
                last = is_(b, NB - 1)
                for i in range(HALF):
                    exponent(b, p, i)
                    if i == 0 and not last:
                        copy_turned(b + 1, 1 - p)
                    if i == 3 and not last:
                        bias_qk(b + 1, 1 - p)

            copy_turned(0, 0)
            bias_qk(0, 0)
            all_sequences(act, step, lambda: None)

        @block.gpsimd
        def _(pool):
            def spread(b, p):
                pool.wait_ge(s["q_ready"], b + 1)
                if not (isinstance(b, int) and b < 2):
                    pool.wait_ge(s["scores_done"], HALF * b - HALF)
                pool.tensor_tensor(q_wide[p][:, :, :], q_t[p][:, :].unsqueeze(1).broadcast_to([P, HQ, P]),
                                   k.headmask[:, 0, :].unsqueeze(2).broadcast_to([P, HQ, P]),
                                   ALU.mult).then_inc(s["wide_ready"], 1)

            def scale_values(b, p, c):
                pool.wait_ge(s["rsums_ready"], CH * b + c + 1)
                if c == 0:
                    pool.wait_ge(s["v_ready"], b + 1)
                    if not (isinstance(b, int) and b < 2):
                        pool.wait_ge(s["pv_done"], b - 1)
                for j in range(2):
                    jj = 2 * (c % 2) + j
                    own = v_heads[p][0:S2, c // 2, HQ * jj:HQ * (jj + 1), :].rearrange("p h c -> p (h c)")
                    own = own.rearrange("p (h c) -> p h c", c=QUAD)
                    v0 = D * (c // 2) + QUAD * jj
                    t = v_heads[p][0:S2, c // 2, HQ * jj:HQ * (jj + 1), :]
                    diag = bass.AP(tensor=t.tensor, offset=t.offset,
                                   ap=[list(t.ap[0]), [QUAD + DH, HQ], [1, DH]])
                    op = pool.tensor_tensor(
                        diag, v_sb[p][0:S2, v0:v0 + QUAD].rearrange("p (h d) -> p h d", d=DH),
                        rsums[0:S2, c, HQ * j:HQ * (j + 1)].unsqueeze(2).broadcast_to([S2, HQ, DH]), ALU.mult)
                op.then_inc(s["v_heads_ready"], 1)

            def keep_queries(b, p):
                if not early(b):
                    pool.wait_ge(s["o_ready"], b - 1)
                pool.tensor_tensor(q_keep[p][:, :], q_t[p][:, :], k.zeros[:, 0:P], ALU.add).then_inc(s["q_kept"], 1)

            def fill_slots(b):
                if not is_(b, 0):
                    pool.wait_ge(filled, 8 * b)
                pool.sem_inc(fill_go, 1)
                pool.tensor_copy(fill[:, :, D], k.fill_rows[:, bass.ds(b * (FILL // 2), FILL)]).then_inc(fill_ready, 2)
                pool.wait_ge(fill_ready, b + 2)
                pool.dma_start(k.slots[bass.ds(b * (FILL * P // 2), FILL * P), :].rearrange("(p r) d -> p (r d)", p=P),
                               fill[:, :, :].rearrange("p r d -> p (r d)")).then_inc(filled, 16)

            def step(b, p):
                last = is_(b, NB - 1)
                if not is_(b, 0):
                    scale_values(b - 1, 1 - p, 3)
                    keep_queries(b - 1, 1 - p)
                if not isinstance(b, int) and p == 0:
                    fill_slots(b)
                if not last:
                    spread(b + 1, 1 - p)
                scale_values(b, p, 0)
                scale_values(b, p, 1)
                scale_values(b, p, 2)

            for p in range(2):
                pool.memset(v_heads[p][:, :, :, :], 0.0).then_inc(s["zeroed"], 1)
            pool.memset(fill[:, :, :], 0.0).then_inc(s["zeroed"], 1)
            pool.wait_ge(s["zeroed"], 3)
            spread(0, 0)
            fill_slots(0)
            def last():
                scale_values(NB - 1, 1, 3)
                keep_queries(NB - 1, 1)
                pool.wait_ge(filled, 16 * (NB // 2 - 1))
            all_sequences(pool, step, last)

        @block.vector
        def _(dve):
            def normalise(b, p):
                if not (isinstance(b, int) and b < 2):
                    dve.wait_ge(s["turned"], b - 1)
                dve.tensor_scalar(xn[p][:, :], k.x_res[:, b, :], k.mean[:, bass.ds(b, 1)], k.rstd[:, bass.ds(b, 1)],
                                  ALU.subtract, ALU.mult).then_inc(s["xn_ready"], 1)

            def bias_values(b, p):
                dve.wait_ge(s["v_done"], b + 1)
                if not (isinstance(b, int) and b < 2):
                    dve.wait_ge(s["v_heads_ready"], CH * b - CH)
                dve.tensor_tensor(v_sb[p][0:S2, :], vv[0:S2, 0:2 * D], k.v_bias[0:S2, :],
                                  ALU.add).then_inc(s["v_ready"], 1)
                dve.tensor_tensor(k.vo_res[0:S2, b, :], vv[0:S2, 2 * D:3 * D], k.bvo[0:S2, :],
                                  ALU.add).then_inc(s["vo_ready"], 1)

            def maximum(b, i):
                dve.wait_ge(s["scores_done"], HALF * b + i + 1)
                if not (is_(b, 0) and i < 4):
                    dve.wait_ge(s["shifted"], HALF * b + i - 3)
                dve.tensor_reduce(maxima[0:S2, i % 4, :], bank(i).rearrange("p (h q) -> p h q", q=P),
                                  AX.X, ALU.max, negate=True).then_inc(s["max_ready"], 1)

            def total(b, p, c):
                dve.wait_ge(s["probs_ready"], HALF * b + 2 * c + 2)
                h0 = HC * (c % 2)
                dve.tensor_reduce(sums[0:S2, c % 2, :], probs[p][0:S2, c // 2, h0:h0 + HC, :],
                                  AX.X, ALU.add).then_inc(s["sums_ready"], 1)
                dve.wait_ge(s["sums_ready"], CH * b + c + 1)
                if not is_(b, 0):
                    dve.wait_ge(s["v_heads_ready"], CH * b + c - CH + 1)
                dve.reciprocal(rsums[0:S2, c, :], sums[0:S2, c % 2, :]).then_inc(s["rsums_ready"], 1)

            def add_queries(b, p):
                dve.wait_ge(s["pv_done"], b + 1)
                dve.wait_ge(s["o_turned"], b)
                dve.wait_ge(s["q_kept"], b + 1)
                dve.tensor_tensor(o_t[:, :], pv[:, 0:P], q_keep[p][:, :], ALU.add).then_inc(s["o_ready"], 1)

            def keep_output(b):
                dve.wait_ge(s["o_turned"], b + 1)
                dve.bn_stats(k.stats[:, b, :], vv[:, 3 * D:4 * D]).then_inc(s["stats"], 1)
                dve.tensor_copy(k.tmp_res[:, b, :], vv[:, 3 * D:4 * D]).then_inc(s["out_ready"], 1)

            def step(b, p):
                first, last = is_(b, 0), is_(b, NB - 1)
                old = not (first or is_(b, 1))
                maximum(b, 0)
                maximum(b, 1)
                if old:
                    add_queries(b - 2, p)
                if not first:
                    total(b - 1, 1 - p, 3)
                if not (last or is_(b, NB - 2)):
                    normalise(b + 2, p)
                maximum(b, 2)
                maximum(b, 3)
                total(b, p, 0)
                if old:
                    keep_output(b - 2)
                maximum(b, 4)
                maximum(b, 5)
                total(b, p, 1)
                maximum(b, 6)
                maximum(b, 7)
                total(b, p, 2)
                if not last:
                    bias_values(b + 1, 1 - p)

            def last():
                total(NB - 1, 1, 3)
                add_queries(NB - 2, 0)
                keep_output(NB - 2)
                add_queries(NB - 1, 1)
                keep_output(NB - 1)
                dve.wait_ge(s["out_ready"], NB)
                dve.wait_ge(s["stats"], NB)

            normalise(0, 0)
            normalise(1, 1)
            bias_values(0, 0)
            all_sequences(dve, step, last)



def build_rstd(k, name, composed=False):
    nc = k.nc
    link = Chain(k.sem(name + "_chain"))
    eps_added = k.sem(name + "_eps_added")
    root_done = k.sem(name + "_root_done")
    with nc.Block() as block:
        @block.scalar
        def _(act):
            act.wait_ge(eps_added, 1)
            act.activation(k.rstd[:, :], k.rstd[:, :], ACT.Sqrt).then_inc(root_done, 1)
            if composed:
                act.wait_ge(eps_added, 2)
                act.activation(k.rstd2[:, :], k.rstd2[:, :], ACT.Sqrt).then_inc(root_done, 1)

        @block.vector
        def _(dve):
            combine_stats(k, dve, link)
            dve.tensor_scalar(k.rstd[:, :], k.var[:, :], EPS, None, ALU.add).then_inc(eps_added, 1)
            dve.wait_ge(root_done, 1)
            link(dve, dve.reciprocal(k.rstd[:, :], k.rstd[:, :]))
            if composed:
                link(dve, dve.tensor_tensor(k.rstd2[:, :], k.rstd[:, :], k.rstd[:, :], ALU.mult))
                link(dve, dve.tensor_tensor(k.rstd2[:, :], k.rstd2[:, :], k.var[:, :], ALU.mult))
                dve.tensor_scalar(k.rstd2[:, :], k.rstd2[:, :], EPS, None, ALU.add).then_inc(eps_added, 1)
                dve.wait_ge(root_done, 2)
                link(dve, dve.reciprocal(k.rstd2[:, :], k.rstd2[:, :]))


def normalise_group(k, dve, to, of, g, rstd, done):
    for n in range(GROUP):
        b = GROUP * g + n
        dve.tensor_scalar(to[:, n, :], of[:, b, :], k.mean[:, bass.ds(b, 1)], rstd[:, bass.ds(b, 1)],
                          ALU.subtract, ALU.mult).then_inc(done, 1)


def group_of(tensor, g):
    return tensor[:, bass.ds(GROUP * g, GROUP), :]


def all_groups(eng, NB, step, peel=2):
    NG = NB // GROUP
    for g in range(peel):
        step(g, g % 2)
    if NG > peel:
        with eng.Fori(peel // 2, NG // 2) as i:
            for p in (0, 1):
                step(2 * i + p, p)


def early(g, n=2):
    return isinstance(g, int) and g < n



def build_context_output(k):
    nc, NB, w = k.nc, k.NB, k.w
    N = GROUP * D
    with ExitStack() as ctx:
        sb = lambda n, s, dt=F32: k.sb(n, s, dt, ctx)
        normed = [sb(f"normed{p}", [P, GROUP, D]) for p in range(2)]
        o_t = [sb(f"out_t{p}", [P, N]) for p in range(2)]
        r_t = [sb(f"relu_t{p}", [P, N]) for p in range(2)]
        turned = [k.psum(f"bo_turned{p}", [P, N], ctx) for p in range(2)]
        product = [k.psum(f"bo_product{p}", [P, N], ctx) for p in range(2)]
        back = [k.psum(f"bo_back{p}", [P, N], ctx) for p in range(2)]
        s = {n: k.sem("o_" + n) for n in ("normed", "turned", "affine", "product", "relu", "sum", "back", "kept", "stats")}
        block = ctx.enter_context(nc.Block())

        @block.tensor
        def _(pe):
            def turn(g, p):
                pe.wait_ge(s["normed"], GROUP * (g + 1))
                if not early(g):
                    pe.wait_ge(s["affine"], g - 1)
                for n in range(GROUP):
                    mm = pe.transpose(turned[p][:, n * P:(n + 1) * P], normed[p][:, n, :], k.ident[:, :])
                mm.then_inc(s["turned"], 1)

            def multiply(g, p):
                pe.wait_ge(s["affine"], g + 1)
                if not early(g):
                    pe.wait_ge(s["relu"], g - 1)
                pe.matmul(product[p][:, :], w["L0_xattn_Wo"][:, :], o_t[p][:, :], start=True, stop=True).then_inc(s["product"], 1)

            def turn_back(g, p):
                pe.wait_ge(s["sum"], g + 1)
                if not early(g):
                    pe.wait_ge(s["kept"], g - 1)
                    pe.wait_ge(s["stats"], GROUP * (g - 1))
                for n in range(GROUP):
                    mm = pe.transpose(back[p][:, n * P:(n + 1) * P], r_t[p][:, n * P:(n + 1) * P], k.ident[:, :])
                mm.then_inc(s["back"], 1)

            def step(g, p):
                turn(g, p)
                if not early(g, 1):
                    multiply(g - 1, 1 - p)
                if not early(g):
                    turn_back(g - 2, p)
            all_groups(pe, NB, step, peel=4)
            NG = NB // GROUP
            multiply(NG - 1, 1)
            turn_back(NG - 2, 0)
            turn_back(NG - 1, 1)

        @block.scalar
        def _(act):
            def step(g, p):
                act.wait_ge(s["turned"], g + 1)
                if not early(g):
                    act.wait_ge(s["sum"], g - 1)
                act.activation(o_t[p][:, :], turned[p][:, :], ACT.Identity, bias=w["L0_xattn_beta0"][:, 0:1],
                               scale=w["L0_xattn_g0"][:, 0:1]).then_inc(s["affine"], 1)
                if not early(g, 1):
                    relu(g - 1, 1 - p)

            def relu(g, p):
                act.wait_ge(s["product"], g + 1)
                if not early(g):
                    act.wait_ge(s["back"], g - 1)
                act.activation(r_t[p][:, :], product[p][:, :], ACT.Relu,
                               bias=w["L0_xattn_bo"][:, 0:1]).then_inc(s["relu"], 1)
            all_groups(act, NB, step)
            relu(NB // GROUP - 1, 1)

        @block.gpsimd
        def _(pool):
            def step(g, p):
                pool.wait_ge(s["relu"], g + 1)
                pool.tensor_tensor(r_t[p][:, :], r_t[p][:, :], o_t[p][:, :], ALU.add).then_inc(s["sum"], 1)
            all_groups(pool, NB, step)

        @block.vector
        def _(dve):
            def step(g, p):
                if not early(g):
                    dve.wait_ge(s["turned"], g - 1)
                normalise_group(k, dve, normed[p], k.tmp_res, g, k.rstd, s["normed"])
                if not early(g, 3):
                    finish(g - 3, 1 - p)

            def finish(g, p):
                dve.wait_ge(s["back"], g + 1)
                for n in range(GROUP):
                    dve.bn_stats(k.stats[:, GROUP * g + n, :], back[p][:, n * P:(n + 1) * P]).then_inc(s["stats"], 1)
                dve.tensor_copy(group_of(k.tmp_res, g), back[p][:, :].rearrange("p (n d) -> p n d", d=D)).then_inc(s["kept"], 1)
            all_groups(dve, NB, step, peel=4)
            finish(NB // GROUP - 3, 1)
            finish(NB // GROUP - 2, 0)
            finish(NB // GROUP - 1, 1)
            dve.wait_ge(s["kept"], NB // GROUP)


def build_context_residual(k):
    nc, NB = k.nc, k.NB
    RING, NG = 4, NB // GROUP
    with ExitStack() as ctx:
        normed = [k.sb(f"r_normed{p}", [P, GROUP, D], F32, ctx) for p in range(RING)]
        s = {n: k.sem("r_" + n) for n in ("normed", "scaled", "moved", "added", "stats")}
        block = ctx.enter_context(nc.Block())

        def each(eng, step):
            for p in range(RING):
                step(p, p)
            with eng.Fori(1, NG // RING) as i:
                for p in range(RING):
                    step(RING * i + p, p)

        def rows(t):
            return t[:, :].unsqueeze(1).broadcast_to([P, GROUP, D])

        @block.gpsimd
        def _(pool):
            def step(g, p):
                pool.wait_ge(s["normed"], GROUP * (g + 1))
                pool.tensor_tensor(normed[p][:, :, :], normed[p][:, :, :], rows(k.g1_rows), ALU.mult).then_inc(s["scaled"], 1)
                pool.wait_ge(s["scaled"], g + 1)
                pool.tensor_tensor(normed[p][:, :, :], normed[p][:, :, :], rows(k.beta1_rows), ALU.add).then_inc(s["moved"], 1)
            each(pool, step)

        @block.vector
        def _(dve):
            def step(g, p):
                if not early(g, RING):
                    dve.wait_ge(s["added"], g - RING + 1)
                normalise_group(k, dve, normed[p], k.tmp_res, g, k.rstd, s["normed"])
                if not early(g):
                    finish(g - 2, (p - 2) % RING)

            def finish(g, p):
                dve.wait_ge(s["moved"], g + 1)
                dve.tensor_tensor(group_of(k.x_res, g), group_of(k.x_res, g), normed[p][:, :, :], ALU.add).then_inc(s["added"], 1)
                dve.wait_ge(s["added"], g + 1)
                for n in range(GROUP):
                    dve.bn_stats(k.stats[:, GROUP * g + n, :], k.x_res[:, GROUP * g + n, :]).then_inc(s["stats"], 1)
            each(dve, step)
            finish(NG - 2, RING - 2)
            finish(NG - 1, RING - 1)
            dve.wait_ge(s["stats"], NB)



class Experts:

    def __init__(self, name, inner, down_chunks, top, act):
        self.name, self.inner, self.chunks, self.top, self.act = name, inner, down_chunks, top, act

    def first_slot(self, NB):
        return 0 if self.top == 2 else 2 * NB + E

    def results_row(self, NB, j):
        return (filled_slots(NB) + j * NB) * P

    def tiles(self, NB):
        return self.top * NB + E


def build_prepare(k, m, columns, affine, gate_bias, weights):
    nc, NB = k.nc, k.NB
    n_cols = columns.shape[1]
    source = k.tmp_res if affine else k.x_res
    NG = NB // GROUP
    with ExitStack() as ctx:
        sb = lambda n, s_, dt=F32: k.sb(m.name + n, s_, dt, ctx)
        xn = [sb(f"pn{p}", [P, GROUP, D]) for p in range(2)]
        xa = [sb(f"pa{p}", [P, GROUP, D]) for p in range(2)] if affine else xn
        x_t = [sb(f"pt{p}", [P, GROUP, P]) for p in range(2)]
        turned = [k.psum(f"{m.name}pturn{p}", [P, GROUP, P], ctx) for p in range(2)]
        logit = [k.psum(f"{m.name}plogit{p}", [P, 512], ctx) for p in range(2)]
        s = {n: k.sem(m.name + "p_" + n) for n in ("normed", "scaled", "moved", "turned", "copied", "logits", "kept", "logits_kept")}
        stored = [k.sem(f"{m.name}p_stored{p}") for p in range(2)]
        block = ctx.enter_context(nc.Block())

        @block.sync
        def _(sp):
            def step(g, p):
                if affine:
                    sp.wait_ge(s["moved"], g + 1)
                else:
                    sp.wait_ge(s["normed"], GROUP * (g + 1))
                sp.dma_start(k.xf_dram[bass.ds(g * (GROUP * P), GROUP * P), :].rearrange("(n t) d -> t n d", t=P),
                             xa[p][:, :, :]).then_inc(stored[p], 16)
            all_groups(sp, NB, step)
            for p in range(2):
                sp.wait_ge(stored[p], 8 * NG)
            sp.wait_ge(*weights)

        @block.tensor
        def _(pe):
            def logits(g, p):
                pe.wait_ge(s["copied"], g + 1)
                if not early(g):
                    pe.wait_ge(s["logits_kept"], g - 1)
                for n in range(GROUP):
                    mm = pe.matmul(logit[p][:, n * n_cols:(n + 1) * n_cols], x_t[p][:, n, :], columns, start=True, stop=True)
                mm.then_inc(s["logits"], 1)

            def step(g, p):
                pe.wait_ge(s["normed"], GROUP * (g + 1))
                if not early(g):
                    pe.wait_ge(s["copied"], g - 1)
                for n in range(GROUP):
                    mm = pe.transpose(turned[p][:, n, :], xn[p][:, n, :], k.ident[:, :])
                mm.then_inc(s["turned"], 1)
                if not early(g, 1):
                    logits(g - 1, 1 - p)
            all_groups(pe, NB, step)
            logits(NG - 1, 1)

        @block.scalar
        def _(act):
            def step(g, p):
                act.wait_ge(s["turned"], g + 1)
                if not early(g):
                    act.wait_ge(s["logits"], g - 1)
                    act.wait_ge(s["kept"], g - 1)
                if affine:
                    act.activation(x_t[p][:, :, :], turned[p][:, :, :], ACT.Identity, bias=affine[1][:, 0:1],
                                   scale=affine[0][:, 0:1]).then_inc(s["copied"], 1)
                else:
                    act.activation(x_t[p][:, :, :], turned[p][:, :, :], ACT.Copy).then_inc(s["copied"], 1)
            all_groups(act, NB, step)

        if affine:
            @block.gpsimd
            def _(pool):
                def rows(t):
                    return t[:, :].unsqueeze(1).broadcast_to([P, GROUP, D])

                def step(g, p):
                    pool.wait_ge(s["normed"], GROUP * (g + 1))
                    if not early(g):
                        pool.wait_ge(stored[p], 8 * (g - p))
                    pool.tensor_tensor(xa[p][:, :, :], xn[p][:, :, :], rows(affine[2]), ALU.mult).then_inc(s["scaled"], 1)
                    pool.wait_ge(s["scaled"], g + 1)
                    pool.tensor_tensor(xa[p][:, :, :], xa[p][:, :, :], rows(affine[3]), ALU.add).then_inc(s["moved"], 1)
                all_groups(pool, NB, step)

        @block.vector
        def _(dve):
            def keep(g, p):
                dve.wait_ge(s["copied"], g + 1)
                dve.tensor_scalar(group_of(k.tmp_res, g), x_t[p][:, :, :], 1.0, None, ALU.mult).then_inc(s["kept"], 1)
                dve.wait_ge(s["logits"], g + 1)
                to = k.logits[:, bass.ds(GROUP * g, GROUP), 0:n_cols]
                of = logit[p][:, 0:GROUP * n_cols].rearrange("p (n c) -> p n c", c=n_cols)
                if gate_bias is None:
                    by = k.rstd2[:, bass.ds(GROUP * g, GROUP)].unsqueeze(2).broadcast_to([P, GROUP, n_cols])
                    dve.tensor_tensor(to, of, by, ALU.mult).then_inc(s["logits_kept"], 1)
                else:
                    dve.tensor_tensor(to, of, gate_bias[:, :].unsqueeze(1).broadcast_to([P, GROUP, n_cols]),
                                      ALU.add).then_inc(s["logits_kept"], 1)

            def step(g, p):
                if not early(g):
                    dve.wait_ge(s["turned"], g - 1)
                    if affine:
                        dve.wait_ge(s["scaled"], g - 1)
                    else:
                        dve.wait_ge(stored[p], 8 * (g - p))
                normalise_group(k, dve, xn[p], source, g, k.rstd, s["normed"])
                if not early(g):
                    keep(g - 2, p)
            all_groups(dve, NB, step)
            keep(NG - 2, 0)
            keep(NG - 1, 1)
            dve.wait_ge(s["logits_kept"], NG)


def build_route(k, m, logit_bias):
    nc, NB, NT = k.nc, k.NB, m.tiles(k.NB)
    with ExitStack() as ctx:
        sb = lambda n, s_, dt=F32: k.sb(m.name + n, s_, dt, ctx)
        t0, t1, probs, counts = (sb(n, [P, NB, E]) for n in ("rt0", "rt1", "rprobs", "rcounts"))
        chosen = [sb(f"rchosen{j}", [P, NB, E]) for j in range(2)]
        both = sb("rboth", [P, NB, E], BF16)
        triangle = sb("rtriangle", [P, P], BF16)
        ones = sb("rones", [P, P], BF16)
        v = [sb(f"rv{i}", [P, NB]) for i in range(3)]
        small = [sb(f"rs{i}", [P, E]) for i in range(4)]
        small_i = sb("rsi", [P, E], I32)
        tile_cmp = sb("rcmp", [P, NT, E])
        tile_of = sb("rtile", [P, NT])
        ranks = k.psum(m.name + "ranks", [P, NB * E], ctx)
        totals = k.psum(m.name + "totals", [P, NB * E], ctx)
        link = Chain(k.sem(m.name + "r_chain"))
        ready, exp_done, counted = (k.sem(m.name + "r_" + n) for n in ("shifted", "exp_done", "counted"))
        onehots = k.sem(m.name + "r_onehots")
        block = ctx.enter_context(nc.Block())

        def over_e(t):
            return t[:, :].unsqueeze(2).broadcast_to([P, NB, E])

        def over_b(t):
            return t[:, 0:E].unsqueeze(1).broadcast_to([P, NB, E])

        n_exp = 2 if m.top == 1 else 1

        @block.scalar
        def _(act):
            act.wait_ge(ready, 1)
            act.activation(probs[:, :, :], t0[:, :, :], ACT.Exp).then_inc(exp_done, 1)
            if n_exp == 2:
                act.wait_ge(ready, 2)
                act.activation(k.coef[:, :, :], k.coef[:, :, :], ACT.Exp).then_inc(exp_done, 1)

        @block.tensor
        def _(pe):
            pe.wait_ge(onehots, 1)
            pe.matmul(ranks[:, :], triangle[:, :], both[:, :, :], start=True, stop=True)
            pe.matmul(totals[:, :], ones[:, :], both[:, :, :], start=True, stop=True).then_inc(counted, 1)

        @block.vector
        def _(dve):
            def do(op):
                link(dve, op)

            TT, TS = dve.tensor_tensor, dve.tensor_scalar
            do(dve.tensor_copy(triangle[:, :], k.tables[:, 0:P]))
            do(dve.memset(ones[:, :], 1.0))
            L = k.logits[:, :, 0:E]
            if logit_bias is not None:
                do(TT(L, L, over_b(logit_bias), ALU.add))
            do(dve.tensor_reduce(v[0][:, :], L, AX.X, ALU.max))
            TT(t0[:, :, :], L, over_e(v[0]), ALU.subtract).then_inc(ready, 1)
            if n_exp == 2:
                C = k.logits[:, :, E:E + 2]
                do(dve.tensor_reduce(v[1][:, :], C, AX.X, ALU.max))
                TT(k.coef[:, :, :], C, v[1][:, :].unsqueeze(2).broadcast_to([P, NB, 2]), ALU.subtract).then_inc(ready, 1)
                dve.wait_ge(exp_done, 2)
                do(dve.tensor_reduce(v[1][:, :], k.coef[:, :, :], AX.X, ALU.add))
                do(dve.reciprocal(v[1][:, :], v[1][:, :]))
                do(TT(k.coef[:, :, :], k.coef[:, :, :], v[1][:, :].unsqueeze(2).broadcast_to([P, NB, 2]), ALU.mult))
            dve.wait_ge(exp_done, 1)
            do(dve.tensor_reduce(v[0][:, :], probs[:, :, :], AX.X, ALU.add))
            do(dve.reciprocal(v[0][:, :], v[0][:, :]))
            do(TT(probs[:, :, :], probs[:, :, :], over_e(v[0]), ALU.mult))
            for j in range(m.top):
                best = k.choice_w[j]
                do(dve.tensor_reduce(best[:, :], probs[:, :, :], AX.X, ALU.max))
                do(TT(t0[:, :, :], probs[:, :, :], over_e(best), ALU.is_equal))
                do(dve.scalar_tensor_tensor(out=t1[:, :, :], in0=t0[:, :, :], scalar=-float(E),
                                            in1=over_b(k.tables[:, P:P + E]), op0=ALU.mult, op1=ALU.add))
                do(dve.tensor_reduce(v[1][:, :], t1[:, :, :], AX.X, ALU.min))
                do(TS(v[1][:, :], v[1][:, :], float(E), None, ALU.add))
                do(TT(chosen[j][:, :, :], over_b(k.tables[:, P:P + E]), over_e(v[1]), ALU.is_equal))
                if j + 1 < m.top:
                    do(dve.scalar_tensor_tensor(out=probs[:, :, :], in0=chosen[j][:, :, :], scalar=-2.0,
                                                in1=probs[:, :, :], op0=ALU.mult, op1=ALU.add))
            if m.top == 2:
                TT(both[:, :, :], chosen[0][:, :, :], chosen[1][:, :, :], ALU.add).then_inc(onehots, 1)
                do(TT(v[0][:, :], k.choice_w[0][:, :], k.choice_w[1][:, :], ALU.add))
                do(TS(v[0][:, :], v[0][:, :], EPS, None, ALU.add))
                do(dve.reciprocal(v[0][:, :], v[0][:, :]))
                for j in range(2):
                    do(TT(k.choice_w[j][:, :], k.choice_w[j][:, :], v[0][:, :], ALU.mult))
            else:
                dve.tensor_copy(both[:, :, :], chosen[0][:, :, :]).then_inc(onehots, 1)
                do(TT(k.choice_w[0][:, :], k.choice_w[0][:, :], k.coef[:, :, 0], ALU.mult))
                do(dve.tensor_copy(k.coef_shared[:, :], k.coef[:, :, 1]))
            dve.wait_ge(counted, 1)
            do(dve.tensor_copy(counts[:, :, :], totals[:, :].rearrange("p (b e) -> p b e", e=E)))
            a, b_, shift = counts, t0, 1
            while shift < NB:
                dve.tensor_copy(b_[:, 0:shift, :], a[:, 0:shift, :]).then_inc(link.sem, 1)
                link.n += 1
                do(TT(b_[:, shift:NB, :], a[:, shift:NB, :], a[:, 0:NB - shift, :], ALU.add))
                a, b_ = b_, (t1 if b_ is t0 else t0)
                shift *= 2
            do(TS(small_i[:, :], a[:, NB - 1, :], float(P - 1), None, ALU.add))
            do(TS(small_i[:, :], small_i[:, :], 7, None, ALU.arith_shift_right))
            do(dve.tensor_copy(small[0][:, :], small_i[:, :]))
            ea, eb, shift = small[0], small[1], 1
            while shift < E:
                dve.tensor_copy(eb[:, 0:shift], ea[:, 0:shift]).then_inc(link.sem, 1)
                link.n += 1
                do(TT(eb[:, shift:E], ea[:, shift:E], ea[:, 0:E - shift], ALU.add))
                ea, eb = eb, (small[2] if eb is small[1] else small[1])
                shift *= 2
            do(TT(small[3][:, :], ea[:, :], small[0][:, :], ALU.subtract))
            do(TS(small[3][:, :], small[3][:, :], float(P), None, ALU.mult))
            rest = t1 if a is t0 else t0
            do(TT(rest[:, :, :], a[:, :, :], counts[:, :, :], ALU.subtract))
            do(TT(rest[:, :, :], rest[:, :, :], over_b(small[3]), ALU.add))
            do(TT(rest[:, :, :], ranks[:, :].rearrange("p (b e) -> p b e", e=E), rest[:, :, :], ALU.add))
            for j in range(m.top):
                do(TT(chosen[j][:, :, :], chosen[j][:, :, :], rest[:, :, :], ALU.mult))
                do(dve.tensor_reduce(v[1][:, :], chosen[j][:, :, :], AX.X, ALU.add))
                do(TS(k.place[j][:, :], v[1][:, :], float(m.first_slot(NB) * P), None, ALU.add))
            tile_no = k.tables[:, P + E:P + E + NT]
            do(TT(tile_cmp[:, :, :], tile_no.unsqueeze(2).broadcast_to([P, NT, E]),
                  ea[:, :].unsqueeze(1).broadcast_to([P, NT, E]), ALU.is_ge))
            do(dve.tensor_reduce(tile_of[:, :], tile_cmp[:, :, :], AX.X, ALU.add))
            do(TS(k.slot_expert[:, 2:2 + NT], tile_of[:, :], float(E - 1), None, ALU.min))


def build_dispatch(k, m, s_up, s_down, shared_bias=None):
    nc, NB = k.nc, k.NB
    RING = 4
    N = GROUP * P
    UP = s_up.shape[1] // P
    C = m.chunks
    with ExitStack() as ctx:
        sb = lambda n, s_, dt=F32: k.sb(m.name + n, s_, dt, ctx)
        rows = [[sb(f"drow{r}_{j}", [P, SLOT]) for j in range(m.top)] for r in range(RING)]
        places = [[sb(f"dplace{r}_{j}", [P, 1], I32) for j in range(m.top)] for r in range(RING)]
        g = [sb(f"sg{c}", [P, N]) for c in range(2)]
        h_t = [[sb(f"sh{p}_{c}", [P, N]) for c in range(C)] for p in range(2)]
        extra = sb("sextra", [P, GROUP, D])
        hidden = [k.psum(f"{m.name}shid{c}", [P, N], ctx) for c in range(4)]
        result = [k.psum(f"{m.name}sres{p}", [P, N], ctx) for p in range(2)]
        loaded = [k.sem(f"{m.name}d_loaded{r}") for r in range(RING)]
        sent = [k.pool_dma_sem(f"{m.name}d_sent{r}") for r in range(RING)]
        s = {n: k.sem(m.name + "d_" + n) for n in
             ("cleared", "placed", "go", "hidden", "gated", "h_ready", "half_result", "result", "added", "scaled")}
        block = ctx.enter_context(nc.Block())
        per = 16 * m.top

        @block.sync
        def _(sp):
            def load(b, r):
                for j in range(m.top):
                    sp.dma_start(rows[r][j][:, 0:D], k.xf_dram[bass.ds(b * P, P), :]).then_inc(loaded[r], 16)

            for r in range(RING):
                load(r, r)
            with sp.Fori(1, NB // RING) as i:
                for r in range(RING):
                    sp.wait_ge(sent[r], per * i)
                    load(RING * i + r, r)

        @block.gpsimd
        def _(pool):
            def step(i, r):
                pool.wait_ge(s["placed"], 2 * m.top * (RING * i + r + 1))
                pool.wait_ge(loaded[r], per * i + per)
                pool.sem_inc(s["go"], 1)
                for j in range(m.top):
                    pool.indirect_dma_start(k.slots, bass.IndirectOffsetOnAxis(places[r][j][:, 0:1], 0),
                                            rows[r][j][:, :], None).then_inc(sent[r], 16)
            for r in range(RING):
                for j in range(m.top):
                    pool.memset(rows[r][j][:, D:SLOT], 0.0).then_inc(s["cleared"], 1)
            for r in range(RING):
                step(0, r)
            with pool.Fori(1, NB // RING) as i:
                for r in range(RING):
                    step(i, r)
            for r in range(RING):
                pool.wait_ge(sent[r], per * (NB // RING))

        @block.tensor
        def _(pe):
            def go_up(g_, chunks):
                for c in chunks:
                    if not early(g_, 1):
                        pe.wait_ge(s["h_ready"], C * (g_ - 1) + c % C + 1)
                    pe.matmul(hidden[c][:, :], s_up[:, c * P:(c + 1) * P], group_of(k.tmp_res, g_),
                              start=True, stop=True).then_inc(s["hidden"], 1)

            def go_down(g_, p, members):
                pe.wait_ge(s["h_ready"], C * (g_ + 1))
                if not early(g_):
                    pe.wait_ge(s["added"], g_ - 1)
                for n in members:
                    for c in range(C):
                        mm = pe.matmul(result[p][:, n * D:(n + 1) * D], h_t[p][c][:, n * P:(n + 1) * P], s_down[:, c, :],
                                       start=(c == 0), stop=(c == C - 1))
                mm.then_inc(s["result"] if members[-1] == GROUP - 1 else s["half_result"], 1)

            def step(g_, p):
                go_up(g_, (0, 1))
                if not early(g_, 1):
                    go_down(g_ - 1, 1 - p, (0, 1))
                go_up(g_, (2, 3))
                if not early(g_, 1):
                    go_down(g_ - 1, 1 - p, (2, 3))
            all_groups(pe, NB, step, peel=4)
            go_down(NB // GROUP - 1, 1, (0, 1, 2, 3))

        @block.scalar
        def _(act):
            def step(g_, p):
                for c in range(C):
                    act.wait_ge(s["hidden"], UP * g_ + c + 1)
                    if shared_bias is None:
                        if not early(g_, 1):
                            act.wait_ge(s["h_ready"], C * (g_ - 1) + c + 1)
                        act.activation(g[c][:, :], hidden[c][:, :], m.act).then_inc(s["gated"], 1)
                    else:
                        if c == 0 and not early(g_):
                            act.wait_ge(s["result"], g_ - 1)
                        act.activation(h_t[p][c][:, :], hidden[c][:, :], m.act,
                                       bias=shared_bias[0][:, c:c + 1]).then_inc(s["h_ready"], 1)
            all_groups(act, NB, step)

        @block.vector
        def _(dve):
            def place(b, r):
                for j in range(m.top):
                    dve.tensor_scalar(places[r][j][:, :], k.place[j][:, bass.ds(b, 1)], 1.0, None,
                                      ALU.mult).then_inc(s["placed"], 1)
                    dve.tensor_scalar(rows[r][j][:, D:D + 1], k.token_rows[:, j, bass.ds(b, 1)], 1.0, None,
                                      ALU.mult).then_inc(s["placed"], 1)

            def hide(g_, p):
                if not early(g_):
                    dve.wait_ge(s["result"], g_ - 1)
                for c in range(C):
                    dve.wait_ge(s["gated"], C * g_ + c + 1)
                    dve.wait_ge(s["hidden"], UP * g_ + C + c + 1)
                    dve.tensor_tensor(h_t[p][c][:, :], g[c][:, :], hidden[C + c][:, :], ALU.mult).then_inc(s["h_ready"], 1)

            def finish(g_, p):
                res = result[p][:, :].rearrange("p (n d) -> p n d", d=D)
                x4 = group_of(k.x_res, g_)
                dve.wait_ge(s["result"], g_ + 1)
                if shared_bias is None:
                    dve.tensor_tensor(x4, x4, res, ALU.add).then_inc(s["added"], 1)
                    return
                if not early(g_, 1):
                    dve.wait_ge(s["scaled"], GROUP * g_)
                dve.tensor_tensor(extra[:, :, :], res, shared_bias[1][:, :].unsqueeze(1).broadcast_to([P, GROUP, D]),
                                  ALU.add).then_inc(s["added"], 1)
                dve.wait_ge(s["added"], g_ + 1)
                for n in range(GROUP):
                    b = GROUP * g_ + n
                    dve.scalar_tensor_tensor(out=k.x_res[:, b, :], in0=extra[:, n, :], scalar=k.coef_shared[:, bass.ds(b, 1)],
                                             in1=k.x_res[:, b, :], op0=ALU.mult, op1=ALU.add).then_inc(s["scaled"], 1)

            def step(g_, p):
                for r in range(RING):
                    if not early(g_, 1):
                        dve.wait_ge(sent[r], per * g_)
                    place(RING * g_ + r, r)
                if shared_bias is None:
                    hide(g_, p)
                if not early(g_):
                    finish(g_ - 2, p)
            dve.wait_ge(s["cleared"], m.top * RING)
            all_groups(dve, NB, step, peel=4)
            finish(NB // GROUP - 2, 0)
            finish(NB // GROUP - 1, 1)
            dve.wait_ge(s["added"], NB // GROUP)
            if shared_bias is not None:
                dve.wait_ge(s["scaled"], NB)


def build_experts(k, m, up, down, up_bias=None, down_bias=None):
    nc, NT = k.nc, m.tiles(k.NB)
    C = m.chunks
    R, QD = 8, 4
    NR = NT // R
    with ExitStack() as ctx:
        sb = lambda n, s_, dt=F32: k.sb(m.name + n, s_, dt, ctx)
        x_in = [sb(f"ex{q}", [P, QD, SLOT]) for q in range(2)]
        to_row = [[sb(f"erow{q}_{i}", [P, 1], I32) for i in range(QD)] for q in range(2)]
        x_t = [sb(f"ext{p}", [P, P]) for p in range(2)]
        g = [sb(f"eg{p}", [P, 512]) for p in range(2)]
        h = [sb(f"eh{p}", [P, C * P]) for p in range(2)]
        h_t = [sb(f"eht{p}", [P, C * P]) for p in range(2)]
        y = [sb(f"ey{q}", [P, QD, D]) for q in range(2)]
        turned = [k.psum(f"{m.name}eturn{p}", [P, 512], ctx) for p in range(2)]
        hidden = [k.psum(f"{m.name}ehid{p}", [P, 512], ctx) for p in range(2)]
        h_turned = [k.psum(f"{m.name}ehturn{p}", [P, 512], ctx) for p in range(2)]
        result = [k.psum(f"{m.name}eres{p}", [P, 512], ctx) for p in range(2)]
        loaded = [k.sem(f"{m.name}e_loaded{q}") for q in range(2)]
        stored = [k.pool_dma_sem(f"{m.name}e_stored{q}") for q in range(2)]
        s = {n: k.sem(m.name + "e_" + n) for n in
             ("turned", "x_ready", "hidden", "biased", "gated", "h_ready", "h_turned", "h_t_ready", "result", "y_ready",
              "rows_copied", "go", "gone")}
        block = ctx.enter_context(nc.Block())

        def rows_of(t, quad):
            return t[bass.ds(quad * QD * P, QD * P), :].rearrange("(n p) d -> p n d", p=P)

        def each(eng, step):
            for r in range(R):
                step(0, r)
            with eng.Fori(1, NR - 1) as n:
                for r in range(R):
                    step(n, r)
            for r in range(R):
                step(NR - 1, r)

        def off(n, r, d):
            n, r = n + (r + d) // R, (r + d) % R
            return None if isinstance(n, int) and not 0 <= n < NR else (n, r)

        def slot(at):
            return R * at[0] + at[1]

        def round_experts(engine, n):
            return nc.values_load_multi_w_load_instructions(
                k.slot_expert[0:1, bass.ds(R * n, 2 + R)], engines=(engine,), min_val=0, max_val=E - 1,
                skip_runtime_bounds_check_because="the routing bounds every entry to the experts there are")[1]

        def back2(at):
            return off(*at, -2) is not None

        @block.sync
        def _(sp):
            def load(n, q):
                if not early(n, 1):
                    sp.wait_ge(s["turned"], R * (n - 1) + QD * (q + 1))
                    sp.wait_ge(s["rows_copied"], R * (n - 1) + QD * (q + 1))
                sp.dma_start(x_in[q][:, :, :], rows_of(k.slots, 2 * n + q + m.first_slot(k.NB) // QD)).then_inc(loaded[q], 16)

            for q in range(2):
                load(0, q)
            with sp.Fori(1, NR) as n:
                for q in range(2):
                    load(n, q)

        @block.gpsimd
        def _(pool):
            def store(n, q):
                pool.wait_ge(loaded[q], 16 * n + 16)
                if not early(n, 1):
                    pool.wait_ge(stored[q], 16 * QD * n)
                pool.sem_inc(s["go"], 1)
                for i in range(QD):
                    pool.tensor_copy(to_row[q][i][:, :], x_in[q][:, i, D:D + 1]).then_inc(s["rows_copied"], 1)
                pool.wait_ge(s["rows_copied"], R * n + QD * (q + 1))
                for i in range(QD):
                    pool.wait_ge(s["y_ready"], R * n + QD * q + i + 1)
                    pool.sem_inc(s["gone"], 1)
                    pool.indirect_dma_start(k.results, bass.IndirectOffsetOnAxis(to_row[q][i][:, 0:1], 0),
                                            y[q][:, i, :], None).then_inc(stored[q], 16)

            for q in range(2):
                store(0, q)
            with pool.Fori(1, NR) as n:
                for q in range(2):
                    store(n, q)
            for q in range(2):
                pool.wait_ge(stored[q], 16 * QD * NR)

        @block.tensor
        def _(pe):
            experts = []

            def turn_x(at, of):
                n, r = at
                if r % QD == 0:
                    pe.wait_ge(loaded[r // QD], 16 * n + 16)
                if back2(at):
                    pe.wait_ge(s["x_ready"], slot(at) - 1)
                pe.transpose(turned[r % 2][:, 0:P], x_in[r // QD][:, r % QD, 0:D], k.ident[:, :]).then_inc(s["turned"], 1)

            def go_up(at, of):
                p = at[1] % 2
                e = experts[of]
                pe.wait_ge(s["x_ready"], slot(at) + 1)
                if back2(at):
                    pe.wait_ge(s["biased" if up_bias is not None else "h_ready"], slot(at) - 1)
                pe.matmul(hidden[p][:, :], x_t[p][:, :], up[:, e, :], start=True, stop=True).then_inc(s["hidden"], 1)

            def turn_h(at, of):
                p = at[1] % 2
                pe.wait_ge(s["h_ready"], slot(at) + 1)
                if back2(at):
                    pe.wait_ge(s["h_t_ready"], slot(at) - 1)
                for c in range(C):
                    mm = pe.transpose(h_turned[p][:, c * P:(c + 1) * P], h[p][:, c * P:(c + 1) * P], k.ident[:, :])
                mm.then_inc(s["h_turned"], 1)

            def go_down(at, of):
                p = at[1] % 2
                e = experts[of]
                pe.wait_ge(s["h_t_ready"], slot(at) + 1)
                if back2(at):
                    pe.wait_ge(s["y_ready"], slot(at) - 1)
                for c in range(C):
                    mm = pe.matmul(result[p][:, 0:D], h_t[p][:, c * P:(c + 1) * P], down[:, e, c, :],
                                   start=(c == 0), stop=(c == C - 1))
                mm.then_inc(s["result"], 1)

            def step(n, r):
                if r == 0:
                    experts[:] = round_experts(mybir.EngineType.PE, n)
                for d, work in ((1, turn_x), (0, go_up), (-1, turn_h), (-2, go_down)):
                    at = off(n, r, d)
                    if at is not None:
                        work(at, 2 + r + d)
            turn_x((0, 0), 2)
            each(pe, step)
            turn_h((NR - 1, R - 1), R + 1)
            go_down((NR - 1, R - 2), R)
            go_down((NR - 1, R - 1), R + 1)

        @block.scalar
        def _(act):
            def copy_x(at):
                p = at[1] % 2
                act.wait_ge(s["turned"], slot(at) + 1)
                if back2(at):
                    act.wait_ge(s["hidden"], slot(at) - 1)
                act.activation(x_t[p][:, :], turned[p][:, 0:P], ACT.Copy).then_inc(s["x_ready"], 1)

            def gate(at):
                p = at[1] % 2
                if up_bias is not None:
                    act.wait_ge(s["biased"], slot(at) + 1)
                    if back2(at):
                        act.wait_ge(s["h_turned"], slot(at) - 1)
                    act.activation(h[p][:, :], g[p][:, :], m.act).then_inc(s["h_ready"], 1)
                else:
                    act.wait_ge(s["hidden"], slot(at) + 1)
                    if back2(at):
                        act.wait_ge(s["h_ready"], slot(at) - 1)
                    act.activation(g[p][:, 0:m.inner], hidden[p][:, 0:m.inner], m.act).then_inc(s["gated"], 1)

            def step(n, r):
                nxt = off(n, r, 1)
                if nxt is not None:
                    copy_x(nxt)
                gate((n, r))
            copy_x((0, 0))
            each(act, step)

        @block.vector
        def _(dve):
            experts = []

            def open_(at, of):
                p = at[1] % 2
                if up_bias is not None:
                    e = experts[of]
                    dve.wait_ge(s["hidden"], slot(at) + 1)
                    if back2(at):
                        dve.wait_ge(s["h_ready"], slot(at) - 1)
                    dve.tensor_tensor(g[p][:, :], hidden[p][:, :], up_bias[:, e, :], ALU.add).then_inc(s["biased"], 1)
                else:
                    dve.wait_ge(s["gated"], slot(at) + 1)
                    if back2(at):
                        dve.wait_ge(s["h_turned"], slot(at) - 1)
                    dve.tensor_tensor(h[p][:, :], g[p][:, 0:m.inner], hidden[p][:, m.inner:2 * m.inner],
                                      ALU.mult).then_inc(s["h_ready"], 1)

            def copy_h(at, of):
                p = at[1] % 2
                dve.wait_ge(s["h_turned"], slot(at) + 1)
                if back2(at):
                    dve.wait_ge(s["result"], slot(at) - 1)
                dve.tensor_copy(h_t[p][:, :], h_turned[p][:, 0:C * P]).then_inc(s["h_t_ready"], 1)

            def close(at, of):
                n, r = at
                p, q = r % 2, r // QD
                e = experts[of] if down_bias is not None else None
                dve.wait_ge(s["result"], slot(at) + 1)
                if r % QD == 0 and not early(n, 1):
                    dve.wait_ge(stored[q], 16 * QD * n)
                if down_bias is not None:
                    op = dve.tensor_tensor(y[q][:, r % QD, :], result[p][:, 0:D], down_bias[:, e, :], ALU.add)
                else:
                    op = dve.tensor_copy(y[q][:, r % QD, :], result[p][:, 0:D])
                op.then_inc(s["y_ready"], 1)

            def step(n, r):
                if r == 0 and up_bias is not None:
                    experts[:] = round_experts(mybir.EngineType.DVE, n)
                for d, work in ((-1, copy_h), (0, open_), (-2, close)):
                    at = off(n, r, d)
                    if at is not None:
                        work(at, 2 + r + d)
            each(dve, step)
            copy_h((NR - 1, R - 1), R + 1)
            close((NR - 1, R - 2), R)
            close((NR - 1, R - 1), R + 1)


def build_combine(k, m, final=False):
    nc, NB = k.nc, k.NB
    with ExitStack() as ctx:
        RING = 4
        rows = [[k.sb(f"{m.name}crow{r}_{j}", [P, GROUP, D], F32, ctx) for j in range(m.top)] for r in range(RING)]
        loaded = [k.sem(f"{m.name}c_loaded{r}") for r in range(RING)]
        s = {n: k.sem(m.name + "c_" + n) for n in ("first", "second", "stats")}
        taken = s["second" if m.top == 2 else "first"]
        stored = k.sem(m.name + "c_stored")
        block = ctx.enter_context(nc.Block())
        NG = NB // GROUP

        def each(eng, step):
            for r in range(RING):
                step(r, r, 0)
            with eng.Fori(1, NG // RING) as i:
                for r in range(RING):
                    step(RING * i + r, r, i)

        @block.sync
        def _(sp):
            def step(g, r, i):
                if not early(g, RING):
                    sp.wait_ge(taken, GROUP * (g - RING + 1))
                for j in range(m.top):
                    first = m.results_row(NB, j)
                    sp.dma_start(rows[r][j][:, :, :],
                                 k.results[bass.ds(g * (GROUP * P) + first, GROUP * P), :].rearrange("(n t) d -> t n d", t=P)
                                 ).then_inc(loaded[r], 16)
            each(sp, step)

        if final:
            @block.scalar
            def _(act):
                def step(g, r, i):
                    act.wait_ge(taken, GROUP * (g + 1))
                    act.dma_start(k.out[bass.ds(GROUP * g, GROUP)].rearrange("b t d -> t b d"),
                                  group_of(k.x_res, g)).then_inc(stored, 16)
                each(act, step)
                act.wait_ge(stored, 16 * NG)

        @block.vector
        def _(dve):
            def step(g, r, i):
                dve.wait_ge(loaded[r], 16 * m.top * i + 16 * m.top)
                for j in range(m.top):
                    done = s["first"] if j == 0 else s["second"]
                    for n in range(GROUP):
                        b = GROUP * g + n
                        dve.scalar_tensor_tensor(out=k.x_res[:, b, :], in0=rows[r][j][:, n, :],
                                                 scalar=k.choice_w[j][:, bass.ds(b, 1)], in1=k.x_res[:, b, :],
                                                 op0=ALU.mult, op1=ALU.add).then_inc(done, 1)
                    dve.wait_ge(done, GROUP * (g + 1))
                if not final:
                    for n in range(GROUP):
                        b = GROUP * g + n
                        dve.bn_stats(k.stats[:, b, :], k.x_res[:, b, :]).then_inc(s["stats"], 1)
            each(dve, step)
            if not final:
                dve.wait_ge(s["stats"], NB)


def build_expert_layer_0(k):
    nc, ins = k.nc, k.ins
    m = Experts("m0_", 256, 2, 2, ACT.Silu)
    with ExitStack() as ctx:
        up = k.sb("m0_up", [P, E, 512], F32, ctx)
        down = k.sb("m0_down", [P, E, 2, D], F32, ctx)
        s_up = k.sb("m0_s_up", [P, 512], F32, ctx)
        s_down = k.sb("m0_s_down", [P, 2, D], F32, ctx)
        gate = k.sb("m0_gate", [P, E], F32, ctx)
        scale = k.sb("m0_scale", [P, 1], F32, ctx)
        bias = k.sb("m0_bias", [P, 1], F32, ctx)
        bias_wide = k.sb("m0_bias_wide", [P, P], F32, ctx)
        gate_scaled = k.sb("m0_gate_scaled", [P, E], F32, ctx)
        logit_bias = k.sb("m0_logit_bias", [P, E], F32, ctx)
        loaded = k.sem("m0_loaded")
        link = Chain(k.sem("m0_chain"))
        product = k.sem("m0_bias_product")
        weights_loaded = k.sem("m0_weights_loaded")
        weights = [(up[:, :, 0:256], ins["L0_ffn_Wg"].rearrange("e h i -> h e i")),
                 (up[:, :, 256:512], ins["L0_ffn_Wu"].rearrange("e h i -> h e i")),
                 (down[:, :, :, :], ins["L0_ffn_Wd"].rearrange("e (c p) h -> p e c h", p=P)),
                 (s_up[:, 0:256], ins["L0_ffn_sWg"]), (s_up[:, 256:512], ins["L0_ffn_sWu"]),
                 (s_down[:, :, :], ins["L0_ffn_sWd"].rearrange("(c p) h -> p c h", p=P))]
        loads = [(gate[:, :], ins["L0_ffn_gate_w"].rearrange("e h -> h e")),
                 (scale[:, :], column(ins["L0_ffn_ln_scale"])), (bias[:, :], column(ins["L0_ffn_ln_bias"]))]
        with ExitStack() as inner:
            ps = k.psum("m0_bias_ps", [P, 512], inner)
            block = inner.enter_context(nc.Block())

            @block.sync
            def _(sp):
                for to, of in loads:
                    sp.dma_start(to, of, allow_slow_non_contiguous=True).then_inc(loaded, 16)
                for to, of in weights:
                    sp.dma_start(to, of).then_inc(weights_loaded, 16)

            @block.vector
            def _(dve):
                dve.wait_ge(loaded, 16 * len(loads))
                link(dve, dve.tensor_scalar(gate_scaled[:, :], gate[:, :], scale[:, 0:1], None, ALU.mult))
                link(dve, dve.tensor_copy(bias_wide[:, :], bias[:, 0:1].broadcast_to([P, P])))
                dve.wait_ge(product, 1)
                link(dve, dve.tensor_copy(logit_bias[:, :], ps[:, 0:E]))

            @block.tensor
            def _(pe):
                pe.wait_ge(link.sem, 2)
                pe.matmul(ps[:, 0:E], bias_wide[:, :], gate[:, :], start=True, stop=True).then_inc(product, 1)
        build_rstd(k, "m0_rstd", composed=True)
        build_prepare(k, m, gate_scaled[:, :], None, None, (weights_loaded, 16 * len(weights)))
        build_route(k, m, logit_bias)
        build_dispatch(k, m, s_up, s_down)
        build_experts(k, m, up, down)
        build_combine(k, m)



TOP_DELAYS = 9


def build_correlation(k):
    nc, ins, NB = k.nc, k.ins, k.NB
    N = GROUP * P
    with ExitStack() as ctx:
        sb = lambda n, s_, dt=F32: k.sb(n, s_, dt, ctx)
        wq, wk = sb("c_wq", [P, D]), sb("c_wk", [P, D])
        bq, bk = sb("c_bq", [1, D]), sb("c_bk", [1, D])
        dft, inverse, flip = sb("c_dft", [P, P]), sb("c_inverse", [P, P]), sb("c_flip", [P, 2 * P])
        dft_sums = sb("c_dft_sums", [1, 2, P])
        ones = sb("c_ones", [P, 1])
        xn = [sb(f"c_xn{p}", [P, GROUP, D]) for p in range(2)]
        cx = [sb(f"c_cx{p}", [P, GROUP, D]) for p in range(2)]
        xf = [sb(f"c_xf{p}", [P, N]) for p in range(2)]
        cf = [sb(f"c_cf{p}", [P, N]) for p in range(2)]
        kf, qf = sb("c_kf", [P, GROUP, P]), sb("c_qf", [P, GROUP, P])
        bias_spec = sb("c_bias_spec", [P, 2, P])
        product = [sb(f"c_product{p}", [P, GROUP, P]) for p in range(2)]
        spectrum = sb("c_spectrum", [P, NB])
        corr, work, weight = sb("c_corr", [NB, P]), sb("c_work", [NB, P]), sb("c_weight", [NB, P])
        best, ninth = sb("c_best", [NB, 8]), sb("c_ninth", [NB, 8])
        total = sb("c_total", [NB, 1])
        weight_t = sb("c_weight_t", [P, NB])
        twice = sb("c_twice", [NB, 2 * P])
        x_spec, c_spec = k.psum("c_x_spec", [P, N], ctx), k.psum("c_c_spec", [P, N], ctx)
        q_spec, k_spec = k.psum("c_q_spec", [P, N], ctx), k.psum("c_k_spec", [P, N], ctx)
        power = k.psum("c_power", [P, 512], ctx)
        back = k.psum("c_back", [P, 512], ctx)
        loaded = k.sem("c_loaded")
        cx_loaded = [k.sem(f"c_cx_loaded{p}") for p in range(2)]
        link = Chain(k.sem("c_chain"))
        s = {n: k.sem("c_" + n) for n in ("ones_set", "normed", "x_spec", "c_spec", "xf", "cf", "q_spec", "k_spec", "kf", "qf", "bias_product", "bias_ready",
                                          "product", "power", "spectrum", "corr", "shifted", "exp_done", "weighted", "turned", "turn_copied", "flipped", "twice", "stored")}
        loads = [(wq[:, :], ins["L1_xattn_Wq"]), (wk[:, :], ins["L1_xattn_Wk"]), (bq[:, :], ins["L1_xattn_bq"].unsqueeze(0)),
                 (bk[:, :], ins["L1_xattn_bk"].unsqueeze(0)), (dft[:, :], ins["c_dft"]), (inverse[:, :], ins["c_inverse"]),
                 (flip[:, :], ins["c_flip"]), (dft_sums[:, :, :], ins["c_dft_sums"].unsqueeze(0))]
        block = ctx.enter_context(nc.Block())
        NG = NB // GROUP

        @block.sync
        def _(sp):
            for to, of in loads:
                sp.dma_start(to, of).then_inc(loaded, 16)

            def step(g, p):
                if not early(g):
                    sp.wait_ge(s["c_spec"], g - 1)
                sp.dma_start(cx[p][0:S2, :, :], ins["ctx_1024"][bass.ds(GROUP * g, GROUP)].rearrange("b t d -> t b d")).then_inc(cx_loaded[p], 16)
            all_groups(sp, NB, step)
            sp.wait_ge(s["twice"], 1)
            sp.dma_start(k.circulant, twice[:, :]).then_inc(s["stored"], 16)
            sp.wait_ge(s["stored"], 16)

        @block.tensor
        def _(pe):
            def spectra(g, p):
                pe.wait_ge(s["normed"], GROUP * (g + 1))
                pe.wait_ge(s["xf"], g)
                for n in range(GROUP):
                    mm = pe.matmul(x_spec[:, n * P:(n + 1) * P], xn[p][:, n, :], dft[:, :], start=True, stop=True)
                mm.then_inc(s["x_spec"], 1)
                pe.wait_ge(cx_loaded[p], 8 * (g - p) + 16)
                pe.wait_ge(s["cf"], g)
                for n in range(GROUP):
                    mm = pe.matmul(c_spec[:, n * P:(n + 1) * P], cx[p][0:S2, n, :], dft[0:S2, :], start=True, stop=True)
                mm.then_inc(s["c_spec"], 1)

            def project(g, p):
                pe.wait_ge(s["cf"], g + 1)
                pe.wait_ge(s["kf"], g)
                pe.matmul(k_spec[:, :], wk[:, :], cf[p][:, :], start=True, stop=True).then_inc(s["k_spec"], 1)
                pe.wait_ge(s["xf"], g + 1)
                pe.wait_ge(s["qf"], g)
                pe.matmul(q_spec[:, :], wq[:, :], xf[p][:, :], start=True, stop=True).then_inc(s["q_spec"], 1)

            def powers(g, p):
                pe.wait_ge(s["product"], g + 1)
                for n in range(GROUP):
                    mm = pe.matmul(power[:, bass.ds(GROUP * g + n, 1)], product[p][:, n, :], ones[:, :], start=True, stop=True)
                mm.then_inc(s["power"], 1)

            def step(g, p):
                spectra(g, p)
                if not early(g, 1):
                    project(g - 1, 1 - p)
                if not early(g, 3):
                    powers(g - 3, 1 - p)
            pe.wait_ge(loaded, 16 * len(loads))
            pe.wait_ge(s["ones_set"], 1)
            pe.matmul(back[:, 0:P], bk[:, :], dft_sums[:, 1, :], start=True, stop=True)
            pe.matmul(back[:, P:2 * P], bq[:, :], dft_sums[:, 0, :], start=True, stop=True).then_inc(s["bias_product"], 1)
            all_groups(pe, NB, step, peel=4)
            project(NG - 1, 1)
            powers(NG - 3, 1)
            powers(NG - 2, 0)
            powers(NG - 1, 1)
            pe.wait_ge(s["spectrum"], 1)
            pe.matmul(back[0:NB, 0:P], spectrum[:, :], inverse[:, :], start=True, stop=True).then_inc(s["corr"], 1)
            pe.wait_ge(s["weighted"], 1)
            pe.transpose(power[:, 0:NB], weight[:, :], k.ident[0:NB, 0:NB]).then_inc(s["turned"], 1)
            pe.wait_ge(s["turn_copied"], 1)
            pe.matmul(back[0:NB, 0:2 * P], weight_t[:, :], flip[:, :], start=True, stop=True).then_inc(s["flipped"], 1)

        @block.scalar
        def _(act):
            def step(g, p):
                act.wait_ge(s["x_spec"], g + 1)
                if not early(g):
                    act.wait_ge(s["q_spec"], g - 1)
                act.activation(xf[p][:, :], x_spec[:, :], ACT.Copy).then_inc(s["xf"], 1)
                act.wait_ge(s["c_spec"], g + 1)
                if not early(g):
                    act.wait_ge(s["k_spec"], g - 1)
                act.activation(cf[p][:, :], c_spec[:, :], ACT.Copy).then_inc(s["cf"], 1)
            all_groups(act, NB, step)
            act.wait_ge(s["shifted"], 1)
            act.activation(work[:, :], corr[:, :], ACT.Exp).then_inc(s["exp_done"], 1)

        @block.vector
        def _(dve):
            def multiply(g, p):
                def of(spec):
                    return spec[:, :].rearrange("p (n d) -> p n d", d=P)

                def bias(n):
                    return bias_spec[:, n, :].unsqueeze(1).broadcast_to([P, GROUP, P])
                dve.wait_ge(s["k_spec"], g + 1)
                dve.wait_ge(s["product"], g)
                dve.tensor_tensor(kf[:, :, :], of(k_spec), bias(0), ALU.add).then_inc(s["kf"], 1)
                dve.wait_ge(s["q_spec"], g + 1)
                dve.tensor_tensor(qf[:, :, :], of(q_spec), bias(1), ALU.add).then_inc(s["qf"], 1)
                dve.wait_ge(s["kf"], g + 1)
                dve.wait_ge(s["qf"], g + 1)
                if not early(g):
                    dve.wait_ge(s["power"], g - 1)
                dve.tensor_tensor(product[p][:, :, :], qf[:, :, :], kf[:, :, :], ALU.mult).then_inc(s["product"], 1)

            def step(g, p):
                if not early(g):
                    dve.wait_ge(s["x_spec"], g - 1)
                normalise_group(k, dve, xn[p], k.x_res, g, k.rstd, s["normed"])
                if not early(g):
                    multiply(g - 2, p)
            dve.memset(ones[:, :], 1.0).then_inc(s["ones_set"], 1)
            dve.wait_ge(s["bias_product"], 1)
            dve.tensor_copy(bias_spec[:, :, :].rearrange("p n d -> p (n d)"), back[:, 0:2 * P]).then_inc(s["bias_ready"], 1)
            dve.wait_ge(s["bias_ready"], 1)
            all_groups(dve, NB, step, peel=4)
            multiply(NG - 2, 0)
            multiply(NG - 1, 1)
            dve.wait_ge(s["power"], NG)
            dve.tensor_copy(spectrum[:, :], power[:, 0:NB]).then_inc(s["spectrum"], 1)
            dve.wait_ge(s["corr"], 1)

            def do(op):
                link(dve, op)
            LOW = -3.0e38
            do(dve.tensor_copy(corr[:, :], back[0:NB, 0:P]))
            do(dve.max(best[:, :], corr[:, :]))
            do(dve.match_replace(work[:, :], best[:, :], corr[:, :], LOW))
            do(dve.max(ninth[:, :], work[:, :]))
            do(dve.memset(ninth[:, 1:8], LOW))
            do(dve.match_replace(weight[:, :], ninth[:, :], work[:, :], LOW))
            do(dve.tensor_scalar(weight[:, :], weight[:, :], LOW, None, ALU.is_equal))
            dve.tensor_scalar(corr[:, :], corr[:, :], best[:, 0:1], None, ALU.subtract).then_inc(s["shifted"], 1)
            dve.wait_ge(s["exp_done"], 1)
            do(dve.tensor_tensor(weight[:, :], weight[:, :], work[:, :], ALU.mult))
            do(dve.tensor_reduce(total[:, :], weight[:, :], AX.X, ALU.add))
            do(dve.reciprocal(total[:, :], total[:, :]))
            dve.tensor_scalar(weight[:, :], weight[:, :], total[:, 0:1], None, ALU.mult).then_inc(s["weighted"], 1)
            dve.wait_ge(s["turned"], 1)
            dve.tensor_copy(weight_t[:, :], power[:, 0:NB]).then_inc(s["turn_copied"], 1)
            dve.wait_ge(s["flipped"], 1)
            dve.tensor_copy(twice[:, :], back[0:NB, 0:2 * P]).then_inc(s["twice"], 1)


def build_roll(k):
    nc, ins, NB = k.nc, k.ins, k.NB
    N = GROUP * P
    with ExitStack() as ctx:
        roll = [k.sb(f"v_roll{p}", [P, GROUP, P], F32, ctx) for p in range(2)]
        bo_rows = k.sb("v_bo", [P, D], F32, ctx)
        rolled = [k.psum(f"v_rolled{p}", [P, N], ctx) for p in range(2)]
        loaded = [k.sem(f"v_loaded{p}") for p in range(2)]
        bo_loaded = k.sem("v_bo_loaded")
        s = {n: k.sem("v_" + n) for n in ("rolled", "biased", "added", "stats")}
        block = ctx.enter_context(nc.Block())

        @block.sync
        def _(sp):
            sp.dma_start(bo_rows[:, :], row_broadcast(ins["L1_xattn_bo"], P)).then_inc(bo_loaded, 16)

            def step(g, p):
                if not early(g):
                    sp.wait_ge(s["rolled"], g - 1)
                rows = k.circulant[bass.ds(GROUP * g, GROUP), P - S2 + 1:2 * P - S2 + 1]
                sp.dma_start(roll[p][0:S2, :, :],
                             bass.AP(tensor=rows.tensor, offset=rows.offset,
                                     ap=[[1, S2], [2 * P, GROUP], [1, P]])).then_inc(loaded[p], 16)
            all_groups(sp, NB, step)

        @block.tensor
        def _(pe):
            def step(g, p):
                pe.wait_ge(loaded[p], 8 * (g - p) + 16)
                if not early(g):
                    pe.wait_ge(s["biased"], g - 1)
                for n in range(GROUP):
                    mm = pe.matmul(rolled[p][:, n * D:(n + 1) * D], roll[p][0:S2, n, :], k.vo_res[0:S2, GROUP * g + n, :],
                                   start=True, stop=True)
                mm.then_inc(s["rolled"], 1)
            all_groups(pe, NB, step)

        @block.gpsimd
        def _(pool):
            def step(g, p):
                pool.tensor_tensor(group_of(k.x_res, g), group_of(k.x_res, g),
                                   bo_rows[:, :].unsqueeze(1).broadcast_to([P, GROUP, D]), ALU.add).then_inc(s["added"], 1)
            pool.wait_ge(bo_loaded, 16)
            all_groups(pool, NB, step)

        @block.vector
        def _(dve):
            def step(g, p):
                dve.wait_ge(s["rolled"], g + 1)
                dve.wait_ge(s["added"], g + 1)
                dve.tensor_tensor(group_of(k.x_res, g), rolled[p][:, :].rearrange("p (n d) -> p n d", d=D),
                                  group_of(k.x_res, g), ALU.add).then_inc(s["biased"], 1)
                dve.wait_ge(s["biased"], g + 1)
                for n in range(GROUP):
                    dve.bn_stats(k.stats[:, GROUP * g + n, :], k.x_res[:, GROUP * g + n, :]).then_inc(s["stats"], 1)
            all_groups(dve, NB, step)
            dve.wait_ge(s["stats"], NB)



def build_self_attention(k):
    nc, ins, NB = k.nc, k.ins, k.NB
    W = HQ * P
    CH = H // HQ
    COL = 2 * QUAD
    with ExitStack() as ctx:
        sb = lambda n, s_, dt=F32: k.sb(n, s_, dt, ctx)
        wqkv, wo = sb("s_wqkv", [P, 3 * D]), sb("s_wo", [P, D])
        gain, shift_ = sb("s_gain", [P, 1]), sb("s_shift", [P, 1])
        bq, bk = sb("s_bq", [P, 1]), sb("s_bk", [P, 1])
        bv_rows, bo_rows = sb("s_bv_rows", [P, D]), sb("s_bo_rows", [P, D])
        rstd12 = sb("s_rstd12", [P, NB])
        xn = [sb(f"s_xn{p}", [P, D]) for p in range(2)]
        xf = sb("s_xf", [P, D])
        xn_t = [sb(f"s_xn_t{p}", [P, P]) for p in range(2)]
        q_t = [sb(f"s_q_t{p}", [P, P]) for p in range(2)]
        k_t = [sb(f"s_k_t{p}", [P, P]) for p in range(2)]
        k_wide = [sb(f"s_k_wide{p}", [P, HQ, P]) for p in range(2)]
        v_heads = [sb(f"s_v_heads{p}", [P, H, COL]) for p in range(2)]
        maxima = [sb(f"s_maxima{i}", [P, HQ], F32 if i % 2 else BF16) for i in range(CH)]
        probs = [sb(f"s_probs{i}", [P, W]) for i in range(CH)]
        probs_t = [sb(f"s_probs_t{i}", [P, W]) for i in range(CH)]
        o_t = sb("s_o_t", [P, 2 * P])
        rsum = sb("s_rsum", [P, H])
        mixed = sb("s_mixed", [P, D])
        mixed_t = sb("s_mixed_t", [P, P])

        scores = [k.psum(f"s_scores{i}", [P, W], ctx) for i in range(CH)]
        p_turned = [k.psum(f"s_p_turned{j}", [P, W], ctx) for j in range(2)]
        front = k.psum("s_front", [P, 512], ctx)
        out_ps = k.psum("s_out", [P, 512], ctx)
        loaded = k.sem("s_loaded")
        link = Chain(k.sem("s_chain"))
        s = {n: k.sem("s_" + n) for n in
             ("zeroed", "ones_set", "xn_ready", "xf_ready", "turned", "xn_t_ready", "qkv_done", "qk_ready", "v_ready", "wide_ready",
              "scores_done", "max_ready", "shifted", "probs_ready", "p_turned", "p_copied_even", "p_copied_odd", "pv_part", "pv_done",
              "o_ready", "o_turned", "recip", "mixed", "mixed_turned", "mixed_t_ready", "projected", "x2_ready",
              "x2_biased", "stats", "grown")}
        P_ = "L1_ffn_"
        loads = [(wqkv[:, :], ins[P_ + "Wqkv"]), (wo[:, :], ins[P_ + "Wo"]), (gain[:, :], column(ins[P_ + "ln1_g"])),
                 (shift_[:, :], column(ins[P_ + "ln1_b"])), (bq[:, :], column(ins[P_ + "bqkv"][0:D])),
                 (bk[:, :], column(ins[P_ + "bqkv"][D:2 * D])), (bv_rows[:, :], row_broadcast(ins[P_ + "bqkv"][2 * D:3 * D], P)),
                 (bo_rows[:, :], row_broadcast(ins[P_ + "bo"], P))]
        block = ctx.enter_context(nc.Block())

        def each(eng, step, last):
            for b in (0, 1):
                step(b, b)
            with eng.Fori(1, NB // 2 - 1) as i:
                for p in (0, 1):
                    step(2 * i + p, p)
            for b in (NB - 2, NB - 1):
                step(b, b % 2)
            last()

        def is_(b, n):
            return isinstance(b, int) and b == n

        @block.sync
        def _(sp):
            for to, of in loads:
                sp.dma_start(to, of).then_inc(loaded, 16)

        @block.tensor
        def _(pe):
            def turn_x(b, p):
                pe.wait_ge(s["xn_ready"], b + 1)
                pe.wait_ge(s["v_ready"], b)
                pe.transpose(front[:, 3 * P:4 * P], xn[p][:, :], k.ident[:, :]).then_inc(s["turned"], 1)

            def project(b, p):
                pe.wait_ge(s["xn_t_ready"], b + 1)
                pe.matmul(front[:, 0:P], wqkv[:, 0:D], xn_t[p][:, :], start=True, stop=True)
                pe.matmul(front[:, P:2 * P], wqkv[:, D:2 * D], xn_t[p][:, :], start=True, stop=True)
                pe.matmul(front[:, 2 * P:3 * P], xn_t[p][:, :], wqkv[:, 2 * D:3 * D], start=True, stop=True).then_inc(s["qkv_done"], 1)

            def score(b, p, i):
                if i == 0:
                    pe.wait_ge(s["wide_ready"], b + 1)
                if not is_(b, 0):
                    pe.wait_ge(s["probs_ready"], CH * (b - 1) + i + 1)
                q0 = QUAD * i
                pe.matmul(scores[i][:, :], q_t[p][q0:q0 + QUAD, :], k_wide[p][q0:q0 + QUAD, :, :],
                          start=True, stop=True).then_inc(s["scores_done"], 1)

            def shift(b, i):
                if i % 2:
                    return
                pe.wait_ge(s["max_ready"], CH * b + i + 1)
                pe.matmul(scores[i][:, :], k.identb[:, :], maxima[i][:, :].unsqueeze(2).broadcast_to([P, HQ, P]),
                          start=False, stop=True, skip_group_check=True).then_inc(s["shifted"], 1)

            def turn_p(b, i):
                pe.wait_ge(s["probs_ready"], CH * b + i + 1)
                pe.wait_ge(s["p_copied_odd" if i % 2 else "p_copied_even"], 2 * b + i // 2)
                for h in range(HQ):
                    mm = pe.transpose(p_turned[i % 2][:, h * P:(h + 1) * P], probs[i][:, h * P:(h + 1) * P], k.ident[:, :])
                mm.then_inc(s["p_turned"], 1)

            def weigh(b, p, c):
                pe.wait_ge(s["p_copied_even"], 2 * b + c + 1)
                pe.wait_ge(s["p_copied_odd"], 2 * b + c + 1)
                if c == 0:
                    pe.wait_ge(s["v_ready"], b + 1)
                    pe.wait_ge(s["mixed_t_ready"], b)
                else:
                    pe.wait_ge(s["x2_ready"], b)
                for h in range(HQ):
                    for half in range(2):
                        mm = pe.matmul(out_ps[COL * half:COL * (half + 1), c * P:(c + 1) * P],
                                       v_heads[p][:, HQ * (2 * c + half) + h, :], probs_t[2 * c + half][:, h * P:(h + 1) * P],
                                       start=(h == 0), stop=(h == HQ - 1))
                mm.then_inc(s["pv_done"] if c else s["pv_part"], 1)

            def turn_o(b):
                pe.wait_ge(s["o_ready"], b + 1)
                for jj in range(2):
                    mm = pe.transpose(out_ps[:, (2 + jj) * P:(3 + jj) * P], o_t[:, jj * P:(jj + 1) * P], k.ident[:, :])
                mm.then_inc(s["o_turned"], 1)

            def turn_mixed(b):
                pe.wait_ge(s["mixed"], b + 1)
                pe.transpose(out_ps[:, 2 * P:3 * P], mixed[:, :], k.ident[:, :]).then_inc(s["mixed_turned"], 1)

            def output(b):
                pe.wait_ge(s["mixed_t_ready"], b + 1)
                pe.matmul(out_ps[:, 3 * P:4 * P], mixed_t[:, :], wo[:, :], start=True, stop=True).then_inc(s["projected"], 1)

            def step(b, p):
                last, first = is_(b, NB - 1), is_(b, 0)
                score(b, p, 2)
                shift(b, 0)
                if not first:
                    turn_p(b - 1, 3)
                if not last:
                    project(b + 1, 1 - p)

                score(b, p, 3)
                shift(b, 1)
                turn_p(b, 0)
                if not first:
                    weigh(b - 1, 1 - p, 1)

                if not last:
                    score(b + 1, 1 - p, 0)
                if not first:
                    turn_o(b - 1)
                shift(b, 2)
                turn_p(b, 1)

                if not last:
                    score(b + 1, 1 - p, 1)
                if not first:
                    turn_mixed(b - 1)
                shift(b, 3)
                turn_p(b, 2)
                if not (last or is_(b, NB - 2)):
                    turn_x(b + 2, p)
                weigh(b, p, 0)
                if not first:
                    output(b - 1)

            def last():
                turn_p(NB - 1, 3)
                weigh(NB - 1, 1, 1)
                turn_o(NB - 1)
                turn_mixed(NB - 1)
                output(NB - 1)
            pe.wait_ge(loaded, 16 * len(loads))
            turn_x(0, 0)
            project(0, 0)
            score(0, 0, 0)
            score(0, 0, 1)
            turn_x(1, 1)
            each(pe, step, last)

        @block.scalar
        def _(act):
            def affine(b, p):
                act.wait_ge(s["turned"], b + 1)
                if not early(b):
                    act.wait_ge(s["qkv_done"], b - 1)
                act.activation(xn_t[p][:, :], front[:, 3 * P:4 * P], ACT.Identity, bias=shift_[:, 0:1],
                               scale=gain[:, 0:1]).then_inc(s["xn_t_ready"], 1)

            def bias_qk(b, p):
                act.wait_ge(s["qkv_done"], b + 1)
                if not early(b):
                    act.wait_ge(s["scores_done"], CH * (b - 1))
                    act.wait_ge(s["wide_ready"], b - 1)
                act.activation(q_t[p][:, :], front[:, 0:P], ACT.Identity, bias=bq[:, 0:1])
                act.activation(k_t[p][:, :], front[:, P:2 * P], ACT.Identity, bias=bk[:, 0:1]).then_inc(s["qk_ready"], 1)

            def exponent(b, i):
                if i % 2:
                    act.wait_ge(s["max_ready"], CH * b + i + 1)
                else:
                    act.wait_ge(s["shifted"], CH // 2 * b + i // 2 + 1)
                if not is_(b, 0):
                    act.wait_ge(s["p_turned"], CH * (b - 1) + i + 1)
                if i % 2:
                    for h in range(HQ):
                        op = act.activation(probs[i][:, h * P:(h + 1) * P], scores[i][:, h * P:(h + 1) * P], ACT.Exp,
                                            bias=maxima[i][:, h:h + 1])
                else:
                    op = act.activation(probs[i][:, :], scores[i][:, :], ACT.Exp)
                op.then_inc(s["probs_ready"], 1)

            def copy_p(b, i):
                act.wait_ge(s["p_turned"], CH * b + i + 1)
                if not is_(b, 0):
                    act.wait_ge(s["pv_done"] if i // 2 else s["pv_part"], b)
                act.activation(probs_t[i][:, :], p_turned[0][:, :], ACT.Copy).then_inc(s["p_copied_even"], 1)

            def copy_mixed(b):
                act.wait_ge(s["mixed_turned"], b + 1)
                act.wait_ge(s["projected"], b)
                act.activation(mixed_t[:, :], out_ps[:, 2 * P:3 * P], ACT.Copy).then_inc(s["mixed_t_ready"], 1)

            def step(b, p):
                last, first = is_(b, NB - 1), is_(b, 0)
                exponent(b, 0)
                if not last:
                    bias_qk(b + 1, 1 - p)
                exponent(b, 1)
                copy_p(b, 0)
                exponent(b, 2)
                if not first:
                    copy_mixed(b - 1)
                exponent(b, 3)
                copy_p(b, 2)
                if not (last or is_(b, NB - 2)):
                    affine(b + 2, p)

            act.wait_ge(loaded, 16 * len(loads))
            affine(0, 0)
            bias_qk(0, 0)
            affine(1, 1)
            each(act, step, lambda: copy_mixed(NB - 1))

        @block.gpsimd
        def _(pool):
            def spread(b, p):
                pool.wait_ge(s["qk_ready"], b + 1)
                if not early(b):
                    pool.wait_ge(s["scores_done"], CH * (b - 1))
                pool.tensor_tensor(k_wide[p][:, :, :], k_t[p][:, :].unsqueeze(1).broadcast_to([P, HQ, P]),
                                   k.headmask[:, 1, :].unsqueeze(2).broadcast_to([P, HQ, P]), ALU.mult).then_inc(s["wide_ready"], 1)

            def grow(b):
                pool.wait_ge(s["x2_ready"], b + 1)
                pool.tensor_tensor(k.x_res[:, b, :], k.x_res[:, b, :], k.tmp_res[:, b, :], ALU.add).then_inc(s["grown"], 1)

            def step(b, p):
                if not is_(b, NB - 1):
                    spread(b + 1, 1 - p)
                if not (is_(b, 0) or is_(b, 1)):
                    grow(b - 2)

            def last():
                grow(NB - 2)
                grow(NB - 1)
            for p in range(2):
                pool.memset(v_heads[p][:, :, :], 0.0).then_inc(s["zeroed"], 1)
            pool.wait_ge(s["zeroed"], 2)
            for p in range(2):
                first = v_heads[p][:, :, :]
                pool.memset(bass.AP(tensor=first.tensor, offset=first.offset + QUAD,
                                    ap=[list(first.ap[0]), [HQ * COL, H // HQ], [COL + 1, HQ]]), 1.0).then_inc(s["ones_set"], 1)
            pool.wait_ge(s["ones_set"], 2)
            spread(0, 0)
            each(pool, step, last)
            pool.wait_ge(s["grown"], NB)

        @block.vector
        def _(dve):
            def normalise(b, p):
                if not early(b):
                    dve.wait_ge(s["turned"], b - 1)
                dve.tensor_scalar(xn[p][:, :], k.x_res[:, b, :], k.mean[:, bass.ds(b, 1)], rstd12[:, bass.ds(b, 1)],
                                  ALU.subtract, ALU.mult).then_inc(s["xn_ready"], 1)

            def bias_v(b, p):
                dve.wait_ge(s["qk_ready"], b + 1)
                if not early(b):
                    dve.wait_ge(s["pv_done"], b - 1)
                first = v_heads[p][:, :, :]
                blocks = bass.AP(tensor=first.tensor, offset=first.offset,
                                 ap=[list(first.ap[0]), [HQ * COL, H // HQ], [COL + DH, HQ], [1, DH]])
                dve.tensor_tensor(blocks, front[:, 2 * P:3 * P].rearrange("p (j h d) -> p j h d", h=HQ, d=DH),
                                  bv_rows[:, :].rearrange("p (j h d) -> p j h d", h=HQ, d=DH), ALU.add).then_inc(s["v_ready"], 1)

            def maximum(b, i):
                dve.wait_ge(s["scores_done"], CH * b + i + 1)
                if not is_(b, 0):
                    if i % 2:
                        dve.wait_ge(s["probs_ready"], CH * (b - 1) + i + 1)
                    else:
                        dve.wait_ge(s["shifted"], CH // 2 * (b - 1) + i // 2 + 1)
                dve.tensor_reduce(maxima[i][:, :], scores[i][:, :].rearrange("p (h q) -> p h q", q=P),
                                  AX.X, ALU.max, negate=True).then_inc(s["max_ready"], 1)

            def copy_p(b, i):
                dve.wait_ge(s["p_turned"], CH * b + i + 1)
                if not is_(b, 0):
                    dve.wait_ge(s["pv_done"] if i // 2 else s["pv_part"], b)
                dve.tensor_copy(probs_t[i][:, :], p_turned[1][:, :]).then_inc(s["p_copied_odd"], 1)

            def copy_o(b):
                dve.wait_ge(s["pv_done"], b + 1)
                dve.wait_ge(s["o_turned"], b)
                dve.tensor_copy(o_t[:, :], out_ps[:, 0:2 * P]).then_inc(s["o_ready"], 1)

            def mix(b):
                dve.wait_ge(s["o_turned"], b + 1)
                both = out_ps[:, 2 * P:4 * P].rearrange("p (j c) -> p j c", c=COL)
                dve.reciprocal(rsum[:, :].rearrange("p (j h) -> p j h", h=HQ), both[:, :, QUAD:QUAD + HQ]).then_inc(s["recip"], 1)
                dve.wait_ge(s["recip"], b + 1)
                dve.wait_ge(s["mixed_turned"], b)
                dve.tensor_tensor(mixed[:, :].rearrange("p (j h d) -> p j h d", h=HQ, d=DH),
                                  both[:, :, 0:QUAD].rearrange("p j (h d) -> p j h d", d=DH),
                                  rsum[:, :].rearrange("p (j h) -> p j h", h=HQ).unsqueeze(3).broadcast_to([P, H // HQ, HQ, DH]),
                                  ALU.mult).then_inc(s["mixed"], 1)

            def base(b):
                dve.tensor_scalar(xf[:, :], k.x_res[:, b, :], k.mean[:, bass.ds(b, 1)], k.rstd[:, bass.ds(b, 1)],
                                  ALU.subtract, ALU.mult).then_inc(s["xf_ready"], 1)
                dve.wait_ge(s["xf_ready"], b + 1)
                dve.tensor_tensor(xf[:, :], xf[:, :], bo_rows[:, :], ALU.add).then_inc(s["x2_biased"], 1)

            def close(b):
                dve.wait_ge(s["projected"], b + 1)
                dve.wait_ge(s["x2_biased"], b + 1)
                dve.tensor_tensor(k.tmp_res[:, b, :], out_ps[:, 3 * P:4 * P], xf[:, :], ALU.add).then_inc(s["x2_ready"], 1)
                dve.wait_ge(s["x2_ready"], b + 1)
                dve.bn_stats(k.stats[:, b, :], k.tmp_res[:, b, :]).then_inc(s["stats"], 1)

            def step(b, p):
                last, first = is_(b, NB - 1), is_(b, 0)
                maximum(b, 2)
                if not first:
                    copy_p(b - 1, 3)
                if not (first or is_(b, 1)):
                    close(b - 2)
                maximum(b, 3)
                if not last:
                    bias_v(b + 1, 1 - p)
                if not first:
                    copy_o(b - 1)
                if not (last or is_(b, NB - 2)):
                    normalise(b + 2, p)
                if not last:
                    maximum(b + 1, 0)
                if not first:
                    mix(b - 1)
                copy_p(b, 1)
                if not first:
                    base(b - 1)
                if not last:
                    maximum(b + 1, 1)

            def last():
                copy_p(NB - 1, 3)
                close(NB - 2)
                copy_o(NB - 1)
                mix(NB - 1)
                base(NB - 1)
                close(NB - 1)
                dve.wait_ge(s["stats"], NB)
            link(dve, dve.tensor_tensor(rstd12[:, :], k.rstd[:, :], k.rstd2[:, :], ALU.mult))
            dve.wait_ge(loaded, 16 * len(loads))
            dve.wait_ge(s["ones_set"], 2)
            normalise(0, 0)
            bias_v(0, 0)
            normalise(1, 1)
            maximum(0, 0)
            maximum(0, 1)
            each(dve, step, last)


def build_expert_layer_1(k):
    nc, ins, NB = k.nc, k.ins, k.NB
    m = Experts("m1_", 512, 4, 1, ACT.Gelu)
    N_ = "L1_ffn_"
    with ExitStack() as ctx:
        sb = lambda n, s_, dt=F32: k.sb("m1_" + n, s_, dt, ctx)
        columns = sb("columns", [P, E + 2])
        gain, shift_, gain_rows, shift_rows = sb("gain", [P, 1]), sb("shift", [P, 1]), sb("gain_rows", [P, D]), sb("shift_rows", [P, D])
        coef_bias = sb("coef_bias", [P, E + 2])
        up, down = sb("up", [P, E, 512]), sb("down", [P, E, 4, D])
        up_bias, down_bias = sb("up_bias", [P, E, 512]), sb("down_bias", [P, E, D])
        s_up, s_down = sb("s_up", [P, 512]), sb("s_down", [P, 4, D])
        s_up_bias, s_down_rows = sb("s_up_bias", [P, 4]), sb("s_down_rows", [P, D])
        loaded = k.sem("m1_loaded")
        zeroed = k.sem("m1_zeroed")
        loads = [(columns[:, 0:E], ins[N_ + "gate_w"]), (columns[:, E:E + 2], ins[N_ + "coef_w"]),
                 (gain[:, :], column(ins[N_ + "ln2_g"])), (shift_[:, :], column(ins[N_ + "ln2_b"])),
                 (gain_rows[:, :], row_broadcast(ins[N_ + "ln2_g"], P)), (shift_rows[:, :], row_broadcast(ins[N_ + "ln2_b"], P)),
                 (coef_bias[:, E:E + 2], row_broadcast(ins[N_ + "coef_b"], P))]
        weights_loaded = k.sem("m1_weights_loaded")
        weights = [(up[:, :, :], ins[N_ + "W1"].rearrange("e h i -> h e i")),
                 (down[:, :, :, :], ins[N_ + "W2"].rearrange("e (c p) h -> p e c h", p=P)),
                 (up_bias[:, :, :], row_broadcast(ins[N_ + "b1"], P)), (down_bias[:, :, :], row_broadcast(ins[N_ + "b2"], P)),
                 (s_up[:, :], ins[N_ + "rW1"]), (s_down[:, :, :], ins[N_ + "rW2"].rearrange("(c p) h -> p c h", p=P)),
                 (s_up_bias[:, :], ins[N_ + "rb1"].rearrange("(c p) -> p c", p=P)),
                 (s_down_rows[:, :], row_broadcast(ins[N_ + "rb2"], P))]
        with nc.Block() as block:
            @block.sync
            def _(sp):
                for to, of in loads:
                    sp.dma_start(to, of, allow_slow_non_contiguous=True).then_inc(loaded, 16)
                for to, of in weights:
                    sp.dma_start(to, of, allow_slow_non_contiguous=True).then_inc(weights_loaded, 16)
                sp.wait_ge(loaded, 16 * len(loads))

            @block.vector
            def _(dve):
                dve.memset(coef_bias[:, 0:E], 0.0).then_inc(zeroed, 1)
                dve.wait_ge(zeroed, 1)
        build_rstd(k, "m1_rstd")
        build_prepare(k, m, columns[:, :], (gain, shift_, gain_rows, shift_rows), coef_bias,
                      (weights_loaded, 16 * len(weights)))
        build_route(k, m, None)
        build_dispatch(k, m, s_up, s_down, (s_up_bias, s_down_rows))
        build_experts(k, m, up, down, up_bias, down_bias)
        build_combine(k, m, final=True)


def build(nc, ins, out):
    with ExitStack() as ctx:
        k = Kernel(nc, ctx, ins, out)
        build_load(k)
        build_context_attention(k)
        build_rstd(k, "o0")
        build_context_output(k)
        build_rstd(k, "o1")
        build_context_residual(k)
        build_expert_layer_0(k)
        k.retire_semaphores()
        build_rstd(k, "c0")
        build_correlation(k)
        build_roll(k)
        build_rstd(k, "s0", composed=True)
        build_self_attention(k)
        build_expert_layer_1(k)
        k.sem_ctx.close()


def kernel(**inputs):
    import numpy as np
    import concourse.bacc as bacc
    from concourse import mybir as mb
    from concourse.bass_utils import run_bass_kernel_spmd as run

    nc = bacc.Bacc("TRN2", target_bir_lowering=False, num_devices=1)
    arrays = {"in_" + n: np.ascontiguousarray(a) for n, a in inputs.items()}
    rows = np.arange(P)
    arrays["in_c_ident"] = np.eye(P, dtype=np.float32)
    own_head = (rows[:, None] % QUAD) // DH == np.arange(HQ)
    arrays["in_c_headmask"] = np.stack([own_head / np.sqrt(D), own_head / np.sqrt(DH)], 1).astype(np.float32)
    NB = inputs["x"].shape[0]
    fill_row = np.arange(filled_slots(NB) * P).reshape(-1, P, FILL).transpose(1, 0, 2).reshape(P, -1)
    arrays["in_c_fill_rows"] = fill_row.astype(np.float32)
    token_row = filled_slots(NB) * P + np.arange(2 * NB * P).reshape(2, NB, P).transpose(2, 0, 1)
    arrays["in_c_token_rows"] = token_row.astype(np.float32)
    tables = np.concatenate([rows[:, None] < rows, np.tile(np.arange(E), (P, 1)), np.tile(np.arange(2 * NB + E), (P, 1))], 1)
    arrays["in_c_tables"] = tables.astype(np.float32)
    turns = 2 * np.pi * (np.outer(rows, np.concatenate([np.arange(65), np.arange(1, 64)])) % P) / P
    dft = np.where(np.arange(P) < 65, np.cos(turns), np.sin(turns))
    times = np.where((np.arange(P) == 0) | (np.arange(P) == 64), 1.0, 2.0)
    arrays["in_c_dft"] = dft.astype(np.float32)
    arrays["in_c_inverse"] = (dft.T * times[:, None] / P / P).astype(np.float32)
    arrays["in_c_dft_sums"] = np.stack([dft.sum(0), dft[:S2].sum(0)]).astype(np.float32)
    arrays["in_c_flip"] = (rows[:, None] == (-np.arange(2 * P)) % P).astype(np.float32)
    ins = {n[3:]: nc.dram_tensor(n, a.shape, mb.dt.from_np(a.dtype), kind="ExternalInput").ap()
           for n, a in arrays.items()}
    shape = inputs["x"].shape
    out = nc.dram_tensor("out", shape, mb.dt.float32, kind="ExternalOutput").ap()
    build(nc, ins, out)
    r = run(nc, [arrays], core_ids=[0])
    return r.results[0]["out"]
```
